# Optimizing a Trainium2 kernel written in Bass

```python
import numpy as np
import jax
import jax.numpy as jnp

def _softmax(x, axis=-1):
    return jax.nn.softmax(x, axis=axis)

def _gelu(x):
    return jax.nn.gelu(x, approximate=True)

def _silu(x):
    return jax.nn.silu(x)

def _sigmoid(x):
    return jax.nn.sigmoid(x)

def _layernorm(x, axis=-1, eps=1e-05):
    m = jnp.mean(x, axis=axis, keepdims=True)
    v = jnp.var(x, axis=axis, keepdims=True)
    return (x - m) / jnp.sqrt(v + eps)

def _scatter_add(tgt, idx, src, axis=0):
    return tgt.at[idx].add(src)

def _segment_sum(src, seg, n):
    return jax.ops.segment_sum(src, seg, n)
kernel_name = 'mk_macaron_d1_jaxref_r8_922ee9'

def setup_inputs(seed: int=0):
    np.random.seed(seed)
    _w = jnp.asarray

    def _L0_attn_setup():
        import jax, jax.numpy as jnp
        import numpy as np
        from jax import lax
        D_MODEL = 128
        D_STATE = 16
        BATCH = 8
        SEQ = 256

        def _silu(x):
            return x * jax.nn.sigmoid(x)

        def _depthwise_conv(x, conv_w):
            xc = jnp.swapaxes(x, 1, 2)
            y = lax.conv_general_dilated(xc, conv_w, window_strides=(1,), padding=[(1, 1)], dimension_numbers=('NCH', 'OIH', 'NCH'), feature_group_count=conv_w.shape[0])
            return jnp.swapaxes(y, 1, 2)

        def _ssm(x, A, B_ssm, C_ssm, D_ssm):
            Abar = jax.nn.sigmoid(A)
            b, l, c = x.shape
            h0 = jnp.zeros((b, c, A.shape[1]), x.dtype)

            def step(h, xt):
                h = h * Abar + xt[..., None] * B_ssm
                y = jnp.einsum('bcs,cs->bc', h, C_ssm) + D_ssm * xt
                return (h, y)
            _, ys = lax.scan(step, h0, jnp.swapaxes(x, 0, 1))
            return jnp.swapaxes(ys, 0, 1)
        key = jax.random.key(seed)
        ks = jax.random.split(key, 12)
        s = 0.02
        return {'x': jax.random.normal(ks[0], (BATCH, SEQ, D_MODEL), jnp.float32), 'w1_w': jax.random.normal(ks[1], (D_MODEL, D_MODEL), jnp.float32) * s, 'w1_b': jnp.zeros((D_MODEL,), jnp.float32), 'v1_w': jax.random.normal(ks[2], (D_MODEL, D_MODEL), jnp.float32) * s, 'v1_b': jnp.zeros((D_MODEL,), jnp.float32), 'w2_w': jax.random.normal(ks[3], (D_MODEL, D_MODEL), jnp.float32) * s, 'w2_b': jnp.zeros((D_MODEL,), jnp.float32), 'conv_w': jax.random.normal(ks[4], (D_MODEL, 1, 3), jnp.float32) * s, 'A': jax.random.normal(ks[5], (D_MODEL, D_STATE), jnp.float32), 'B_ssm': jax.random.normal(ks[6], (D_MODEL, D_STATE), jnp.float32) * s, 'C_ssm': jax.random.normal(ks[7], (D_MODEL, D_STATE), jnp.float32) * s, 'D_ssm': jnp.ones((D_MODEL,), jnp.float32)}
    _L0_attn_in = _L0_attn_setup()

    def _L0_ffn_setup():
        import jax, jax.numpy as jnp
        import numpy as np
        E = 8
        TOP_K = 2
        H = 128
        F = 512
        LN_EPS = 1e-12
        key = jax.random.key(seed)
        ks = jax.random.split(key, 9)
        s = lambda k, shape, scale: jax.random.normal(k, shape, dtype=jnp.float32) * scale
        return {'hidden_states': s(ks[0], (4, 256, H), 1.0), 'Wr': s(ks[1], (E, H), 0.02), 'br': jnp.zeros((E,), jnp.float32), 'W1': s(ks[2], (E, F, H), 0.02), 'b1': jnp.zeros((E, F), jnp.float32), 'W2': s(ks[3], (E, H, F), 0.02), 'b2': jnp.zeros((E, H), jnp.float32), 'ln_w': jnp.ones((H,), jnp.float32), 'ln_b': jnp.zeros((H,), jnp.float32)}
    _L0_ffn_in = _L0_ffn_setup()
    _d = {'L0_attn_x': _L0_attn_in['x'], 'L0_attn_w1_w': _L0_attn_in['w1_w'], 'L0_attn_w1_b': _L0_attn_in['w1_b'], 'L0_attn_v1_w': _L0_attn_in['v1_w'], 'L0_attn_v1_b': _L0_attn_in['v1_b'], 'L0_attn_w2_w': _L0_attn_in['w2_w'], 'L0_attn_w2_b': _L0_attn_in['w2_b'], 'L0_attn_conv_w': _L0_attn_in['conv_w'], 'L0_attn_A': _L0_attn_in['A'], 'L0_attn_B_ssm': _L0_attn_in['B_ssm'], 'L0_attn_C_ssm': _L0_attn_in['C_ssm'], 'L0_attn_D_ssm': _L0_attn_in['D_ssm'], 'L0_ffn_Wr': _L0_ffn_in['Wr'], 'L0_ffn_br': _L0_ffn_in['br'], 'L0_ffn_W1': _L0_ffn_in['W1'], 'L0_ffn_b1': _L0_ffn_in['b1'], 'L0_ffn_W2': _L0_ffn_in['W2'], 'L0_ffn_b2': _L0_ffn_in['b2'], 'L0_ffn_ln_w': _L0_ffn_in['ln_w'], 'L0_ffn_ln_b': _L0_ffn_in['ln_b']}
    _x0 = _d['L0_attn_x']
    _d['L0_attn_x'] = jax.random.normal(jax.random.fold_in(jax.random.key(seed), 1), (8, 512, 128), dtype=_x0.dtype)
    del _x0
    return _d

def reference(L0_attn_x, L0_attn_w1_w, L0_attn_w1_b, L0_attn_v1_w, L0_attn_v1_b, L0_attn_w2_w, L0_attn_w2_b, L0_attn_conv_w, L0_attn_A, L0_attn_B_ssm, L0_attn_C_ssm, L0_attn_D_ssm, L0_ffn_Wr, L0_ffn_br, L0_ffn_W1, L0_ffn_b1, L0_ffn_W2, L0_ffn_b2, L0_ffn_ln_w, L0_ffn_ln_b):

    def _L0_attn_ref(x, w1_w, w1_b, v1_w, v1_b, w2_w, w2_b, conv_w, A, B_ssm, C_ssm, D_ssm):
        import jax, jax.numpy as jnp
        import numpy as np
        from jax import lax
        D_MODEL = 128
        D_STATE = 16
        BATCH = 8
        SEQ = 256

        def _silu(x):
            return x * jax.nn.sigmoid(x)

        def _depthwise_conv(x, conv_w):
            xc = jnp.swapaxes(x, 1, 2)
            y = lax.conv_general_dilated(xc, conv_w, window_strides=(1,), padding=[(1, 1)], dimension_numbers=('NCH', 'OIH', 'NCH'), feature_group_count=conv_w.shape[0])
            return jnp.swapaxes(y, 1, 2)

        def _ssm(x, A, B_ssm, C_ssm, D_ssm):
            Abar = jax.nn.sigmoid(A)
            b, l, c = x.shape
            h0 = jnp.zeros((b, c, A.shape[1]), x.dtype)

            def step(h, xt):
                h = h * Abar + xt[..., None] * B_ssm
                y = jnp.einsum('bcs,cs->bc', h, C_ssm) + D_ssm * xt
                return (h, y)
            _, ys = lax.scan(step, h0, jnp.swapaxes(x, 0, 1))
            return jnp.swapaxes(ys, 0, 1)
        x1 = x @ w1_w.T + w1_b
        x_conv = _silu(_depthwise_conv(x1, conv_w))
        x_ssm = _ssm(x_conv, A, B_ssm, C_ssm, D_ssm)
        v = _silu(x @ v1_w.T + v1_b)
        return x_ssm * v @ w2_w.T + w2_b

    def _L0_ffn_ref(hidden_states, Wr, br, W1, b1, W2, b2, ln_w, ln_b):
        import jax, jax.numpy as jnp
        import numpy as np
        E = 8
        TOP_K = 2
        H = 128
        F = 512
        LN_EPS = 1e-12
        bsz, seqlen, h = hidden_states.shape
        x = hidden_states.reshape(-1, h)
        logits = x @ Wr.T + br
        topk_vals, topk_idx = jax.lax.top_k(logits, TOP_K)
        topk_w = jax.nn.softmax(topk_vals, axis=-1)
        out = jnp.zeros_like(x)
        for e in range(E):
            cw = jnp.sum(topk_w * (topk_idx == e), axis=-1)
            y = jax.nn.gelu(x @ W1[e].T + b1[e], approximate=False) @ W2[e].T + b2[e]
            out = out + cw[:, None] * y
        z = out + x
        mu = jnp.mean(z, axis=-1, keepdims=True)
        var = jnp.mean(jnp.square(z - mu), axis=-1, keepdims=True)
        z = (z - mu) * jax.lax.rsqrt(var + LN_EPS) * ln_w + ln_b
        return z.reshape(bsz, seqlen, h)
    x = L0_attn_x
    x = x + 0.5 * _L0_ffn_ref(_layernorm(x, axis=-1), L0_ffn_Wr, L0_ffn_br, L0_ffn_W1, L0_ffn_b1, L0_ffn_W2, L0_ffn_b2, L0_ffn_ln_w, L0_ffn_ln_b)
    x = x + _L0_attn_ref(_layernorm(x, axis=-1), L0_attn_w1_w, L0_attn_w1_b, L0_attn_v1_w, L0_attn_v1_b, L0_attn_w2_w, L0_attn_w2_b, L0_attn_conv_w, L0_attn_A, L0_attn_B_ssm, L0_attn_C_ssm, L0_attn_D_ssm)
    x = x + 0.5 * _L0_ffn_ref(_layernorm(x, axis=-1), L0_ffn_Wr, L0_ffn_br, L0_ffn_W1, L0_ffn_b1, L0_ffn_W2, L0_ffn_b2, L0_ffn_ln_w, L0_ffn_ln_b)
    return x

_drawn_inputs = setup_inputs


def setup_inputs(seed=0):
    import zlib

    import numpy as np

    out = dict(_drawn_inputs(seed))
    spreads = {'L0_attn_w1_b': (0.0, 0.8),
     'L0_attn_v1_b': (0.0, 0.8),
     'L0_attn_w2_b': (0.0, 0.392),
     'L0_attn_D_ssm': (1.0, 0.6),
     'L0_ffn_br': (0.0, 0.1),
     'L0_ffn_b1': (0.0, 0.771),
     'L0_ffn_b2': (0.0, 0.274),
     'L0_ffn_ln_w': (1.0, 0.2),
     'L0_ffn_ln_b': (0.0, 0.1)}
    factors = {'L0_attn_w1_w': 8.0,
     'L0_attn_v1_w': 8.0,
     'L0_attn_w2_w': 8.0,
     'L0_attn_conv_w': 8.0,
     'L0_attn_A': 8.0,
     'L0_attn_B_ssm': 8.0,
     'L0_attn_C_ssm': 8.0,
     'L0_ffn_W1': 3.058}
    for name, (base, spread) in spreads.items():
        noise = np.random.default_rng([zlib.crc32(name.encode()), seed]).standard_normal(out[name].shape)
        drawn = base * np.exp(spread * noise) if base else spread * noise
        out[name] = jnp.asarray(drawn.astype(out[name].dtype))
    for name, factor in factors.items():
        out[name] = (out[name] * factor).astype(out[name].dtype)
    return out
```

```python
from contextlib import ExitStack

import concourse.bass as bass
from concourse import mybir

F32 = mybir.dt.float32
F16 = mybir.dt.float16
I32 = mybir.dt.int32
ALU = mybir.AluOpType
ACT = mybir.ActivationFunctionType
X_AXIS = mybir.AxisListType.X

P = 128
D = 128
BATCH, SEQ = 8, 512
GROUPS = 2
CHUNK = 16
STEPS = CHUNK
TOKENS = BATCH * SEQ // GROUPS
SEQS = BATCH // GROUPS
CHUNKS_PER_SEQ = SEQ // CHUNK
EXPERTS = 8
HIDDEN = 512
FC = HIDDEN // P
RING = 4
TILES = -(-(2 * TOKENS // P + EXPERTS - 1) // RING) * RING
BLOCKS = TILES // RING
SLOTS = TILES * P
STATES = 16
CPG = P // CHUNK
CGROUPS = D // CPG
QUADS = STEPS // 4
LN_EPS_BLOCK = 1e-5
LN_EPS_FFN = 1e-12
RUNS = 2 * GROUPS
EXPONENT_BITS = 0x7F800000


def build(nc, x, w1_w, w1_b, v1_w, v1_b, w2_w, w2_b, conv_w, A, B_ssm, C_ssm, D_ssm,
          Wr, br, W1, b1, W2, b2, ln_w, ln_b, out):
    ctx = ExitStack()
    with ctx:
        def sb(name, shape, dt=F32):
            return ctx.enter_context(nc.sbuf_tensor(name, shape, dt))

        def sem(name):
            return ctx.enter_context(nc.semaphore(name))

        slot_x = [nc.dram_tensor(f"slot_x{g}", (SLOTS, 2 * D), F16).ap() for g in range(GROUPS)]
        slot_y = [nc.dram_tensor(f"slot_y{g}", (SLOTS, D), F32).ap() for g in range(GROUPS)]
        taps_dram = nc.dram_tensor("taps_dram", (D, 2 * CHUNK - 1), F32).ap()
        decay_dram = nc.dram_tensor("decay_dram", (D, CHUNK + 1, STATES), F32).ap()
        readout_dram = nc.dram_tensor("readout_dram", (D, STATES, CHUNK + 1), F32).ap()

        z_ps = [ctx.enter_context(nc.psum_tensor(f"z_ps{i}", [P, 512], F32)) for i in range(2)]
        xT_ps = [ctx.enter_context(nc.psum_tensor(f"xT_ps{i}", [P, 1024], F16)) for i in range(2)]
        y_ps = [ctx.enter_context(nc.psum_tensor(f"y_ps{i}", [P, 512], F32)) for i in range(2)]
        aux_ps = [ctx.enter_context(nc.psum_tensor(f"aux_ps{i}", [P, 512], F32)) for i in range(2)]

        resid = sb("resid", [P, GROUPS, STEPS, D])
        xn = sb("xn", [P, GROUPS, STEPS, D])
        halves = sb("halves", [P, GROUPS, STEPS, 2 * D], F16)
        stage = sb("stage", [P, GROUPS, 2, STEPS, D])
        W1T = sb("W1T", [P, 2, EXPERTS, HIDDEN], F16)
        W2T = sb("W2T", [P, 2, EXPERTS, FC, D], F16)
        b1T = sb("b1T", [P, EXPERTS * FC])
        b1_rows = sb("b1_rows", [EXPERTS * FC, P])
        b2_bc = sb("b2_bc", [P, EXPERTS, D])
        br_bc = sb("br_bc", [P, EXPERTS])
        half_w_bc = sb("half_w_bc", [P, D])
        half_b_bc = sb("half_b_bc", [P, D])
        ident = sb("ident", [P, P])
        ident16 = sb("ident16", [P, P], F16)
        before = sb("before", [P, P])
        ones = sb("ones", [P, P])
        low_first = sb("low_first", [P, EXPERTS, STEPS])
        not_step0 = sb("not_step0", [P, EXPERTS, STEPS])
        tile_start = sb("tile_start", [1, TILES])
        WrT = sb("WrT", [P, EXPERTS])
        wr_rows = sb("wr_rows", [EXPERTS, D])
        projT = sb("projT", [P, 5, D])
        conv_c = sb("conv_c", [P, 3])
        w1b_bc = sb("w1b_bc", [P, D])
        convb_bc = sb("convb_bc", [P, D])
        edge_w = sb("edge_w", [1, 2, D])
        edge_at = sb("edge_at", [1, 2, P])
        v1b_bc = sb("v1b_bc", [P, D])
        w2b_bc = sb("w2b_bc", [P, D])
        ssm_in = sb("ssm_in", [P, 3, STATES])
        d_in = sb("d_in", [P, 1])
        decay = sb("decay", [P, CHUNK + 1, STATES])
        cb = sb("cb", [P, STATES])
        taps = sb("taps", [P, 2 * CHUNK - 1])
        readout = sb("readout", [P, STATES, CHUNK + 1])
        mT = sb("mT", [P, CGROUPS, CHUNK])
        mU = sb("mU", [P, CGROUPS, STATES])
        mV = sb("mV", [P, CGROUPS, CHUNK + 1])
        same_c = sb("same_c", [P, CPG])
        T = sb("T", [P, CGROUPS, CHUNK * CPG])
        U = sb("U", [P, CGROUPS, STATES * CPG])
        V = sb("V", [P, CGROUPS, CHUNK * CPG])
        keep_chunk = sb("keep_chunk", [P, P])
        chunk_decay = sb("chunk_decay", [P, CGROUPS, P])
        turned = sb("turned", [P, STEPS + 2, P])
        states = sb("states", [P, 1 + CGROUPS * P])
        tile_x = sb("tile_x", [P, RING, 2 * D], F16)
        tile_xT = sb("tile_xT", [P, RING, 2 * P], F16)
        hid = sb("hid", [P, 2, HIDDEN])
        hid_hi = sb("hid_hi", [P, RING, HIDDEN], F16)
        hid_lo = sb("hid_lo", [P, RING, HIDDEN], F16)
        tile_y = sb("tile_y", [P, RING, D])
        mix = stage[:, 0, 0].rearrange("p j d -> p (j d)")
        ssm_x = stage[:, 0, 1]
        gate = halves[:, 1].rearrange("p j d -> p (j d)").bitcast(F32).rearrange("p (j d) -> p j d", j=STEPS)
        scaled = hid
        setup = iter(range(1, 1 + 4 * 3 * D, 3 * D))

        def setup_rows(shape):
            at = next(setup)
            flat = states[:, at:at + shape[0] * shape[1]]
            return flat.rearrange("p (a b) -> p a b", a=shape[0])

        small_w = setup_rows([3, D])
        tap_w = setup_rows([3, D])
        conv_bc = setup_rows([D, 3])
        tap_terms = setup_rows([CHUNK, STATES])
        st = sb("st", [P, STEPS, 6])
        mean = sb("mean", [P, STEPS])
        var = sb("var", [P, STEPS])
        rstd = sb("rstd", [P, STEPS])
        shift = sb("shift", [P, STEPS])
        t1 = sb("t1", [P, STEPS])
        t2 = sb("t2", [P, STEPS])
        lg = sb("lg", [P, EXPERTS, STEPS])
        r1 = sb("r1", [P, EXPERTS, STEPS])
        pick = [sb(f"pick{k}", [P, EXPERTS, STEPS]) for k in range(2)]
        rank = sb("rank", [P, EXPERTS, STEPS])
        best = [sb(f"best{k}", [P, STEPS]) for k in range(2)]
        gap = sb("gap", [P, STEPS])
        gap_exp = sb("gap_exp", [P, STEPS])
        share = sb("share", [P, GROUPS, 2, STEPS])
        counts = sb("counts", [P, 2, EXPERTS])
        whole_i = sb("whole_i", [P, EXPERTS], I32)
        whole = sb("whole", [P, EXPERTS])
        ends = sb("ends", [P, EXPERTS])
        start_f = sb("start_f", [P, EXPERTS])
        slot_f = sb("slot_f", [P, 2, STEPS])
        slots = sb("slots", [P, GROUPS, 2, STEPS], I32)
        past = sb("past", [1, TILES, EXPERTS])
        owner_f = sb("owner_f", [1, TILES])
        owner = sb("owner", [1, GROUPS, TILES], I32)
        zero_rows = tile_y
        big = sb("big", [P, 4])
        big_all = sb("big_all", [P, 4])
        scale_t = sb("scale_t", [P, 4])
        scales = sb("scales", [P, 8])
        S1, INV1, S2, INV2, SH, INVH, INVY = (scales[:, k:k + 1] for k in range(7))

        x_in = [sem(f"x_in{g}") for g in range(GROUPS)]
        small_in = sem("small_in")
        ffn_in = sem("ffn_in")
        pool_const = sem("pool_const")
        pool_step = sem("pool_step")
        zeros_ready = sem("zeros_ready")
        zeroed = [sem(f"zeroed{g}") for g in range(GROUPS)]
        v_step = sem("v_step")
        small_ready = sem("small_ready")
        normed = sem("normed")
        halves_ready = sem("halves_ready")
        slots_ready = sem("slots_ready")
        owner_ready = sem("owner_ready")
        gap_ready = sem("gap_ready")
        gap_exp_ready = sem("gap_exp_ready")
        ones_counted = sem("ones_counted")
        max_ready = sem("max_ready")
        max_all = sem("max_all")
        scales_ready = sem("scales_ready")
        scaled_ready = sem("scaled_ready")
        scaled_used = sem("scaled_used")
        decay_in = sem("decay_in")
        ssm_const = sem("ssm_const")
        ssm_dram = sem("ssm_dram")
        ssm_back = sem("ssm_back")
        ssm_mats = sem("ssm_mats")
        aux_full = sem("aux_full")
        aux_free = [sem(f"aux_free{b}") for b in range(2)]
        scattered = [sem(f"scattered{g}") for g in range(GROUPS)]
        gathered = [sem(f"gathered{g}") for g in range(GROUPS)]
        combined = sem("combined")
        tile_in = [sem(f"tile_in{q}") for q in range(RING)]
        tile_out = [sem(f"tile_out{q}") for q in range(RING)]
        x_turned = sem("x_turned")
        x_copied = sem("x_copied")
        z_ready = sem("z_ready")
        gelu_done = sem("gelu_done")
        hi_ready = sem("hi_ready")
        h_ready = sem("h_ready")
        y_ready = sem("y_ready")
        y_taken = sem("y_taken")
        turned_ready = sem("turned_ready")
        conv_ready = sem("conv_ready")
        gate_in = sem("gate_in")
        gate_ready = sem("gate_ready")
        ssm_x_ready = sem("ssm_x_ready")
        states_ready = sem("states_ready")
        mix_ready = sem("mix_ready")
        x_out = sem("x_out")
        x_final = sem("x_final")

        aux = [("small", 0), ("small", 1)]

        def routing_units(r):
            return [("xnT", r, k) for k in range(QUADS)] + [("logits", r), ("ranks", r)]

        for g in range(GROUPS):
            aux += routing_units(g)
        aux += [("W1T", k) for k in range(EXPERTS)] + [("W2T", k) for k in range(EXPERTS)]
        for g in range(GROUPS):
            for kind in ("aT", "conv", "v", "cT", "u", "y", "yT", "o"):
                aux += [(kind, g, k) for k in range(QUADS)]
            aux += routing_units(GROUPS + g)
        aux_index = {key: n for n, key in enumerate(aux)}

        def bank(key):
            return aux_ps[aux_index[key] % 2]

        def wait_bank(pe, key):
            n = aux_index[key]
            if n >= 2:
                pe.wait_ge(aux_free[n % 2], n // 2)

        def wait_unit(eng, key):
            eng.wait_ge(aux_full, aux_index[key] + 1)

        def freed(ins, key):
            ins.then_inc(aux_free[aux_index[key] % 2], 1)

        def token_rows(ap, g):
            return ap[g * TOKENS:(g + 1) * TOKENS, :].rearrange("(p j) d -> p j d", p=P)

        def normed_count(*key):
            order = [(r,) for r in range(GROUPS)]
            for g in range(GROUPS):
                order += [("a", g), (GROUPS + g,)]
            return order.index(key) + 1

        x_rows = x.rearrange("b t d -> (b t) d")
        out_rows = out.rearrange("b t d -> (b t) d")

        def row(ap):
            return ap.rearrange("(a n) -> a n", a=1)

        def tile_first(r):
            return r * TILES

        SMALL_LOADS = 18
        block = ctx.enter_context(nc.Block())

        @block.sync
        def _(sp):
            for g in range(GROUPS):
                sp.dma_start(resid[:, g], token_rows(x_rows, g)).then_inc(x_in[g], 16)

            for dst, src in ((wr_rows[:, :], Wr), (br_bc[:, :], row(br).to_broadcast([P, EXPERTS])),
                             (small_w[:, 0], w1_w), (small_w[:, 1], v1_w), (small_w[:, 2], w2_w),
                             (b1_rows[:, :], b1.rearrange("e (c f) -> (e c) f", f=P)),
                             (conv_c[:, :], conv_w.rearrange("c a k -> c (a k)")),
                             (conv_bc[:, :, :], conv_w.rearrange("c a k -> a c k").to_broadcast([P, D, 3])),
                             (w1b_bc[:, :], row(w1_b).to_broadcast([P, D])),
                             (v1b_bc[:, :], row(v1_b).to_broadcast([P, D])),
                             (w2b_bc[:, :], row(w2_b).to_broadcast([P, D])),
                             (half_w_bc[:, :], row(ln_w).to_broadcast([P, D])),
                             (half_b_bc[:, :], row(ln_b).to_broadcast([P, D])),
                             (ssm_in[:, 0], A), (ssm_in[:, 1], B_ssm), (ssm_in[:, 2], C_ssm),
                             (d_in[:, :], D_ssm.rearrange("(c a) -> c a", a=1)),
                             (b2_bc[:, :, :], b2.rearrange("(a e) h -> a e h", a=1).to_broadcast([P, EXPERTS, D]))):
                sp.dma_start(dst, src).then_inc(small_in, 16)


            sp.wait_ge(zeros_ready, 1)
            for g in range(GROUPS):
                for k in range(RING):
                    sp.dma_start(slot_x[g][k * SLOTS // RING:(k + 1) * SLOTS // RING, :].rearrange(
                        "(a p) d -> p a d", p=P), zero_rows[:, 0:1, :].bitcast(F16).to_broadcast(
                            [P, TILES // RING, 2 * D])).then_inc(zeroed[g], 16)
            sp.wait_ge(ssm_const, 1)
            sp.dma_start(taps_dram, taps[:, :]).then_inc(ssm_dram, 16)
            sp.dma_start(decay_dram, decay[:, :, :]).then_inc(ssm_dram, 16)
            sp.dma_start(readout_dram, readout[:, :, :]).then_inc(ssm_dram, 16)
            sp.wait_ge(ssm_dram, 48)
            for j in range(CHUNK):
                at = slice(j * CPG, (j + 1) * CPG)
                back = CHUNK - 1 - j
                sp.dma_start(mT[at], taps_dram.rearrange("(g c) t -> c g t", c=CPG)[:, :, back:back + CHUNK])\
                    .then_inc(ssm_back, 16)
                sp.dma_start(mU[at], decay_dram.rearrange("(g c) k s -> c g k s", c=CPG)[:, :, back, :])\
                    .then_inc(ssm_back, 16)
                sp.dma_start(mV[at], readout_dram.rearrange("(g c) s t -> c g s t", c=CPG)[:, :, j, :])\
                    .then_inc(ssm_back, 16)

            def load_tile(r, n, i, q):
                if not (isinstance(n, int) and n < RING):
                    sp.wait_ge(x_turned, n - RING + 1)
                sp.dma_start(tile_x[:, q], slot_x[r % GROUPS][bass.ds(i * P, P), :]).then_inc(tile_in[q], 16)

            def store_tile(r, n, i, q):
                sp.wait_ge(y_taken, n + 1)
                sp.dma_start(slot_y[r % GROUPS][bass.ds(i * P, P), :], tile_y[:, q]).then_inc(tile_out[q], 16)

            for r in range(RUNS):
                g, first = r % GROUPS, tile_first(r)
                sp.wait_ge(scattered[g], 16 * 2 * STEPS * (r // GROUPS + 1))
                if r >= GROUPS:
                    sp.wait_ge(gathered[g], 16 * 2 * STEPS)
                for q in range(RING):
                    load_tile(r, first + q, q, q)
                with sp.Fori(1, BLOCKS) as b:
                    for q in range(RING):
                        load_tile(r, b * RING + (first + q), b * RING + q, q)
                        store_tile(r, b * RING + (first + q - RING), b * RING + (q - RING), q)
                for q in range(RING):
                    store_tile(r, first + TILES - RING + q, TILES - RING + q, q)
                if r >= GROUPS:
                    pass
            for g in range(GROUPS):
                sp.wait_ge(x_final, g + 1)
                sp.dma_start(token_rows(out_rows, g), resid[:, g]).then_inc(x_out, 16)
            sp.wait_ge(x_out, 16 * GROUPS)
            for q in range(RING):
                sp.wait_ge(tile_out[q], 16 * BLOCKS * RUNS)

        @block.gpsimd
        def _(pool):
            steps = 0

            def settle(ins):
                nonlocal steps
                steps += 1
                ins.then_inc(pool_step, 1)
                pool.wait_ge(pool_step, steps)

            nc.gpsimd.memset(zero_rows[:, 0, :], 0.0).then_inc(zeros_ready, 1)
            nc.gpsimd.memset(ones[:, :], 1.0)
            nc.gpsimd.memset(before[:, :], 1.0)
            settle(nc.gpsimd.memset(ident[:, :], 0.0))
            nc.gpsimd.affine_select(out=ident[:, :], in_=ident[:, :], compare_op=ALU.not_equal, fill=1.0,
                                    base=0, pattern=[[-1, P]], channel_multiplier=1).then_inc(pool_const, 1)
            nc.gpsimd.affine_select(out=before[:, :], in_=before[:, :], compare_op=ALU.is_gt, fill=0.0,
                                    base=0, pattern=[[1, P]], channel_multiplier=-1)
            for e in range(EXPERTS):
                nc.gpsimd.memset(low_first[:, e, :], float(EXPERTS - e))
            nc.gpsimd.iota(tile_start[:, :], pattern=[[P, TILES]], base=0, channel_multiplier=0,
                           allow_small_or_imprecise_dtypes=True)
            settle(nc.gpsimd.memset(not_step0[:, :, :], 1.0))
            settle(nc.gpsimd.memset(keep_chunk[:, :], 1.0))
            settle(nc.gpsimd.memset(edge_at[:, :, :], 0.0))
            nc.gpsimd.memset(not_step0[:, :, 0:1], 0.0)
            nc.gpsimd.memset(keep_chunk[:, 0:P:CHUNKS_PER_SEQ], 0.0)
            nc.gpsimd.memset(edge_at[:, 0, 0:P:CHUNKS_PER_SEQ], 1.0)
            nc.gpsimd.memset(edge_at[:, 1, CHUNKS_PER_SEQ - 1:P:CHUNKS_PER_SEQ], 1.0)
            nc.gpsimd.memset(turned[:, 0, :], 0.0)
            nc.gpsimd.memset(turned[:, STEPS + 1, :], 0.0)
            nc.gpsimd.memset(taps[:, 0:CHUNK - 1], 0.0)
            nc.gpsimd.memset(decay[:, 0, :], 1.0)
            nc.gpsimd.memset(states[:, 0:1], 0.0).then_inc(pool_const, 1)

            def scatter(r):
                g, f = r % GROUPS, r // GROUPS
                if f == 0:
                    pool.wait_ge(zeroed[g], 16 * RING)
                for q in range(RING):
                    if f:
                        pool.wait_ge(tile_in[q], 16 * BLOCKS * (tile_first(g + 1) // TILES))
                pool.wait_ge(halves_ready, r + 1)
                pool.wait_ge(slots_ready, r + 1)
                for k in range(2):
                    for j in range(STEPS):
                        pool.indirect_dma_start(
                            out=slot_x[g], in_=halves[:, g, j, :], in_offset=None,
                            out_offset=bass.IndirectOffsetOnAxis(ap=slots[:, g, k, j:j + 1], axis=0))\
                            .then_inc(scattered[g], 16)

            def gather(r):
                g, f = r % GROUPS, r // GROUPS
                for q in range(RING):
                    pool.wait_ge(tile_out[q], 16 * BLOCKS * (r + 1))
                if f:
                    pool.wait_ge(combined, g + 1)
                else:
                    pool.wait_ge(scaled_used, 2 * EXPERTS)
                for k in range(2):
                    for j in range(STEPS):
                        pool.indirect_dma_start(
                            out=stage[:, g, k, j, :], out_offset=None, in_=slot_y[g],
                            in_offset=bass.IndirectOffsetOnAxis(ap=slots[:, g, k, j:j + 1], axis=0))\
                            .then_inc(gathered[g], 16)

            for g in range(GROUPS):
                scatter(g)
                if g == 0:
                    pool.wait_ge(max_ready, 1)
                    nc.gpsimd.partition_all_reduce(big_all[:, 0:3], big[:, 0:3], P,
                                                   bass.bass_isa.ReduceOp.max).then_inc(max_all, 1)
            for g in range(GROUPS):
                gather(g)
            for g in range(GROUPS):
                scatter(GROUPS + g)
            for g in range(GROUPS):
                gather(GROUPS + g)
            for g in range(GROUPS):
                pool.wait_ge(gathered[g], 2 * 16 * 2 * STEPS)

        @block.scalar
        def _(act):
            for g, w in ((0, W1.rearrange("e f d -> (e f) d")), (1, W2.rearrange("e h f -> (e h) f"))):
                pass
            w1_stage = stage[:, 0].rearrange("p k j d -> p (k j) d")
            w2_stage = stage[:, 1].rearrange("p k j d -> p (k j d)").rearrange("p (e f) -> p e f", e=EXPERTS)
            act.dma_start(w1_stage, W1.rearrange("e (c f) d -> f (e c) d", f=P)).then_inc(ffn_in, 16)
            act.dma_start(w2_stage, W2.rearrange("e h f -> h e f")).then_inc(ffn_in, 16)
            act.wait_ge(small_in, 16 * SMALL_LOADS)
            nc.scalar.activation(decay[:, 1, :], ssm_in[:, 0], ACT.Sigmoid).then_inc(decay_in, 1)

            def copy_small():
                wait_unit(act, ("small", 0))
                freed(nc.scalar.activation(projT[:, 0:4, :], bank(("small", 0))[:, :], ACT.Copy), ("small", 0))
                wait_unit(act, ("small", 1))
                nc.scalar.activation(projT[:, 4, :], bank(("small", 1))[:, 0:P], ACT.Copy)
                nc.scalar.activation(b1T[:, :], bank(("small", 1))[:, P:P + EXPERTS * FC], ACT.Copy)
                ins = nc.scalar.activation(WrT[:, :], bank(("small", 1))[:, 2 * P:2 * P + EXPERTS], ACT.Copy)
                freed(ins, ("small", 1))

            def copy_turned(kind, r, k, last_reader):
                if k == 0 and last_reader is not None:
                    wait_unit(act, last_reader)
                key = (kind, r, k)
                wait_unit(act, key)
                src = bank(key)
                ins = nc.scalar.activation(turned[:, 1 + 4 * k:5 + 4 * k, :], src[:, :], ACT.Copy)
                if kind == "aT" and k in (0, QUADS - 1):
                    m = CHUNKS_PER_SEQ
                    seqs = src[:, :].rearrange("d (i s c) -> d i s c", i=4, c=m)
                    if k == 0:
                        ins = nc.scalar.activation(
                            turned[:, STEPS + 1, :].rearrange("d (s c) -> d s c", c=m)[:, :, 0:m - 1],
                            seqs[:, 0, :, 1:m], ACT.Copy)
                    else:
                        ins = nc.scalar.activation(
                            turned[:, 0, :].rearrange("d (s c) -> d s c", c=m)[:, :, 1:m],
                            seqs[:, 3, :, 0:m - 1], ACT.Copy)
                freed(ins, key)

            def route(r, last_reader):
                for k in range(QUADS):
                    copy_turned("xnT", r, k, last_reader)
                act.wait_ge(gap_ready, r + 1)
                nc.scalar.activation(gap_exp[:, :], gap[:, :], ACT.Exp).then_inc(gap_exp_ready, 1)

            def scale_weights():
                act.wait_ge(scales_ready, 1)
                for n in range(2 * EXPERTS):
                    key = ("W1T", n) if n < EXPERTS else ("W2T", n - EXPERTS)
                    wait_unit(act, key)
                    if n >= 2:
                        act.wait_ge(scaled_used, n - 1)
                    ins = nc.scalar.activation(scaled[:, n % 2, :], bank(key)[:, :], ACT.Copy,
                                               scale=S1 if n < EXPERTS else S2)
                    ins.then_inc(scaled_ready, 1)
                    act.wait_ge(scaled_ready, n + 1)
                    act.sem_inc(aux_free[aux_index[key] % 2], 1)

            def copy_x(n, q):
                act.wait_ge(x_turned, n + 1)
                if not (isinstance(n, int) and n < RING):
                    act.wait_ge(z_ready, n - RING + 1)
                nc.scalar.activation(tile_xT[:, q, :], xT_ps[q % 2][:, 0:2 * P], ACT.Copy).then_inc(x_copied, 1)

            def gelu(r, n, i, q):
                e = act.value_load(owner[0:1, r % GROUPS, bass.ds(i, 1)], min_val=0, max_val=EXPERTS - 1)
                act.wait_ge(z_ready, n + 1)
                if not (isinstance(n, int) and n < 2):
                    act.wait_ge(h_ready, n - 1)
                for c in range(FC):
                    ins = nc.scalar.activation(hid[:, q % 2, c * P:(c + 1) * P], z_ps[q % 2][:, c * P:(c + 1) * P],
                                               ACT.Gelu, bias=b1T[:, bass.ds(e * FC + c, 1)], scale=INV1)
                ins.then_inc(gelu_done, 1)

            def tiles(r):
                first = tile_first(r)
                act.wait_ge(owner_ready, r + 1)
                copy_x(first, 0)
                for q in range(RING):
                    copy_x(first + q + 1, (q + 1) % RING)
                    gelu(r, first + q, q, q)
                with act.Fori(1, BLOCKS - 1) as b:
                    for q in range(RING):
                        copy_x(b * RING + (first + q + 1), (q + 1) % RING)
                        gelu(r, b * RING + (first + q), b * RING + q, q)
                for q in range(RING):
                    i = TILES - RING + q
                    if q < RING - 1:
                        copy_x(first + i + 1, (q + 1) % RING)
                    gelu(r, first + i, i, q)

            def mixer(g):
                last = ("logits", GROUPS - 1) if g == 0 else ("logits", GROUPS + g - 1)
                for k in range(QUADS):
                    copy_turned("aT", g, k, last)
                    if k == QUADS - 1:
                        act.wait_ge(aux_free[aux_index[("aT", g, k)] % 2], aux_index[("aT", g, k)] // 2 + 1)
                act.sem_inc(turned_ready, 1)
                for k in range(QUADS):
                    act.wait_ge(gate_in, QUADS * g + k + 1)
                    nc.scalar.activation(gate[:, 4 * k:4 * k + 4, :], gate[:, 4 * k:4 * k + 4, :], ACT.Silu)\
                        .then_inc(gate_ready, 1)
                for k in range(QUADS):
                    key = ("cT", g, k)
                    wait_unit(act, key)
                    ins = nc.scalar.activation(ssm_x[:, 4 * k:4 * k + 4, :], bank(key)[:, :], ACT.Silu)
                    ins.then_inc(ssm_x_ready, 1)
                    act.wait_ge(ssm_x_ready, QUADS * g + k + 1)
                    act.sem_inc(aux_free[aux_index[key] % 2], 1)
                for k in range(QUADS):
                    copy_turned("yT", g, k, ("v", g, QUADS - 1))

            copy_small()
            for g in range(GROUPS):
                route(g, None if g == 0 else ("logits", g - 1))
            scale_weights()
            for g in range(GROUPS):
                tiles(g)
            for g in range(GROUPS):
                mixer(g)
                route(GROUPS + g, ("o", g, QUADS - 1))
            for g in range(GROUPS):
                tiles(GROUPS + g)

        @block.tensor
        def _(pe):
            def turn(key, sources, rows=P):
                wait_bank(pe, key)
                for i, src in enumerate(sources):
                    ins = nc.tensor.transpose(bank(key)[:, i * P:i * P + src.shape[0]], src,
                                              ident[0:src.shape[0], 0:src.shape[0]])
                ins.then_inc(aux_full, 1)

            def route(r):
                g = r % GROUPS
                pe.wait_ge(normed, normed_count(r))
                for k in range(QUADS):
                    turn(("xnT", r, k), [xn[:, g, 4 * k + i, :] for i in range(4)])
                key = ("logits", r)
                wait_bank(pe, key)
                last = ("xnT", r, QUADS - 1)
                for k in (-2, -1):
                    n = aux_index[last] + 1 + k
                    pe.wait_ge(aux_free[n % 2], n // 2 + 1)
                for j in range(STEPS):
                    ins = nc.tensor.matmul(bank(key)[:, j * EXPERTS:(j + 1) * EXPERTS], turned[:, 1 + j, :],
                                           WrT[:, :], start=True, stop=True)
                ins.then_inc(aux_full, 1)
                key = ("ranks", r)
                wait_bank(pe, key)
                pe.wait_ge(ones_counted, r + 1)
                nc.tensor.matmul(bank(key)[:, 0:EXPERTS], before[:, :], rank[:, :, STEPS - 1],
                                 start=True, stop=True)
                nc.tensor.matmul(bank(key)[:, EXPERTS:2 * EXPERTS], ones[:, :], rank[:, :, STEPS - 1],
                                 start=True, stop=True).then_inc(aux_full, 1)

            def turn_x(n, q):
                pe.wait_ge(tile_in[q], in_value(n, q))
                if not (isinstance(n, int) and n < 2):
                    pe.wait_ge(x_copied, n - 1)
                nc.tensor.transpose(xT_ps[q % 2][:, 0:P], tile_x[:, q, 0:D], ident16[:, :])
                nc.tensor.transpose(xT_ps[q % 2][:, P:2 * P], tile_x[:, q, D:2 * D], ident16[:, :])\
                    .then_inc(x_turned, 1)

            def in_value(n, q):
                return (n // RING + 1) * 16 if isinstance(n, int) else (n - q) * (16 // RING) + 16

            def hidden(r, n, i, q):
                e = pe.value_load(owner[0:1, r % GROUPS, bass.ds(i, 1)], min_val=0, max_val=EXPERTS - 1)
                pe.wait_ge(x_copied, n + 1)
                if not (isinstance(n, int) and n < 2):
                    pe.wait_ge(gelu_done, n - 1)
                w = W1T[:, :, :, :].rearrange("p k e f -> p (k e f)")
                x_hi, x_lo = tile_xT[:, q, 0:P], tile_xT[:, q, P:2 * P]
                for c in range(FC):
                    z = z_ps[q % 2][:, c * P:(c + 1) * P]
                    w_hi = w[:, bass.ds(e * HIDDEN + c * P, P)]
                    w_lo = w[:, bass.ds(e * HIDDEN + (EXPERTS * HIDDEN + c * P), P)]
                    nc.tensor.matmul(z, w_hi, x_hi, start=True, stop=False)
                    nc.tensor.matmul(z, w_hi, x_lo, start=False, stop=False)
                    ins = nc.tensor.matmul(z, w_lo, x_hi, start=False, stop=True)
                ins.then_inc(z_ready, 1)

            def result(r, n, i, q):
                e = pe.value_load(owner[0:1, r % GROUPS, bass.ds(i, 1)], min_val=0, max_val=EXPERTS - 1)
                pe.wait_ge(h_ready, n + 1)
                if not (isinstance(n, int) and n < 2):
                    pe.wait_ge(y_taken, n - 1)
                w = W2T[:, :, :, :, :].rearrange("p k e c h -> p (k e c h)")
                y = y_ps[q % 2][:, 0:D]
                for c in range(FC):
                    h_hi, h_lo = hid_hi[:, q, c * P:(c + 1) * P], hid_lo[:, q, c * P:(c + 1) * P]
                    w_hi = w[:, bass.ds(e * (FC * D) + c * D, D)]
                    w_lo = w[:, bass.ds(e * (FC * D) + (EXPERTS * FC * D + c * D), D)]
                    nc.tensor.matmul(y, h_hi, w_hi, start=(c == 0), stop=False)
                    nc.tensor.matmul(y, h_hi, w_lo, start=False, stop=False)
                    ins = nc.tensor.matmul(y, h_lo, w_hi, start=False, stop=(c == FC - 1))
                ins.then_inc(y_ready, 1)

            def tiles(r):
                first = tile_first(r)
                pe.wait_ge(owner_ready, r + 1)
                turn_x(first, 0)
                for q in range(RING):
                    turn_x(first + q + 1, (q + 1) % RING)
                    hidden(r, first + q, q, q)
                    if q >= 2:
                        result(r, first + q - 2, q - 2, q - 2)
                with pe.Fori(1, BLOCKS - 1) as b:
                    for q in range(RING):
                        turn_x(b * RING + (first + q + 1), (q + 1) % RING) if q < RING - 1 else \
                            turn_x_next(b, first)
                        hidden(r, b * RING + (first + q), b * RING + q, q)
                        result(r, b * RING + (first + q - 2), b * RING + (q - 2), (q - 2) % RING)
                for q in range(RING):
                    i = TILES - RING + q
                    if q < RING - 1:
                        turn_x(first + i + 1, q + 1)
                    hidden(r, first + i, i, q)
                    result(r, first + i - 2, i - 2, (q - 2) % RING)
                for q in (2, 3):
                    result(r, first + TILES - RING + q, TILES - RING + q, q)

            def turn_x_next(b, first):
                turn_x(b * RING + (first + RING), 0)

            def mixer(g):
                pe.wait_ge(normed, normed_count("a", g))
                for k in range(QUADS):
                    turn(("aT", g, k), [xn[:, g, 4 * k + i, :] for i in range(4)])
                pe.wait_ge(turned_ready, g + 1)
                for k in range(QUADS):
                    key = ("conv", g, k)
                    wait_bank(pe, key)
                    for i in range(4):
                        j = 4 * k + i
                        y = bank(key)[:, i * D:(i + 1) * D]
                        edge = 0 if j == 0 else 1 if j == STEPS - 1 else None
                        if edge is not None:
                            nc.tensor.matmul(y, edge_at[:, edge, :], edge_w[:, edge, :], start=True, stop=False)
                        for tap in range(3):
                            ins = nc.tensor.matmul(y, turned[:, j + tap, :], projT[:, tap, :],
                                                   start=(tap == 0 and edge is None), stop=(tap == 2))
                    ins.then_inc(aux_full, 1)
                for k in range(QUADS):
                    key = ("v", g, k)
                    wait_bank(pe, key)
                    for i in range(4):
                        ins = nc.tensor.matmul(bank(key)[:, i * D:(i + 1) * D], turned[:, 1 + 4 * k + i, :],
                                               projT[:, 3, :], start=True, stop=True)
                    ins.then_inc(aux_full, 1)
                pe.wait_ge(conv_ready, QUADS * (g + 1))
                by_cg = mix[:, :].rearrange("p (g m) -> p g m", g=CGROUPS)
                for k in range(QUADS):
                    turn(("cT", g, k), [by_cg[:, 4 * k + i, :] for i in range(4)])
                if g == 0:
                    pe.wait_ge(ssm_mats, 1)
                for k in range(QUADS):
                    key = ("u", g, k)
                    wait_bank(pe, key)
                    pe.wait_ge(ssm_x_ready, QUADS * g + k + 1)
                    for i in range(4):
                        cg = 4 * k + i
                        ins = nc.tensor.matmul(bank(key)[:, i * P:(i + 1) * P], U[:, cg, :], ssm_x[:, cg, :],
                                               start=True, stop=True)
                    ins.then_inc(aux_full, 1)
                for k in range(QUADS):
                    key = ("y", g, k)
                    wait_bank(pe, key)
                    pe.wait_ge(states_ready, QUADS * g + k + 1)
                    for i in range(4):
                        cg = 4 * k + i
                        y = bank(key)[:, i * P:(i + 1) * P]
                        nc.tensor.matmul(y, ssm_x[:, cg, :], T[:, cg, :], start=True, stop=False)
                        ins = nc.tensor.matmul(y, states[:, cg * P:(cg + 1) * P], V[:, cg, :],
                                               start=False, stop=True)
                    ins.then_inc(aux_full, 1)
                pe.wait_ge(mix_ready, QUADS * (g + 1))
                by_step = mix[:, :].rearrange("p (j c) -> p j c", j=STEPS)
                for k in range(QUADS):
                    turn(("yT", g, k), [by_step[:, 4 * k + i, :] for i in range(4)])
                for k in range(QUADS):
                    key = ("o", g, k)
                    wait_bank(pe, key)
                    n = aux_index[("yT", g, k)]
                    pe.wait_ge(aux_free[n % 2], n // 2 + 1)
                    for i in range(4):
                        ins = nc.tensor.matmul(bank(key)[:, i * D:(i + 1) * D], turned[:, 1 + 4 * k + i, :],
                                               projT[:, 4, :], start=True, stop=True)
                    ins.then_inc(aux_full, 1)

            pe.wait_ge(pool_const, 1)
            pe.wait_ge(small_in, 16 * SMALL_LOADS)
            pe.wait_ge(small_ready, 1)
            turn(("small", 0), [tap_w[:, 0], tap_w[:, 1], tap_w[:, 2], small_w[:, 1]])
            turn(("small", 1), [small_w[:, 2], b1_rows[:, :], wr_rows[:, :]])
            pe.wait_ge(aux_free[1], 1)
            pe.wait_ge(pool_const, 2)
            for g in range(GROUPS):
                route(g)
            pe.wait_ge(ffn_in, 32)
            w1_stage = stage[:, 0].rearrange("p k j d -> p (k j) d")
            w2_stage = stage[:, 1].rearrange("p k j d -> p (k j d)").rearrange("p (e f) -> p e f", e=EXPERTS)
            for e in range(EXPERTS):
                turn(("W1T", e), [w1_stage[:, e * FC + c, :] for c in range(FC)])
            for e in range(EXPERTS):
                turn(("W2T", e), [w2_stage[:, e, c * P:(c + 1) * P] for c in range(FC)])
            pe.wait_ge(scaled_used, 2 * EXPERTS)
            for g in range(GROUPS):
                tiles(g)
            for g in range(GROUPS):
                mixer(g)
                route(GROUPS + g)
            for g in range(GROUPS):
                tiles(GROUPS + g)

        @block.vector
        def _(dve):
            steps = 0

            def settle(ins):
                nonlocal steps
                steps += 1
                ins.then_inc(v_step, 1)
                dve.wait_ge(v_step, steps)
                return ins

            def publish(ins, signal, value):
                ins.then_inc(signal, 1)
                dve.wait_ge(signal, value)

            def statistics(src, eps):
                for j in range(STEPS):
                    ins = nc.vector.bn_stats(st[:, j, :], src[:, j, :])
                settle(ins)
                nc.vector.tensor_tensor(mean[:, :], st[:, :, 1], st[:, :, 4], ALU.add)
                nc.vector.tensor_tensor(t1[:, :], st[:, :, 1], st[:, :, 4], ALU.subtract)
                settle(nc.vector.tensor_tensor(var[:, :], st[:, :, 2], st[:, :, 5], ALU.add))
                nc.vector.tensor_scalar(mean[:, :], mean[:, :], 0.5, None, ALU.mult)
                settle(nc.vector.scalar_tensor_tensor(t1[:, :], t1[:, :], 0.25, t1[:, :], ALU.mult, ALU.mult))
                settle(nc.vector.scalar_tensor_tensor(var[:, :], var[:, :], 1.0 / D, t1[:, :], ALU.mult, ALU.add))
                settle(nc.vector.tensor_scalar(var[:, :], var[:, :], eps, None, ALU.add))
                settle(nc.vector.tensor_scalar(t1[:, :].bitcast(I32), var[:, :].bitcast(I32), 1, None,
                                               ALU.arith_shift_right))
                settle(nc.vector.tensor_scalar(rstd[:, :].bitcast(I32), t1[:, :].bitcast(I32), -1.0,
                                               float(0x5F3759DF), ALU.mult, ALU.add))
                for _ in range(4):
                    settle(nc.vector.tensor_tensor(t1[:, :], var[:, :], rstd[:, :], ALU.mult))
                    settle(nc.vector.tensor_tensor(t1[:, :], t1[:, :], rstd[:, :], ALU.mult))
                    settle(nc.vector.tensor_scalar(t1[:, :], t1[:, :], -0.5, 1.5, ALU.mult, ALU.add))
                    settle(nc.vector.tensor_tensor(rstd[:, :], rstd[:, :], t1[:, :], ALU.mult))
                settle(nc.vector.scalar_tensor_tensor(shift[:, :], mean[:, :], -1.0, rstd[:, :],
                                                      ALU.mult, ALU.mult))

            def normalise(dst, src, eps):
                statistics(src, eps)
                for j in range(STEPS):
                    ins = nc.vector.tensor_scalar(dst[:, j, :], src[:, j, :], rstd[:, j:j + 1], shift[:, j:j + 1],
                                                  ALU.mult, ALU.add)
                return ins

            def route(r):
                g = r % GROUPS
                if r < GROUPS:
                    dve.wait_ge(x_in[g], 16)
                publish(normalise(xn[:, g], resid[:, g], LN_EPS_BLOCK), normed, normed_count(r))
                if r >= GROUPS:
                    dve.wait_ge(scattered[g], 16 * 2 * STEPS)
                settle(nc.vector.tensor_copy(halves[:, g, :, 0:D], xn[:, g]))
                nc.vector.tensor_tensor(halves[:, g, :, D:2 * D], xn[:, g], halves[:, g, :, 0:D],
                                        ALU.subtract).then_inc(halves_ready, 1)
                key = ("logits", r)
                wait_unit(dve, key)
                by_expert = bank(key)[:, 0:EXPERTS * STEPS].rearrange("p (j e) -> p e j", e=EXPERTS)
                ins = nc.vector.tensor_tensor(lg[:, :, :], by_expert,
                                              br_bc[:, :].unsqueeze(2).to_broadcast([P, EXPERTS, STEPS]), ALU.add)
                settle(ins)
                dve.sem_inc(aux_free[aux_index[key] % 2], 1)
                for k in range(2):
                    e_last = lg[:, :, :].rearrange("p e j -> p j e")
                    settle(nc.vector.tensor_reduce(best[k][:, :], e_last, X_AXIS, ALU.max))
                    every = [P, EXPERTS, STEPS]
                    settle(nc.vector.tensor_tensor(r1[:, :, :], lg[:, :, :],
                                                   best[k][:, :].unsqueeze(1).to_broadcast(every), ALU.is_equal))
                    settle(nc.vector.tensor_tensor(r1[:, :, :], r1[:, :, :], low_first[:, :, :], ALU.mult))
                    settle(nc.vector.tensor_reduce(t1[:, :], r1[:, :, :].rearrange("p e j -> p j e"),
                                                   X_AXIS, ALU.max))
                    settle(nc.vector.tensor_tensor(pick[k][:, :, :], low_first[:, :, :],
                                                   t1[:, :].unsqueeze(1).to_broadcast(every), ALU.is_equal))
                    if k == 0:
                        settle(nc.vector.scalar_tensor_tensor(lg[:, :, :], pick[0][:, :, :], -3e38, lg[:, :, :],
                                                              ALU.mult, ALU.add))
                nc.vector.tensor_tensor(gap[:, :], best[1][:, :], best[0][:, :], ALU.subtract).then_inc(gap_ready, 1)
                settle(nc.vector.tensor_tensor(r1[:, :, :], pick[0][:, :, :], pick[1][:, :, :], ALU.add))
                flat = "p e j -> p (e j)"
                nc.vector.tensor_tensor_scan(rank[:, :, :].rearrange(flat), not_step0[:, :, :].rearrange(flat),
                                             r1[:, :, :].rearrange(flat), 0.0, ALU.mult, ALU.add)\
                    .then_inc(ones_counted, 1)
                key = ("ranks", r)
                wait_unit(dve, key)
                settle(nc.vector.tensor_copy(counts[:, :, :], bank(key)[:, 0:2 * EXPERTS]))
                dve.sem_inc(aux_free[aux_index[key] % 2], 1)
                settle(nc.vector.tensor_scalar(whole_i[:, :], counts[:, 1, :], float(P - 1), None, ALU.add))
                shift_bits = P.bit_length() - 1
                settle(nc.vector.tensor_scalar(whole_i[:, :], whole_i[:, :], shift_bits, None,
                                               ALU.arith_shift_right))
                settle(nc.vector.tensor_scalar(whole[:, :], whole_i[:, :], float(P), None, ALU.mult))
                settle(nc.vector.tensor_tensor_scan(ends[:, :], ones[:, 0:EXPERTS], whole[:, :], 0.0,
                                                    ALU.mult, ALU.add))
                settle(nc.vector.tensor_tensor(start_f[:, :], ends[:, :], whole[:, :], ALU.subtract))
                settle(nc.vector.tensor_tensor(start_f[:, :], start_f[:, :], counts[:, 0, :], ALU.add))
                settle(nc.vector.tensor_tensor(rank[:, :, :], rank[:, :, :], r1[:, :, :], ALU.subtract))
                settle(nc.vector.tensor_tensor(rank[:, :, :], rank[:, :, :],
                                               start_f[:, :].unsqueeze(2).to_broadcast([P, EXPERTS, STEPS]), ALU.add))
                if r >= GROUPS:
                    dve.wait_ge(gathered[g], 16 * 2 * STEPS)
                for k in range(2):
                    settle(nc.vector.tensor_tensor(r1[:, :, :], rank[:, :, :], pick[k][:, :, :], ALU.mult))
                    settle(nc.vector.tensor_reduce(slot_f[:, k, :], r1[:, :, :].rearrange("p e j -> p j e"),
                                                   X_AXIS, ALU.add))
                nc.vector.tensor_copy(slots[:, g], slot_f[:, :, :]).then_inc(slots_ready, 1)
                if r >= GROUPS:
                    dve.wait_ge(y_taken, tile_first(g + 1))
                shape = [1, TILES, EXPERTS]
                settle(nc.vector.tensor_tensor(past[:, :, :], ends[0:1, :].unsqueeze(1).to_broadcast(shape),
                                               tile_start[:, :].unsqueeze(2).to_broadcast(shape), ALU.is_le))
                settle(nc.vector.tensor_reduce(owner_f[:, :], past[:, :, :], X_AXIS, ALU.add))
                nc.vector.tensor_scalar(owner[:, g], owner_f[:, :], float(EXPERTS - 1), None, ALU.min)\
                    .then_inc(owner_ready, 1)
                dve.wait_ge(gap_exp_ready, r + 1)
                settle(nc.vector.tensor_scalar(t1[:, :], gap_exp[:, :], 1.0, None, ALU.add))
                settle(nc.vector.reciprocal(share[:, g, 0, :], t1[:, :]))
                settle(nc.vector.tensor_tensor(share[:, g, 1, :], gap_exp[:, :], share[:, g, 0, :], ALU.mult))

            def find_scales():
                dve.wait_ge(ffn_in, 32)
                nc.vector.tensor_reduce(big[:, 0:1], stage[:, 0].rearrange("p k j d -> p (k j d)"), X_AXIS,
                                        ALU.max, apply_absolute_value=True)
                nc.vector.tensor_reduce(big[:, 1:2], stage[:, 1].rearrange("p k j d -> p (k j d)"), X_AXIS,
                                        ALU.max, apply_absolute_value=True)
                nc.vector.tensor_reduce(big[:, 2:3], b1T[:, :], X_AXIS, ALU.max, apply_absolute_value=True)\
                    .then_inc(max_ready, 1)
                dve.wait_ge(max_all, 1)
                settle(nc.vector.scalar_tensor_tensor(big_all[:, 2:3], big_all[:, 0:1], float(D), big_all[:, 2:3],
                                                      ALU.mult, ALU.add))
                settle(nc.vector.tensor_scalar(big_all[:, 0:3], big_all[:, 0:3], 1e-25, None, ALU.max))
                settle(nc.vector.tensor_scalar(scale_t[:, 0:3].bitcast(I32), big_all[:, 0:3].bitcast(I32),
                                               EXPONENT_BITS, None, ALU.bitwise_and))
                settle(nc.vector.reciprocal(big[:, 0:3], scale_t[:, 0:3]))
                for k, (s, inv, top) in enumerate(((S1, INV1, 13), (S2, INV2, 13), (SH, INVH, 14))):
                    nc.vector.tensor_scalar(s, big[:, k:k + 1], 2.0 ** top, None, ALU.mult)
                    settle(nc.vector.tensor_scalar(inv, scale_t[:, k:k + 1], 2.0 ** -top, None, ALU.mult))
                publish(nc.vector.tensor_tensor(INVY, INV2, INVH, ALU.mult), scales_ready, 1)

            def split_weights():
                flat1 = W1T[:, :, :, :].rearrange("p k e f -> p k (e f)")
                flat2 = W2T[:, :, :, :, :].rearrange("p k e c h -> p k (e c h)")
                for n in range(2 * EXPERTS):
                    w, at = (flat1, n) if n < EXPERTS else (flat2, n - EXPERTS)
                    at = slice(at * 512, (at + 1) * 512)
                    dve.wait_ge(scaled_ready, n + 1)
                    settle(nc.vector.tensor_copy(w[:, 0, at], scaled[:, n % 2, :]))
                    ins = nc.vector.tensor_tensor(w[:, 1, at], scaled[:, n % 2, :], w[:, 0, at], ALU.subtract)
                    ins.then_inc(scaled_used, 1)

            def ssm_constants():
                dve.wait_ge(decay_in, 1)
                dve.wait_ge(pool_const, 2)
                for k in (1, 2, 4, 8):
                    settle(nc.vector.tensor_tensor(decay[:, k + 1:2 * k + 1, :], decay[:, 1:k + 1, :],
                                                   decay[:, k:k + 1, :].to_broadcast([P, k, STATES]), ALU.mult))
                settle(nc.vector.tensor_tensor(cb[:, :], ssm_in[:, 1], ssm_in[:, 2], ALU.mult))
                settle(nc.vector.tensor_tensor(tap_terms[:, :, :], decay[:, 0:CHUNK, :],
                                               cb[:, :].unsqueeze(1).to_broadcast([P, CHUNK, STATES]), ALU.mult))
                settle(nc.vector.tensor_reduce(taps[:, CHUNK - 1:], tap_terms[:, :, :], X_AXIS, ALU.add))
                nc.vector.tensor_tensor(taps[:, CHUNK - 1:CHUNK], taps[:, CHUNK - 1:CHUNK], d_in[:, :], ALU.add)
                nc.vector.tensor_copy(readout[:, :, CHUNK], decay[:, CHUNK, :])
                nc.vector.tensor_tensor(readout[:, :, 0:CHUNK],
                                        decay[:, 1:CHUNK + 1, :].rearrange("p k s -> p s k"),
                                        cb[:, :].unsqueeze(2).to_broadcast([P, STATES, CHUNK]), ALU.mult)\
                    .then_inc(ssm_const, 1)
                settle(nc.vector.tensor_reduce(same_c[:, :], ident[:, :].rearrange("p (j c) -> p c j", c=CPG),
                                               X_AXIS, ALU.add))
                dve.wait_ge(ssm_back, 16 * 3 * CHUNK)
                shape = [P, CGROUPS, CHUNK, CPG]
                for dst, src in ((T, mT[:, :, :]), (U, mU[:, :, :]), (V, mV[:, :, 0:CHUNK])):
                    nc.vector.tensor_tensor(dst[:, :, :].rearrange("p g (t c) -> p g t c", c=CPG),
                                            src.unsqueeze(3).to_broadcast(shape),
                                            same_c[:, :].unsqueeze(1).unsqueeze(1).to_broadcast(shape), ALU.mult)
                nc.vector.tensor_tensor(
                    chunk_decay[:, :, :], mV[:, :, CHUNK:CHUNK + 1].to_broadcast([P, CGROUPS, P]),
                    keep_chunk[:, :].unsqueeze(1).to_broadcast([P, CGROUPS, P]), ALU.mult).then_inc(ssm_mats, 1)

            def split_hidden(n, q):
                dve.wait_ge(gelu_done, n + 1)
                if not (isinstance(n, int) and n < RING):
                    dve.wait_ge(y_ready, n - RING + 1)
                nc.vector.tensor_scalar(hid_hi[:, q, :], hid[:, q % 2, :], SH, None, ALU.mult).then_inc(hi_ready, 1)
                dve.wait_ge(hi_ready, n + 1)
                nc.vector.scalar_tensor_tensor(hid_lo[:, q, :], hid[:, q % 2, :], SH, hid_hi[:, q, :],
                                               ALU.mult, ALU.subtract).then_inc(h_ready, 1)

            def take_result(r, n, i, q):
                e = dve.value_load(owner[0:1, r % GROUPS, bass.ds(i, 1)], min_val=0, max_val=EXPERTS - 1)
                dve.wait_ge(y_ready, n + 1)
                if isinstance(n, int):
                    if n >= RING:
                        dve.wait_ge(tile_out[q], 16 * (n // RING))
                else:
                    dve.wait_ge(tile_out[q], (n - q) * (16 // RING))
                bias = b2_bc[:, :, :].rearrange("p e h -> p (e h)")[:, bass.ds(e * D, D)]
                nc.vector.scalar_tensor_tensor(tile_y[:, q, :], y_ps[q % 2][:, 0:D], INVY, bias,
                                               ALU.mult, ALU.add).then_inc(y_taken, 1)

            def tiles(r):
                first = tile_first(r)
                for q in range(RING):
                    split_hidden(first + q, q)
                    if q >= 2:
                        take_result(r, first + q - 2, q - 2, q - 2)
                with dve.Fori(1, BLOCKS) as b:
                    for q in range(RING):
                        split_hidden(b * RING + (first + q), q)
                        if q >= 2:
                            take_result(r, b * RING + (first + q - 2), b * RING + (q - 2), q - 2)
                        else:
                            take_result(r, b * RING + (first + q - 2), b * RING + (q - 2), q + 2)
                for q in (2, 3):
                    take_result(r, first + TILES - RING + q, TILES - RING + q, q)

            def combine(r):
                g = r % GROUPS
                dve.wait_ge(gathered[g], 16 * 2 * STEPS * (r // GROUPS + 1))
                z = xn[:, g]
                for k in range(2):
                    for j in range(STEPS):
                        ins = nc.vector.scalar_tensor_tensor(z[:, j, :], stage[:, g, k, j, :], share[:, g, k, j:j + 1],
                                                             z[:, j, :], ALU.mult, ALU.add)
                    settle(ins)
                dve.sem_inc(combined, 1)
                settle(normalise(z, z, LN_EPS_FFN))
                row_shape = [P, STEPS, D]
                settle(nc.vector.tensor_tensor(z, z, half_w_bc[:, :].unsqueeze(1).to_broadcast(row_shape), ALU.mult))
                settle(nc.vector.tensor_tensor(z, z, half_b_bc[:, :].unsqueeze(1).to_broadcast(row_shape), ALU.add))
                settle(nc.vector.tensor_tensor(resid[:, g], resid[:, g], z, ALU.add))

            def mixer(g):
                normalise(xn[:, g], resid[:, g], LN_EPS_BLOCK).then_inc(normed, 1)
                for k in range(QUADS):
                    key = ("conv", g, k)
                    wait_unit(dve, key)
                    shape = [P, 4, CGROUPS, CPG]
                    by_cg = mix[:, :].rearrange("p (g j c) -> p j g c", g=CGROUPS, c=CPG)
                    freed(nc.vector.tensor_tensor(
                        by_cg[:, 4 * k:4 * k + 4], bank(key)[:, :].rearrange("p (j g c) -> p j g c", j=4, c=CPG),
                        convb_bc[:, :].rearrange("p (g c) -> p g c", c=CPG).unsqueeze(1).to_broadcast(shape),
                        ALU.add), key)
                    dve.wait_ge(aux_free[aux_index[key] % 2], aux_index[key] // 2 + 1)
                    dve.sem_inc(conv_ready, 1)
                for k in range(QUADS):
                    key = ("v", g, k)
                    wait_unit(dve, key)
                    freed(nc.vector.tensor_tensor(
                        gate[:, 4 * k:4 * k + 4, :], bank(key)[:, :].rearrange("p (j c) -> p j c", j=4),
                        v1b_bc[:, :].unsqueeze(1).to_broadcast([P, 4, D]), ALU.add), key)
                    dve.wait_ge(aux_free[aux_index[key] % 2], aux_index[key] // 2 + 1)
                    dve.sem_inc(gate_in, 1)
                for k in range(QUADS):
                    key = ("u", g, k)
                    wait_unit(dve, key)
                    at = states[:, 1 + 4 * k * P:1 + 4 * (k + 1) * P]
                    settle(nc.vector.tensor_tensor_scan(
                        at, chunk_decay[:, 4 * k:4 * k + 4, :].rearrange("p g n -> p (g n)"), bank(key)[:, :], 0.0,
                        ALU.mult, ALU.add))
                    dve.sem_inc(aux_free[aux_index[key] % 2], 1)
                    nc.vector.memset(at[:, CHUNKS_PER_SEQ - 1:4 * P:CHUNKS_PER_SEQ], 0.0).then_inc(states_ready, 1)
                dve.wait_ge(gate_ready, QUADS * (g + 1))
                for k in range(QUADS):
                    key = ("y", g, k)
                    wait_unit(dve, key)
                    view = "p (g t c) -> p g t c"
                    freed(nc.vector.tensor_tensor(
                        mix[:, :].rearrange("p (t g c) -> p g t c", g=CGROUPS, c=CPG)[:, 4 * k:4 * k + 4],
                        bank(key)[:, :].rearrange(view, g=4, c=CPG),
                        gate[:, :, :].rearrange("p t (g c) -> p g t c", c=CPG)[:, 4 * k:4 * k + 4], ALU.mult), key)
                    dve.wait_ge(aux_free[aux_index[key] % 2], aux_index[key] // 2 + 1)
                    dve.sem_inc(mix_ready, 1)
                for k in range(QUADS):
                    key = ("o", g, k)
                    wait_unit(dve, key)
                    x_at = resid[:, g, 4 * k:4 * k + 4, :]
                    ins = nc.vector.tensor_tensor(x_at, x_at, bank(key)[:, :].rearrange("p (j c) -> p j c", j=4),
                                                  ALU.add)
                    freed(ins, key)
                    dve.wait_ge(aux_free[aux_index[key] % 2], aux_index[key] // 2 + 1)
                settle(nc.vector.tensor_tensor(resid[:, g], resid[:, g],
                                               w2b_bc[:, :].unsqueeze(1).to_broadcast([P, STEPS, D]), ALU.add))

            dve.wait_ge(small_in, 16 * SMALL_LOADS)
            for k in range(3):
                ins = nc.vector.tensor_scalar(tap_w[:, k, :], small_w[:, 0, :], conv_c[:, k:k + 1], None, ALU.mult)
            ins.then_inc(small_ready, 1)
            dve.wait_ge(pool_const, 1)
            nc.vector.tensor_copy(ident16[:, :], ident[:, :])
            nc.vector.tensor_scalar(half_w_bc[:, :], half_w_bc[:, :], 0.5, None, ALU.mult)
            nc.vector.tensor_scalar(half_b_bc[:, :], half_b_bc[:, :], 0.5, None, ALU.mult)
            for edge, tap in ((0, 0), (1, 2)):
                nc.vector.scalar_tensor_tensor(edge_w[:, edge, :], w1b_bc[0:1, :], -1.0, conv_bc[0:1, :, tap],
                                               ALU.mult, ALU.mult)
            settle(nc.vector.tensor_reduce(convb_bc[:, :], conv_bc[:, :, :], X_AXIS, ALU.add))
            settle(nc.vector.tensor_tensor(convb_bc[:, :], convb_bc[:, :], w1b_bc[:, :], ALU.mult))
            dve.wait_ge(pool_const, 2)
            route(0)
            dve.wait_ge(aux_free[1], 1)
            find_scales()
            for g in range(1, GROUPS):
                route(g)
            split_weights()
            ssm_constants()
            for g in range(GROUPS):
                tiles(g)
            for g in range(GROUPS):
                combine(g)
                mixer(g)
                route(GROUPS + g)
            for g in range(GROUPS):
                tiles(GROUPS + g)
            for g in range(GROUPS):
                combine(GROUPS + g)
                dve.sem_inc(x_final, 1)


_INS = ["x", "w1_w", "w1_b", "v1_w", "v1_b", "w2_w", "w2_b", "conv_w", "A", "B_ssm", "C_ssm", "D_ssm",
        "Wr", "br", "W1", "b1", "W2", "b2", "ln_w", "ln_b"]


def kernel(**inputs):
    import numpy as np
    import concourse.bacc as bacc
    from concourse.bass_utils import run_bass_kernel_spmd

    nc = bacc.Bacc("TRN2", target_bir_lowering=False, num_devices=1)
    arrays, args = {}, []
    for n, name in enumerate(_INS):
        a = np.ascontiguousarray(inputs[("L0_attn_" if n < 12 else "L0_ffn_") + name])
        arrays["in_" + name] = a
        args.append(nc.dram_tensor("in_" + name, a.shape, F32, kind="ExternalInput").ap())
    args.append(nc.dram_tensor("out_x", (BATCH, SEQ, D), F32, kind="ExternalOutput").ap())
    build(nc, *args)
    return run_bass_kernel_spmd(nc, [arrays], core_ids=[0]).results[0]["out_x"]
```

```python
from collections import namedtuple
from contextlib import ExitStack

import concourse.bass as bass
from concourse import mybir

F32 = mybir.dt.float32
F16 = mybir.dt.float16
I32 = mybir.dt.int32
ALU = mybir.AluOpType
ACT = mybir.ActivationFunctionType
X_AXIS = mybir.AxisListType.X

P = 128
D = 128
BATCH, SEQ = 8, 512
GROUPS = 2
CHUNK = 16
STEPS = CHUNK
TOKENS = BATCH * SEQ // GROUPS
SEQS = BATCH // GROUPS
CHUNKS_PER_SEQ = SEQ // CHUNK
EXPERTS = 8
HIDDEN = 512
FC = HIDDEN // P
TILE = 2 * P
RING = 4
PEELED = RING - 1
ROUNDS = -(-(2 * TOKENS // TILE + EXPERTS - 1 - PEELED) // RING)
TILES = PEELED + ROUNDS * RING
OWNER_PAD = RING + 1 - PEELED
DIGIT = 3
SLOTS = TILES * TILE
STATES = 16
CPG = P // CHUNK
CGROUPS = D // CPG
QUADS = STEPS // 4
LN_EPS_BLOCK = 1e-5
LN_EPS_FFN = 1e-12
RUNS = 2 * GROUPS
EXPONENT_BITS = 0x7F800000

Tile = namedtuple("Tile", "n half half_laps slot slot_laps")


def tile_at(start, rounds):
    return Tile(rounds * RING + start, start % 2, rounds * (RING // 2) + start // 2, start % RING, rounds + start // RING)


def early(tile):
    return isinstance(tile.n, int) and tile.n < 2


def build(nc, x, w1_w, w1_b, v1_w, v1_b, w2_w, w2_b, conv_w, A, B_ssm, C_ssm, D_ssm,
          Wr, br, W1, b1, W2, b2, ln_w, ln_b, out):
    ctx = ExitStack()
    with ctx:
        def sb(name, shape, dt=F32):
            return ctx.enter_context(nc.sbuf_tensor(name, shape, dt))

        def sem(name):
            return ctx.enter_context(nc.semaphore(name))

        slot_x = [nc.dram_tensor(f"slot_x{g}", (SLOTS, 2 * D), F16).ap() for g in range(GROUPS)]
        slot_y = [nc.dram_tensor(f"slot_y{g}", (SLOTS, D), F32).ap() for g in range(GROUPS)]
        taps_dram = nc.dram_tensor("taps_dram", (D, 2 * CHUNK - 1), F32).ap()
        decay_dram = nc.dram_tensor("decay_dram", (D, CHUNK + 1, STATES), F32).ap()
        readout_dram = nc.dram_tensor("readout_dram", (D, STATES, CHUNK + 1), F32).ap()

        z_ps = [ctx.enter_context(nc.psum_tensor(f"z_ps{i}", [P, FC, TILE], F32)) for i in range(2)]
        y_ps = [ctx.enter_context(nc.psum_tensor(f"y_ps{i}", [P, 512], F32)) for i in range(2)]
        banks = [ctx.enter_context(nc.psum_tensor(f"aux_ps{i}", [P, 512], F32))[:, :] for i in range(2)]
        banks += [z_ps[k // 2][:, 2 * (k % 2):2 * (k % 2) + 2, :].rearrange("p c n -> p (c n)") for k in range(4)]
        BANKS = len(banks)

        resid = sb("resid", [P, GROUPS, STEPS, D])
        xn = sb("xn", [P, GROUPS, STEPS, D])
        halves = sb("halves", [P, GROUPS, STEPS, 2 * D], F16)
        stage = sb("stage", [P, GROUPS, 2, STEPS, D])
        W1T = sb("W1T", [P, 2, EXPERTS, HIDDEN], F16)
        W2T = sb("W2T", [P, 2, EXPERTS, FC, D], F16)
        b1T = sb("b1T", [P, EXPERTS * FC])
        b1_rows = sb("b1_rows", [EXPERTS * FC, P])
        b2_bc = sb("b2_bc", [P, EXPERTS, D])
        br_bc = sb("br_bc", [P, EXPERTS])
        half_w_bc = sb("half_w_bc", [P, D])
        half_b_bc = sb("half_b_bc", [P, D])
        ident = sb("ident", [P, P])
        before = sb("before", [P, P])
        ones = sb("ones", [P, P])
        low_first = sb("low_first", [P, EXPERTS, STEPS])
        not_step0 = sb("not_step0", [P, EXPERTS, STEPS])
        tile_start = sb("tile_start", [1, TILES])
        WrT = sb("WrT", [P, EXPERTS])
        wr_rows = sb("wr_rows", [EXPERTS, D])
        projT = sb("projT", [P, 5, D])
        conv_c = sb("conv_c", [P, 3])
        w1b_bc = sb("w1b_bc", [P, D])
        convb_bc = sb("convb_bc", [P, D])
        edge_w = sb("edge_w", [1, 2, D])
        edge_at = sb("edge_at", [1, 2, P])
        v1b_bc = sb("v1b_bc", [P, D])
        w2b_bc = sb("w2b_bc", [P, D])
        ssm_in = sb("ssm_in", [P, 3, STATES])
        d_in = sb("d_in", [P, 1])
        decay = sb("decay", [P, CHUNK + 1, STATES])
        cb = sb("cb", [P, STATES])
        taps = sb("taps", [P, 2 * CHUNK - 1])
        readout = sb("readout", [P, STATES, CHUNK + 1])
        mT = sb("mT", [P, CGROUPS, CHUNK])
        mU = sb("mU", [P, CGROUPS, STATES])
        mV = sb("mV", [P, CGROUPS, CHUNK + 1])
        same_c = sb("same_c", [P, CPG])
        T = sb("T", [P, CGROUPS, CHUNK * CPG])
        U = sb("U", [P, CGROUPS, STATES * CPG])
        V = sb("V", [P, CGROUPS, CHUNK * CPG])
        keep_chunk = sb("keep_chunk", [P, P])
        chunk_decay = sb("chunk_decay", [P, CGROUPS, P])
        turned = sb("turned", [P, STEPS + 2, P])
        states = sb("states", [P, 1 + CGROUPS * P])
        tile_x = [sb(f"tile_x{k}", [P, 2, TILE], F16)[:, :, :] for k in range(2)]
        tile_x += [a[:, :, :].rearrange("p a b -> p (a b)")[:, 0:TILE].bitcast(F16).rearrange(
            "p (k n) -> p k n", k=2) for a in (decay, readout)]
        hid = sb("hid", [P, 2, FC, TILE])
        hid_hi = sb("hid_hi", [P, 2, FC, TILE], F16)
        hid_lo = sb("hid_lo", [P, 2, FC, TILE], F16)
        tile_y = sb("tile_y", [P, 2, 2, D])
        mix = stage[:, 0, 0].rearrange("p j d -> p (j d)")
        ssm_x = stage[:, 0, 1]
        gate = halves[:, 1].rearrange("p j d -> p (j d)").bitcast(F32).rearrange("p (j d) -> p j d", j=STEPS)
        setup = iter(range(1, 1 + 4 * 3 * D, 3 * D))

        def setup_rows(shape):
            at = next(setup)
            flat = states[:, at:at + shape[0] * shape[1]]
            return flat.rearrange("p (a b) -> p a b", a=shape[0])

        small_w = setup_rows([3, D])
        tap_w = setup_rows([3, D])
        conv_bc = setup_rows([D, 3])
        tap_terms = setup_rows([CHUNK, STATES])
        st = sb("st", [P, STEPS, 6])
        mean = sb("mean", [P, STEPS])
        var = sb("var", [P, STEPS])
        rstd = sb("rstd", [P, STEPS])
        shift = sb("shift", [P, STEPS])
        t1 = sb("t1", [P, STEPS])
        t2 = sb("t2", [P, STEPS])
        lg = sb("lg", [P, EXPERTS, STEPS])
        r1 = sb("r1", [P, EXPERTS, STEPS])
        pick = [sb(f"pick{k}", [P, EXPERTS, STEPS]) for k in range(2)]
        rank = sb("rank", [P, EXPERTS, STEPS])
        best = [sb(f"best{k}", [P, STEPS]) for k in range(2)]
        gap = sb("gap", [P, STEPS])
        gap_exp = sb("gap_exp", [P, STEPS])
        share = sb("share", [P, GROUPS, 2, STEPS])
        counts = sb("counts", [P, 2, EXPERTS])
        whole_i = sb("whole_i", [P, EXPERTS], I32)
        whole = sb("whole", [P, EXPERTS])
        ends = sb("ends", [P, EXPERTS])
        start_f = sb("start_f", [P, EXPERTS])
        slot_f = sb("slot_f", [P, 2, STEPS])
        slots = sb("slots", [P, GROUPS, 2, STEPS], I32)
        past = hid_hi[0:1].rearrange("p k c n -> p (k c n)").bitcast(F32)[:, 0:TILES * EXPERTS].rearrange(
            "p (i e) -> p i e", e=EXPERTS)
        owner_f = sb("owner_f", [1, OWNER_PAD + TILES])
        owners_f = sb("owners_f", [1, ROUNDS + 1])
        owners = sb("owners", [1, GROUPS, ROUNDS + 1], I32)
        zero_rows = tile_y[:, 0]
        big = sb("big", [P, 4])
        big_all = sb("big_all", [P, 4])
        scale_t = sb("scale_t", [P, 4])
        scales = sb("scales", [P, 8])
        S1, INV1, S2, INV2, SH, INVH, INVY = (scales[:, k:k + 1] for k in range(7))

        x_in = [sem(f"x_in{g}") for g in range(GROUPS)]
        small_in = sem("small_in")
        ffn_in = sem("ffn_in")
        pool_const = sem("pool_const")
        pool_step = sem("pool_step")
        zeros_ready = sem("zeros_ready")
        zeroed = [sem(f"zeroed{g}") for g in range(GROUPS)]
        v_step = sem("v_step")
        small_ready = sem("small_ready")
        normed = sem("normed")
        halves_ready = sem("halves_ready")
        slots_ready = sem("slots_ready")
        owner_ready = sem("owner_ready")
        gap_ready = sem("gap_ready")
        gap_exp_ready = sem("gap_exp_ready")
        ones_counted = sem("ones_counted")
        max_ready = sem("max_ready")
        max_all = sem("max_all")
        scales_ready = sem("scales_ready")
        weight_hi = sem("weight_hi")
        weights_ready = sem("weights_ready")
        half_b_added = sem("half_b_added")
        half_b_ready = sem("half_b_ready")
        w2b_added = sem("w2b_added")
        decay_in = sem("decay_in")
        ssm_const = sem("ssm_const")
        ssm_dram = sem("ssm_dram")
        ssm_back = sem("ssm_back")
        ssm_mats = sem("ssm_mats")
        aux_full = sem("aux_full")
        aux_free = [sem(f"aux_free{b}") for b in range(BANKS)]
        scattered = [sem(f"scattered{g}") for g in range(GROUPS)]
        gathered = [[sem(f"gathered{g}_{part}") for part in range(2)] for g in range(GROUPS)]
        combined = sem("combined")
        tile_in = [sem(f"tile_in{k}") for k in range(RING)]
        tile_out = [sem(f"tile_out{h}") for h in range(2)]
        z_ready = sem("z_ready")
        gelu_done = sem("gelu_done")
        hi_ready = sem("hi_ready")
        h_ready = sem("h_ready")
        y_ready = sem("y_ready")
        y_taken = sem("y_taken")
        turned_ready = sem("turned_ready")
        conv_ready = sem("conv_ready")
        gate_in = sem("gate_in")
        gate_ready = sem("gate_ready")
        ssm_x_ready = sem("ssm_x_ready")
        states_ready = sem("states_ready")
        mix_ready = sem("mix_ready")
        x_out = sem("x_out")
        x_final = sem("x_final")

        def turned_units(r):
            return [("xnT", r, k) for k in range(QUADS)]

        aux = [("small", 0), ("small", 1)] + turned_units(0) + [("logits", 0), ("ranks", 0)] + turned_units(1)
        aux += [("W1T", k) for k in range(EXPERTS)] + [("W2T", k) for k in range(EXPERTS)]
        aux += [("logits", 1), ("ranks", 1)]
        for g in range(GROUPS):
            for kind in ("aT", "conv", "v", "cT", "u", "y", "yT", "o"):
                aux += [(kind, g, k) for k in range(QUADS)]
            aux += turned_units(GROUPS + g) + [("logits", GROUPS + g), ("ranks", GROUPS + g)]
        aux_index = {key: n for n, key in enumerate(aux)}

        def bank(key):
            return banks[aux_index[key] % BANKS]

        def wait_bank(pe, key):
            n = aux_index[key]
            if n >= BANKS:
                pe.wait_ge(aux_free[n % BANKS], n // BANKS)

        def wait_unit(eng, key):
            eng.wait_ge(aux_full, aux_index[key] + 1)

        def wait_emptied(eng, key):
            n = aux_index[key]
            eng.wait_ge(aux_free[n % BANKS], n // BANKS + 1)

        def freed(ins, key):
            ins.then_inc(aux_free[aux_index[key] % BANKS], 1)

        def free_now(eng, key):
            eng.sem_inc(aux_free[aux_index[key] % BANKS], 1)

        def token_rows(ap, g):
            return ap[g * TOKENS:(g + 1) * TOKENS, :].rearrange("(p j) d -> p j d", p=P)

        def normed_before(*key):
            order = [(r,) for r in range(GROUPS)]
            for g in range(GROUPS):
                order += [("a", g), (GROUPS + g,)]
            return QUADS * order.index(key)

        def wait_gathered(eng, g, times, parts=(0, 1)):
            for part in parts:
                eng.wait_ge(gathered[g][part], 16 * STEPS * times)

        x_rows = x.rearrange("b t d -> (b t) d")
        out_rows = out.rearrange("b t d -> (b t) d")

        def row(ap):
            return ap.rearrange("(a n) -> a n", a=1)

        def uses(half, n):
            return (n + 1 - half) // 2

        def experts(word):
            return [(word >> (DIGIT * k)) & (EXPERTS - 1) for k in range(RING + 1)]

        def run_tiles(eng, r, step):
            first = r * TILES
            words = owners[0:1, r % GROUPS, :]
            top = 2 ** (DIGIT * (RING + 1)) - 1
            e = experts(eng.value_load(words[:, 0:1], min_val=0, max_val=top))[-PEELED:]
            for k in range(PEELED):
                step(tile_at(first + k, 0), e[k], tile_at(first + k - 1, 0), e[k - 1] if k else None)
            with eng.Fori(1, ROUNDS + 1) as rounds:
                e = experts(eng.value_load(words[:, bass.ds(rounds, 1)], min_val=0, max_val=top))
                for k in range(RING):
                    start = first + PEELED - RING + k
                    step(tile_at(start, rounds), e[k + 1], tile_at(start - 1, rounds), e[k])

        def last_tile(eng, r):
            word = eng.value_load(owners[0:1, r % GROUPS, ROUNDS:ROUNDS + 1], min_val=0,
                                  max_val=2 ** (DIGIT * (RING + 1)) - 1)
            return tile_at((r + 1) * TILES - 1, 0), experts(word)[-1]

        def final_parts(r):
            half = STEPS // 2
            return [slice(0, half), slice(half, STEPS)] if r == RUNS - 1 else [slice(0, STEPS)]

        SMALL_LOADS = 18
        block = ctx.enter_context(nc.Block())

        def weight_unit(n):
            if n < EXPERTS:
                key, w = ("W1T", n), W1T[:, :, :, :].rearrange("p k e f -> p k (e f)")
            else:
                key, w = ("W2T", n - EXPERTS), W2T[:, :, :, :, :].rearrange("p k e c h -> p k (e c h)")
            return key, w, slice(key[1] * HIDDEN, (key[1] + 1) * HIDDEN)

        @block.sync
        def _(sp):
            sp.dma_start(resid[:, 0], token_rows(x_rows, 0)).then_inc(x_in[0], 16)
            for dst, src in ((wr_rows[:, :], Wr), (br_bc[:, :], row(br).to_broadcast([P, EXPERTS])),
                             (small_w[:, 0], w1_w), (small_w[:, 1], v1_w), (small_w[:, 2], w2_w),
                             (b1_rows[:, :], b1.rearrange("e (c f) -> (e c) f", f=P)),
                             (conv_c[:, :], conv_w.rearrange("c a k -> c (a k)")),
                             (conv_bc[:, :, :], conv_w.rearrange("c a k -> a c k").to_broadcast([P, D, 3])),
                             (w1b_bc[:, :], row(w1_b).to_broadcast([P, D])),
                             (v1b_bc[:, :], row(v1_b).to_broadcast([P, D])),
                             (w2b_bc[:, :], row(w2_b).to_broadcast([P, D])),
                             (half_w_bc[:, :], row(ln_w).to_broadcast([P, D])),
                             (half_b_bc[:, :], row(ln_b).to_broadcast([P, D])),
                             (ssm_in[:, 0], A), (ssm_in[:, 1], B_ssm), (ssm_in[:, 2], C_ssm),
                             (d_in[:, :], D_ssm.rearrange("(c a) -> c a", a=1)),
                             (b2_bc[:, :, :], b2.rearrange("(a e) h -> a e h", a=1).to_broadcast([P, EXPERTS, D]))):
                sp.dma_start(dst, src).then_inc(small_in, 16)
            for g in range(1, GROUPS):
                sp.dma_start(resid[:, g], token_rows(x_rows, g)).then_inc(x_in[g], 16)

            sp.wait_ge(zeros_ready, 1)
            for g in range(GROUPS):
                sp.dma_start(slot_x[g].rearrange("(p a) d -> p a d", p=P),
                             zero_rows[:, 0:1, :].bitcast(F16).to_broadcast([P, SLOTS // P, 2 * D]))\
                    .then_inc(zeroed[g], 16)
            sp.wait_ge(ssm_const, 1)
            sp.dma_start(taps_dram, taps[:, :]).then_inc(ssm_dram, 16)
            sp.dma_start(decay_dram, decay[:, :, :]).then_inc(ssm_dram, 16)
            sp.dma_start(readout_dram, readout[:, :, :]).then_inc(ssm_dram, 16)
            sp.wait_ge(ssm_dram, 48)
            for j in range(CHUNK):
                at = slice(j * CPG, (j + 1) * CPG)
                back = CHUNK - 1 - j
                sp.dma_start(mT[at], taps_dram.rearrange("(g c) t -> c g t", c=CPG)[:, :, back:back + CHUNK])\
                    .then_inc(ssm_back, 16)
                sp.dma_start(mU[at], decay_dram.rearrange("(g c) k s -> c g k s", c=CPG)[:, :, back, :])\
                    .then_inc(ssm_back, 16)
                sp.dma_start(mV[at], readout_dram.rearrange("(g c) s t -> c g s t", c=CPG)[:, :, j, :])\
                    .then_inc(ssm_back, 16)

            def load_tile(r, i, tile):
                if not (isinstance(tile.n, int) and tile.n < RING):
                    sp.wait_ge(z_ready, tile.n + (1 - RING))
                sp.dma_start_transpose(out=tile_x[tile.slot], in_=slot_x[r % GROUPS][bass.ds(i * TILE, TILE), :])\
                    .then_inc(tile_in[tile.slot], 16)

            def store_tile(r, i, tile):
                sp.wait_ge(y_taken, tile.n + 1)
                sp.dma_start(slot_y[r % GROUPS][bass.ds(i * TILE, TILE), :].rearrange("(a p) d -> p a d", p=P),
                             tile_y[:, tile.half]).then_inc(tile_out[tile.half], 16)

            for r in range(RUNS):
                g, first = r % GROUPS, r * TILES

                def start_run(r):
                    g = r % GROUPS
                    sp.wait_ge(scattered[g], 16 * 2 * STEPS * (r // GROUPS + 1))
                    if r >= GROUPS:
                        wait_gathered(sp, g, 1)

                if g == 0:
                    start_run(r)
                    for i in range(RING):
                        load_tile(r, i, tile_at(first + i, 0))
                for i in range(PEELED):
                    store_tile(r, i, tile_at(first + i, 0))
                    load_tile(r, i + RING, tile_at(first + i + RING, 0))
                with sp.Fori(1, ROUNDS) as rounds:
                    for k in range(RING):
                        i = PEELED - RING + k
                        store_tile(r, rounds * RING + i, tile_at(first + i, rounds))
                        load_tile(r, rounds * RING + (i + RING), tile_at(first + i + RING, rounds))
                for i in range(TILES - RING, TILES):
                    store_tile(r, i, tile_at(first + i, 0))
                    if g < GROUPS - 1:
                        if i == TILES - RING:
                            start_run(r + 1)
                        load_tile(r + 1, i - (TILES - RING), tile_at(first + i + RING, 0))
            stores = [(g, part) for g in range(GROUPS) for part in final_parts(GROUPS + g)]
            for n, (g, at) in enumerate(stores):
                sp.wait_ge(x_final, n + 1)
                sp.dma_start(token_rows(out_rows, g)[:, at], resid[:, g, at]).then_inc(x_out, 16)
            sp.wait_ge(x_out, 16 * len(stores))
            for half in range(2):
                sp.wait_ge(tile_out[half], 16 * uses(half, TILES * RUNS))

        @block.gpsimd
        def _(pool):
            steps = 0

            def settle(ins):
                nonlocal steps
                steps += 1
                ins.then_inc(pool_step, 1)
                pool.wait_ge(pool_step, steps)

            nc.gpsimd.memset(zero_rows[:, 0, :], 0.0).then_inc(zeros_ready, 1)
            nc.gpsimd.memset(ones[:, :], 1.0)
            nc.gpsimd.memset(before[:, :], 1.0)
            settle(nc.gpsimd.memset(ident[:, :], 0.0))
            nc.gpsimd.affine_select(out=ident[:, :], in_=ident[:, :], compare_op=ALU.not_equal, fill=1.0,
                                    base=0, pattern=[[-1, P]], channel_multiplier=1).then_inc(pool_const, 1)
            nc.gpsimd.affine_select(out=before[:, :], in_=before[:, :], compare_op=ALU.is_gt, fill=0.0,
                                    base=0, pattern=[[1, P]], channel_multiplier=-1)
            for e in range(EXPERTS):
                nc.gpsimd.memset(low_first[:, e, :], float(EXPERTS - e))
            nc.gpsimd.iota(tile_start[:, :], pattern=[[TILE, TILES]], base=0, channel_multiplier=0,
                           allow_small_or_imprecise_dtypes=True)
            nc.gpsimd.memset(owner_f[:, :], 0.0)
            settle(nc.gpsimd.memset(not_step0[:, :, :], 1.0))
            settle(nc.gpsimd.memset(keep_chunk[:, :], 1.0))
            settle(nc.gpsimd.memset(edge_at[:, :, :], 0.0))
            nc.gpsimd.memset(not_step0[:, :, 0:1], 0.0)
            nc.gpsimd.memset(keep_chunk[:, 0:P:CHUNKS_PER_SEQ], 0.0)
            nc.gpsimd.memset(edge_at[:, 0, 0:P:CHUNKS_PER_SEQ], 1.0)
            nc.gpsimd.memset(edge_at[:, 1, CHUNKS_PER_SEQ - 1:P:CHUNKS_PER_SEQ], 1.0)
            nc.gpsimd.memset(turned[:, 0, :], 0.0)
            nc.gpsimd.memset(turned[:, STEPS + 1, :], 0.0)
            nc.gpsimd.memset(taps[:, 0:CHUNK - 1], 0.0)
            nc.gpsimd.memset(decay[:, 0, :], 1.0)
            nc.gpsimd.memset(states[:, 0:1], 0.0).then_inc(pool_const, 1)

            def scatter(r):
                g, f = r % GROUPS, r // GROUPS
                if f == 0:
                    pool.wait_ge(zeroed[g], 16)
                else:
                    for slot in range(RING):
                        pool.wait_ge(tile_in[slot], 16 * len(range(slot, TILES * (g + 1), RING)))
                pool.wait_ge(halves_ready, r + 1)
                pool.wait_ge(slots_ready, r + 1)
                for k in range(2):
                    for j in range(STEPS):
                        pool.indirect_dma_start(
                            out=slot_x[g], in_=halves[:, g, j, :], in_offset=None,
                            out_offset=bass.IndirectOffsetOnAxis(ap=slots[:, g, k, j:j + 1], axis=0))\
                            .then_inc(scattered[g], 16)

            def gather(r):
                g, f = r % GROUPS, r // GROUPS
                for half in range(2):
                    pool.wait_ge(tile_out[half], 16 * uses(half, TILES * (r + 1)))
                if f:
                    pool.wait_ge(combined, g + 1)
                else:
                    pool.wait_ge(weights_ready, 1)
                for j in range(STEPS):
                    for k in range(2):
                        pool.indirect_dma_start(
                            out=stage[:, g, k, j, :], out_offset=None, in_=slot_y[g],
                            in_offset=bass.IndirectOffsetOnAxis(ap=slots[:, g, k, j:j + 1], axis=0))\
                            .then_inc(gathered[g][j * 2 // STEPS], 16)

            def ssm_matrices():
                pool.wait_ge(ssm_const, 1)
                pool.wait_ge(ssm_back, 16 * 3 * CHUNK)
                shape = [P, CGROUPS, CHUNK, CPG]
                for dst, src in ((T, mT[:, :, :]), (U, mU[:, :, :]), (V, mV[:, :, 0:CHUNK])):
                    nc.gpsimd.tensor_tensor(dst[:, :, :].rearrange("p g (t c) -> p g t c", c=CPG),
                                            src.unsqueeze(3).to_broadcast(shape),
                                            same_c[:, :].unsqueeze(1).unsqueeze(1).to_broadcast(shape), ALU.mult)
                nc.gpsimd.tensor_tensor(
                    chunk_decay[:, :, :], mV[:, :, CHUNK:CHUNK + 1].to_broadcast([P, CGROUPS, P]),
                    keep_chunk[:, :].unsqueeze(1).to_broadcast([P, CGROUPS, P]), ALU.mult).then_inc(ssm_mats, 1)

            def add_to_rows(g, bias, signal):
                nc.gpsimd.tensor_tensor(resid[:, g], resid[:, g],
                                        bias[:, :].unsqueeze(1).to_broadcast([P, STEPS, D]), ALU.add)\
                    .then_inc(signal, 1)

            pool.wait_ge(max_ready, 1)
            nc.gpsimd.partition_all_reduce(big_all[:, 0:3], big[:, 0:3], P,
                                           bass.bass_isa.ReduceOp.max).then_inc(max_all, 1)
            pool.wait_ge(half_b_ready, 1)
            for g in range(GROUPS):
                scatter(g)
            ssm_matrices()
            for g in range(GROUPS):
                add_to_rows(g, half_b_bc, half_b_added)
            for g in range(GROUPS):
                gather(g)
            for g in range(GROUPS):
                pool.wait_ge(normed, normed_before("a", g) + QUADS)
                add_to_rows(g, w2b_bc, w2b_added)
                scatter(GROUPS + g)
            for g in range(GROUPS):
                add_to_rows(g, half_b_bc, half_b_added)
            for g in range(GROUPS):
                gather(GROUPS + g)
            for g in range(GROUPS):
                wait_gathered(pool, g, 2)

        @block.scalar
        def _(act):
            w1_stage = stage[:, 0].rearrange("p k j d -> p (k j) d")
            w2_stage = stage[:, 1].rearrange("p k j d -> p (k j d)").rearrange("p (e f) -> p e f", e=EXPERTS)
            act.wait_ge(x_in[0], 16)
            act.dma_start(w1_stage, W1.rearrange("e (c f) d -> f (e c) d", f=P)).then_inc(ffn_in, 16)
            act.dma_start(w2_stage, W2.rearrange("e h f -> h e f")).then_inc(ffn_in, 16)
            act.wait_ge(small_in, 16 * SMALL_LOADS)
            nc.scalar.activation(decay[:, 1, :], ssm_in[:, 0], ACT.Sigmoid).then_inc(decay_in, 1)

            def copy_small():
                wait_unit(act, ("small", 0))
                freed(nc.scalar.activation(projT[:, 0:4, :], bank(("small", 0)), ACT.Copy), ("small", 0))
                wait_unit(act, ("small", 1))
                nc.scalar.activation(projT[:, 4, :], bank(("small", 1))[:, 0:P], ACT.Copy)
                nc.scalar.activation(b1T[:, :], bank(("small", 1))[:, P:P + EXPERTS * FC], ACT.Copy)
                ins = nc.scalar.activation(WrT[:, :], bank(("small", 1))[:, 2 * P:2 * P + EXPERTS], ACT.Copy)
                freed(ins, ("small", 1))

            def copy_turned(kind, r, k, last_reader):
                if k == 0 and last_reader is not None:
                    wait_unit(act, last_reader)
                key = (kind, r, k)
                wait_unit(act, key)
                src = bank(key)
                ins = nc.scalar.activation(turned[:, 1 + 4 * k:5 + 4 * k, :], src, ACT.Copy)
                if kind == "aT" and k in (0, QUADS - 1):
                    m = CHUNKS_PER_SEQ
                    seqs = src.rearrange("d (i s c) -> d i s c", i=4, c=m)
                    if k == 0:
                        ins = nc.scalar.activation(
                            turned[:, STEPS + 1, :].rearrange("d (s c) -> d s c", c=m)[:, :, 0:m - 1],
                            seqs[:, 0, :, 1:m], ACT.Copy)
                    else:
                        ins = nc.scalar.activation(
                            turned[:, 0, :].rearrange("d (s c) -> d s c", c=m)[:, :, 1:m],
                            seqs[:, 3, :, 0:m - 1], ACT.Copy)
                freed(ins, key)

            def turn_rows(r, last_reader):
                for k in range(QUADS):
                    copy_turned("xnT", r, k, last_reader)

            def exp_gap(r):
                act.wait_ge(gap_ready, r + 1)
                nc.scalar.activation(gap_exp[:, :], gap[:, :], ACT.Exp).then_inc(gap_exp_ready, 1)

            def weights_hi():
                act.wait_ge(scales_ready, 1)
                for n in range(2 * EXPERTS):
                    key, w, at = weight_unit(n)
                    wait_unit(act, key)
                    nc.scalar.activation(w[:, 0, at], bank(key), ACT.Copy, scale=S1 if n < EXPERTS else S2)\
                        .then_inc(weight_hi, 1)

            def gelu(tile, e, _, e_before):
                n, half = tile.n, tile.half
                act.wait_ge(z_ready, n + 1)
                for c2 in range(2):
                    if not early(tile):
                        act.wait_ge(h_ready, n * 2 + (c2 - 3))
                    for c in (2 * c2, 2 * c2 + 1):
                        ins = nc.scalar.activation(hid[:, half, c, :], z_ps[half][:, c, :], ACT.Gelu,
                                                   bias=b1T[:, bass.ds(e * FC + c, 1)], scale=INV1)
                    ins.then_inc(gelu_done, 1)

            def tiles(r):
                act.wait_ge(owner_ready, r + 1)
                run_tiles(act, r, gelu)

            def mixer(g):
                last = ("logits", GROUPS - 1) if g == 0 else ("logits", GROUPS + g - 1)
                for k in range(QUADS):
                    copy_turned("aT", g, k, last)
                    if k == QUADS - 1:
                        wait_emptied(act, ("aT", g, k))
                act.sem_inc(turned_ready, 1)
                for k in range(QUADS):
                    act.wait_ge(gate_in, QUADS * g + k + 1)
                    nc.scalar.activation(gate[:, 4 * k:4 * k + 4, :], gate[:, 4 * k:4 * k + 4, :], ACT.Silu)\
                        .then_inc(gate_ready, 1)
                for k in range(QUADS):
                    key = ("cT", g, k)
                    wait_unit(act, key)
                    ins = nc.scalar.activation(ssm_x[:, 4 * k:4 * k + 4, :], bank(key), ACT.Silu)
                    ins.then_inc(ssm_x_ready, 1)
                    act.wait_ge(ssm_x_ready, QUADS * g + k + 1)
                    free_now(act, key)
                for k in range(QUADS):
                    copy_turned("yT", g, k, ("v", g, QUADS - 1))

            copy_small()
            turn_rows(0, None)
            exp_gap(0)
            turn_rows(1, ("logits", 0))
            weights_hi()
            exp_gap(1)
            for g in range(GROUPS):
                tiles(g)
            for g in range(GROUPS):
                mixer(g)
                turn_rows(GROUPS + g, ("o", g, QUADS - 1))
                exp_gap(GROUPS + g)
            for g in range(GROUPS):
                tiles(GROUPS + g)

        @block.tensor
        def _(pe):
            def turn(key, sources, rows=P):
                wait_bank(pe, key)
                for i, src in enumerate(sources):
                    ins = nc.tensor.transpose(bank(key)[:, i * P:i * P + src.shape[0]], src,
                                              ident[0:src.shape[0], 0:src.shape[0]])
                ins.then_inc(aux_full, 1)

            def turn_rows(kind, index, normed_before, g):
                for k in range(QUADS):
                    pe.wait_ge(normed, normed_before + k + 1)
                    turn((kind, index, k), [xn[:, g, 4 * k + i, :] for i in range(4)])

            def logits(r):
                key = ("logits", r)
                wait_bank(pe, key)
                for k in range(QUADS):
                    wait_emptied(pe, ("xnT", r, k))
                    for j in range(4 * k, 4 * k + 4):
                        ins = nc.tensor.matmul(bank(key)[:, j * EXPERTS:(j + 1) * EXPERTS], turned[:, 1 + j, :],
                                               WrT[:, :], start=True, stop=True)
                ins.then_inc(aux_full, 1)

            def ranks(r):
                key = ("ranks", r)
                wait_bank(pe, key)
                pe.wait_ge(ones_counted, r + 1)
                nc.tensor.matmul(bank(key)[:, 0:EXPERTS], before[:, :], rank[:, :, STEPS - 1],
                                 start=True, stop=True)
                nc.tensor.matmul(bank(key)[:, EXPERTS:2 * EXPERTS], ones[:, :], rank[:, :, STEPS - 1],
                                 start=True, stop=True).then_inc(aux_full, 1)

            def route(r):
                turn_rows("xnT", r, normed_before(r), r % GROUPS)
                logits(r)
                ranks(r)

            def wait_all_emptied(last):
                for n in range(aux_index[last] + 1 - BANKS, aux_index[last] + 1):
                    wait_emptied(pe, aux[n])

            w1_flat = W1T[:, :, :, :].rearrange("p k e f -> p (k e f)")
            w2_flat = W2T[:, :, :, :, :].rearrange("p k e c h -> p (k e c h)")

            def hidden(tile, e):
                n, half = tile.n, tile.half
                pe.wait_ge(tile_in[tile.slot], tile.slot_laps * 16 + 16)
                if not early(tile):
                    pe.wait_ge(gelu_done, n * 2 - 2)
                x_hi, x_lo = tile_x[tile.slot][:, 0, :], tile_x[tile.slot][:, 1, :]
                for c in range(FC):
                    z = z_ps[half][:, c, :]
                    w_hi = w1_flat[:, bass.ds(e * HIDDEN + c * P, P)]
                    w_lo = w1_flat[:, bass.ds(e * HIDDEN + (EXPERTS * HIDDEN + c * P), P)]
                    nc.tensor.matmul(z, w_hi, x_hi, start=True, stop=False)
                    nc.tensor.matmul(z, w_hi, x_lo, start=False, stop=False)
                    ins = nc.tensor.matmul(z, w_lo, x_hi, start=False, stop=True)
                ins.then_inc(z_ready, 1)

            def result(tile, e):
                n, half = tile.n, tile.half
                if not early(tile):
                    pe.wait_ge(y_taken, n - 1)
                for c in range(FC):
                    if c % 2 == 0:
                        pe.wait_ge(h_ready, n * 2 + (c // 2 + 1))
                    w_hi = w2_flat[:, bass.ds(e * (FC * D) + c * D, D)]
                    w_lo = w2_flat[:, bass.ds(e * (FC * D) + (EXPERTS * FC * D + c * D), D)]
                    for s in range(2):
                        y = y_ps[half][:, s * D:(s + 1) * D]
                        at = slice(s * P, (s + 1) * P)
                        nc.tensor.matmul(y, hid_hi[:, half, c, at], w_hi, start=(c == 0 and s == 0), stop=False,
                                         skip_group_check=True)
                        nc.tensor.matmul(y, hid_hi[:, half, c, at], w_lo, start=False, stop=False,
                                         skip_group_check=True)
                        ins = nc.tensor.matmul(y, hid_lo[:, half, c, at], w_hi, start=False, stop=(c == FC - 1),
                                               skip_group_check=True)
                ins.then_inc(y_ready, 1)

            def step(tile, e, before, e_before):
                hidden(tile, e)
                if e_before is not None:
                    result(before, e_before)

            def tiles(r):
                pe.wait_ge(owner_ready, r + 1)
                run_tiles(pe, r, step)
                result(*last_tile(pe, r))

            def mixer(g):
                turn_rows("aT", g, normed_before("a", g), g)
                pe.wait_ge(turned_ready, g + 1)
                for k in range(QUADS):
                    key = ("conv", g, k)
                    wait_bank(pe, key)
                    for i in range(4):
                        j = 4 * k + i
                        y = bank(key)[:, i * D:(i + 1) * D]
                        edge = 0 if j == 0 else 1 if j == STEPS - 1 else None
                        if edge is not None:
                            nc.tensor.matmul(y, edge_at[:, edge, :], edge_w[:, edge, :], start=True, stop=False)
                        for tap in range(3):
                            ins = nc.tensor.matmul(y, turned[:, j + tap, :], projT[:, tap, :],
                                                   start=(tap == 0 and edge is None), stop=(tap == 2))
                    ins.then_inc(aux_full, 1)
                for k in range(QUADS):
                    key = ("v", g, k)
                    wait_bank(pe, key)
                    for i in range(4):
                        ins = nc.tensor.matmul(bank(key)[:, i * D:(i + 1) * D], turned[:, 1 + 4 * k + i, :],
                                               projT[:, 3, :], start=True, stop=True)
                    ins.then_inc(aux_full, 1)
                pe.wait_ge(conv_ready, QUADS * (g + 1))
                by_cg = mix[:, :].rearrange("p (g m) -> p g m", g=CGROUPS)
                for k in range(QUADS):
                    turn(("cT", g, k), [by_cg[:, 4 * k + i, :] for i in range(4)])
                if g == 0:
                    pe.wait_ge(ssm_mats, 1)
                for k in range(QUADS):
                    key = ("u", g, k)
                    wait_bank(pe, key)
                    pe.wait_ge(ssm_x_ready, QUADS * g + k + 1)
                    for i in range(4):
                        cg = 4 * k + i
                        ins = nc.tensor.matmul(bank(key)[:, i * P:(i + 1) * P], U[:, cg, :], ssm_x[:, cg, :],
                                               start=True, stop=True)
                    ins.then_inc(aux_full, 1)
                for k in range(QUADS):
                    key = ("y", g, k)
                    wait_bank(pe, key)
                    pe.wait_ge(states_ready, QUADS * g + k + 1)
                    for i in range(4):
                        cg = 4 * k + i
                        y = bank(key)[:, i * P:(i + 1) * P]
                        nc.tensor.matmul(y, ssm_x[:, cg, :], T[:, cg, :], start=True, stop=False)
                        ins = nc.tensor.matmul(y, states[:, cg * P:(cg + 1) * P], V[:, cg, :],
                                               start=False, stop=True)
                    ins.then_inc(aux_full, 1)
                pe.wait_ge(mix_ready, QUADS * (g + 1))
                by_step = mix[:, :].rearrange("p (j c) -> p j c", j=STEPS)
                for k in range(QUADS):
                    turn(("yT", g, k), [by_step[:, 4 * k + i, :] for i in range(4)])
                for k in range(QUADS):
                    key = ("o", g, k)
                    wait_bank(pe, key)
                    wait_emptied(pe, ("yT", g, k))
                    for i in range(4):
                        ins = nc.tensor.matmul(bank(key)[:, i * D:(i + 1) * D], turned[:, 1 + 4 * k + i, :],
                                               projT[:, 4, :], start=True, stop=True)
                    ins.then_inc(aux_full, 1)

            pe.wait_ge(pool_const, 1)
            pe.wait_ge(small_in, 16 * SMALL_LOADS)
            pe.wait_ge(small_ready, 1)
            turn(("small", 0), [tap_w[:, 0], tap_w[:, 1], tap_w[:, 2], small_w[:, 1]])
            turn(("small", 1), [small_w[:, 2], b1_rows[:, :], wr_rows[:, :]])
            wait_emptied(pe, ("small", 1))
            pe.wait_ge(pool_const, 2)
            route(0)
            turn_rows("xnT", 1, normed_before(1), 1)
            pe.wait_ge(ffn_in, 32)
            w1_stage = stage[:, 0].rearrange("p k j d -> p (k j) d")
            w2_stage = stage[:, 1].rearrange("p k j d -> p (k j d)").rearrange("p (e f) -> p e f", e=EXPERTS)
            for e in range(EXPERTS):
                turn(("W1T", e), [w1_stage[:, e * FC + c, :] for c in range(FC)])
            for e in range(EXPERTS):
                turn(("W2T", e), [w2_stage[:, e, c * P:(c + 1) * P] for c in range(FC)])
            logits(1)
            ranks(1)
            pe.wait_ge(weights_ready, 1)
            wait_all_emptied(("ranks", 1))
            for g in range(GROUPS):
                tiles(g)
            pe.wait_ge(gelu_done, 2 * GROUPS * TILES)
            for g in range(GROUPS):
                mixer(g)
                route(GROUPS + g)
            wait_all_emptied(("ranks", RUNS - 1))
            for g in range(GROUPS):
                tiles(GROUPS + g)

        @block.vector
        def _(dve):
            steps = 0

            def settle(ins):
                nonlocal steps
                steps += 1
                ins.then_inc(v_step, 1)
                dve.wait_ge(v_step, steps)
                return ins

            def publish(ins, signal, value):
                ins.then_inc(signal, 1)
                dve.wait_ge(signal, value)

            def statistics(src, eps, at=slice(0, STEPS)):
                for j in range(at.start, at.stop):
                    ins = nc.vector.bn_stats(st[:, j, :], src[:, j, :])
                settle(ins)
                nc.vector.tensor_tensor(mean[:, at], st[:, at, 1], st[:, at, 4], ALU.add)
                nc.vector.tensor_tensor(t1[:, at], st[:, at, 1], st[:, at, 4], ALU.subtract)
                settle(nc.vector.tensor_tensor(var[:, at], st[:, at, 2], st[:, at, 5], ALU.add))
                nc.vector.tensor_scalar(mean[:, at], mean[:, at], 0.5, None, ALU.mult)
                settle(nc.vector.scalar_tensor_tensor(t1[:, at], t1[:, at], 0.25, t1[:, at], ALU.mult, ALU.mult))
                settle(nc.vector.scalar_tensor_tensor(var[:, at], var[:, at], 1.0 / D, t1[:, at], ALU.mult, ALU.add))
                settle(nc.vector.tensor_scalar(var[:, at], var[:, at], eps, None, ALU.add))
                settle(nc.vector.tensor_scalar(t1[:, at].bitcast(I32), var[:, at].bitcast(I32), 1, None,
                                               ALU.arith_shift_right))
                settle(nc.vector.tensor_scalar(rstd[:, at].bitcast(I32), t1[:, at].bitcast(I32), -1.0,
                                               float(0x5F3759DF), ALU.mult, ALU.add))
                for _ in range(3):
                    settle(nc.vector.tensor_tensor(t1[:, at], var[:, at], rstd[:, at], ALU.mult))
                    settle(nc.vector.tensor_tensor(t1[:, at], t1[:, at], rstd[:, at], ALU.mult))
                    settle(nc.vector.tensor_scalar(t1[:, at], t1[:, at], -0.5, 1.5, ALU.mult, ALU.add))
                    settle(nc.vector.tensor_tensor(rstd[:, at], rstd[:, at], t1[:, at], ALU.mult))
                settle(nc.vector.scalar_tensor_tensor(shift[:, at], mean[:, at], -1.0, rstd[:, at],
                                                      ALU.mult, ALU.mult))

            def apply_norm(dst, src, j):
                return nc.vector.tensor_scalar(dst[:, j, :], src[:, j, :], rstd[:, j:j + 1], shift[:, j:j + 1],
                                               ALU.mult, ALU.add)

            def block_norm(g):
                statistics(resid[:, g], LN_EPS_BLOCK)
                for j in range(STEPS):
                    ins = apply_norm(xn[:, g], resid[:, g], j)
                    if j % 4 == 3:
                        ins.then_inc(normed, 1)

            def route_rows(r):
                g = r % GROUPS
                if r < GROUPS:
                    dve.wait_ge(x_in[g], 16)
                block_norm(g)
                dve.wait_ge(normed, normed_before(r) + QUADS)
                if r >= GROUPS:
                    dve.wait_ge(scattered[g], 16 * 2 * STEPS)
                settle(nc.vector.tensor_copy(halves[:, g, :, 0:D], xn[:, g]))
                nc.vector.tensor_tensor(halves[:, g, :, D:2 * D], xn[:, g], halves[:, g, :, 0:D],
                                        ALU.subtract).then_inc(halves_ready, 1)

            def route(r):
                g = r % GROUPS
                key = ("logits", r)
                wait_unit(dve, key)
                by_expert = bank(key)[:, 0:EXPERTS * STEPS].rearrange("p (j e) -> p e j", e=EXPERTS)
                ins = nc.vector.tensor_tensor(lg[:, :, :], by_expert,
                                              br_bc[:, :].unsqueeze(2).to_broadcast([P, EXPERTS, STEPS]), ALU.add)
                settle(ins)
                free_now(dve, key)
                for k in range(2):
                    e_last = lg[:, :, :].rearrange("p e j -> p j e")
                    settle(nc.vector.tensor_reduce(best[k][:, :], e_last, X_AXIS, ALU.max))
                    every = [P, EXPERTS, STEPS]
                    settle(nc.vector.tensor_tensor(r1[:, :, :], lg[:, :, :],
                                                   best[k][:, :].unsqueeze(1).to_broadcast(every), ALU.is_equal))
                    settle(nc.vector.tensor_tensor(r1[:, :, :], r1[:, :, :], low_first[:, :, :], ALU.mult))
                    settle(nc.vector.tensor_reduce(t1[:, :], r1[:, :, :].rearrange("p e j -> p j e"),
                                                   X_AXIS, ALU.max))
                    settle(nc.vector.tensor_tensor(pick[k][:, :, :], low_first[:, :, :],
                                                   t1[:, :].unsqueeze(1).to_broadcast(every), ALU.is_equal))
                    if k == 0:
                        settle(nc.vector.scalar_tensor_tensor(lg[:, :, :], pick[0][:, :, :], -3e38, lg[:, :, :],
                                                              ALU.mult, ALU.add))
                nc.vector.tensor_tensor(gap[:, :], best[1][:, :], best[0][:, :], ALU.subtract).then_inc(gap_ready, 1)
                settle(nc.vector.tensor_tensor(r1[:, :, :], pick[0][:, :, :], pick[1][:, :, :], ALU.add))
                flat = "p e j -> p (e j)"
                nc.vector.tensor_tensor_scan(rank[:, :, :].rearrange(flat), not_step0[:, :, :].rearrange(flat),
                                             r1[:, :, :].rearrange(flat), 0.0, ALU.mult, ALU.add)\
                    .then_inc(ones_counted, 1)
                key = ("ranks", r)
                wait_unit(dve, key)
                settle(nc.vector.tensor_copy(counts[:, :, :], bank(key)[:, 0:2 * EXPERTS]))
                free_now(dve, key)
                settle(nc.vector.tensor_scalar(whole_i[:, :], counts[:, 1, :], float(TILE - 1), None, ALU.add))
                shift_bits = TILE.bit_length() - 1
                settle(nc.vector.tensor_scalar(whole_i[:, :], whole_i[:, :], shift_bits, None,
                                               ALU.arith_shift_right))
                settle(nc.vector.tensor_scalar(whole[:, :], whole_i[:, :], float(TILE), None, ALU.mult))
                settle(nc.vector.tensor_tensor_scan(ends[:, :], ones[:, 0:EXPERTS], whole[:, :], 0.0,
                                                    ALU.mult, ALU.add))
                settle(nc.vector.tensor_tensor(start_f[:, :], ends[:, :], whole[:, :], ALU.subtract))
                settle(nc.vector.tensor_tensor(start_f[:, :], start_f[:, :], counts[:, 0, :], ALU.add))
                settle(nc.vector.tensor_tensor(rank[:, :, :], rank[:, :, :], r1[:, :, :], ALU.subtract))
                settle(nc.vector.tensor_tensor(rank[:, :, :], rank[:, :, :],
                                               start_f[:, :].unsqueeze(2).to_broadcast([P, EXPERTS, STEPS]), ALU.add))
                if r >= GROUPS:
                    wait_gathered(dve, g, 1)
                for k in range(2):
                    settle(nc.vector.tensor_tensor(r1[:, :, :], rank[:, :, :], pick[k][:, :, :], ALU.mult))
                    settle(nc.vector.tensor_reduce(slot_f[:, k, :], r1[:, :, :].rearrange("p e j -> p j e"),
                                                   X_AXIS, ALU.add))
                nc.vector.tensor_copy(slots[:, g], slot_f[:, :, :]).then_inc(slots_ready, 1)
                if r >= GROUPS:
                    dve.wait_ge(y_taken, TILES * (g + 1))
                shape = [1, TILES, EXPERTS]
                settle(nc.vector.tensor_tensor(past, ends[0:1, :].unsqueeze(1).to_broadcast(shape),
                                               tile_start[:, :].unsqueeze(2).to_broadcast(shape), ALU.is_le))
                of_tile = owner_f[:, OWNER_PAD:]
                settle(nc.vector.tensor_reduce(of_tile, past, X_AXIS, ALU.add))
                settle(nc.vector.tensor_scalar(of_tile, of_tile, float(EXPERTS - 1), None, ALU.min))
                every = RING * ROUNDS + 1
                settle(nc.vector.scalar_tensor_tensor(owners_f[:, :], owner_f[:, RING:RING + every:RING],
                                                      float(EXPERTS), owner_f[:, RING - 1:RING - 1 + every:RING],
                                                      ALU.mult, ALU.add))
                for k in range(RING - 2, -1, -1):
                    settle(nc.vector.scalar_tensor_tensor(owners_f[:, :], owners_f[:, :], float(EXPERTS),
                                                          owner_f[:, k:k + every:RING], ALU.mult, ALU.add))
                nc.vector.tensor_copy(owners[:, g], owners_f[:, :]).then_inc(owner_ready, 1)
                dve.wait_ge(gap_exp_ready, r + 1)
                settle(nc.vector.tensor_scalar(t1[:, :], gap_exp[:, :], 1.0, None, ALU.add))
                settle(nc.vector.reciprocal(share[:, g, 0, :], t1[:, :]))
                settle(nc.vector.tensor_tensor(share[:, g, 1, :], gap_exp[:, :], share[:, g, 0, :], ALU.mult))

            def find_largest():
                dve.wait_ge(ffn_in, 32)
                nc.vector.tensor_reduce(big[:, 0:1], stage[:, 0].rearrange("p k j d -> p (k j d)"), X_AXIS,
                                        ALU.max, apply_absolute_value=True)
                nc.vector.tensor_reduce(big[:, 1:2], stage[:, 1].rearrange("p k j d -> p (k j d)"), X_AXIS,
                                        ALU.max, apply_absolute_value=True)
                wait_emptied(dve, ("small", 1))
                nc.vector.tensor_reduce(big[:, 2:3], b1T[:, :], X_AXIS, ALU.max, apply_absolute_value=True)\
                    .then_inc(max_ready, 1)

            def find_scales():
                dve.wait_ge(max_all, 1)
                settle(nc.vector.scalar_tensor_tensor(big_all[:, 2:3], big_all[:, 0:1], float(D), big_all[:, 2:3],
                                                      ALU.mult, ALU.add))
                settle(nc.vector.tensor_scalar(big_all[:, 0:3], big_all[:, 0:3], 1e-25, None, ALU.max))
                settle(nc.vector.tensor_scalar(scale_t[:, 0:3].bitcast(I32), big_all[:, 0:3].bitcast(I32),
                                               EXPONENT_BITS, None, ALU.bitwise_and))
                settle(nc.vector.reciprocal(big[:, 0:3], scale_t[:, 0:3]))
                for k, (s, inv, top) in enumerate(((S1, INV1, 13), (S2, INV2, 13), (SH, INVH, 14))):
                    nc.vector.tensor_scalar(s, big[:, k:k + 1], 2.0 ** top, None, ALU.mult)
                    settle(nc.vector.tensor_scalar(inv, scale_t[:, k:k + 1], 2.0 ** -top, None, ALU.mult))
                publish(nc.vector.tensor_tensor(INVY, INV2, INVH, ALU.mult), scales_ready, 1)

            def weights_lo():
                for n in range(2 * EXPERTS):
                    key, w, at = weight_unit(n)
                    dve.wait_ge(weight_hi, n + 1)
                    freed(nc.vector.scalar_tensor_tensor(w[:, 1, at], bank(key), S1 if n < EXPERTS else S2,
                                                         w[:, 0, at], ALU.mult, ALU.subtract), key)
                wait_emptied(dve, key)
                dve.sem_inc(weights_ready, 1)

            def ssm_constants():
                dve.wait_ge(decay_in, 1)
                dve.wait_ge(pool_const, 2)
                for k in (1, 2, 4, 8):
                    settle(nc.vector.tensor_tensor(decay[:, k + 1:2 * k + 1, :], decay[:, 1:k + 1, :],
                                                   decay[:, k:k + 1, :].to_broadcast([P, k, STATES]), ALU.mult))
                nc.vector.tensor_reduce(same_c[:, :], ident[:, :].rearrange("p (j c) -> p c j", c=CPG),
                                        X_AXIS, ALU.add)
                settle(nc.vector.tensor_tensor(cb[:, :], ssm_in[:, 1], ssm_in[:, 2], ALU.mult))
                settle(nc.vector.tensor_tensor(tap_terms[:, :, :], decay[:, 0:CHUNK, :],
                                               cb[:, :].unsqueeze(1).to_broadcast([P, CHUNK, STATES]), ALU.mult))
                settle(nc.vector.tensor_reduce(taps[:, CHUNK - 1:], tap_terms[:, :, :], X_AXIS, ALU.add))
                nc.vector.tensor_tensor(taps[:, CHUNK - 1:CHUNK], taps[:, CHUNK - 1:CHUNK], d_in[:, :], ALU.add)
                nc.vector.tensor_copy(readout[:, :, CHUNK], decay[:, CHUNK, :])
                nc.vector.tensor_tensor(readout[:, :, 0:CHUNK],
                                        decay[:, 1:CHUNK + 1, :].rearrange("p k s -> p s k"),
                                        cb[:, :].unsqueeze(2).to_broadcast([P, STATES, CHUNK]), ALU.mult)\
                    .then_inc(ssm_const, 1)


            b2_flat = b2_bc[:, :, :].rearrange("p e h -> p (e h)")

            def split_hidden(tile):
                n, half = tile.n, tile.half
                if not early(tile):
                    dve.wait_ge(y_ready, n - 1)
                for c2 in range(2):
                    at = slice(2 * c2, 2 * c2 + 2)
                    dve.wait_ge(gelu_done, n * 2 + (c2 + 1))
                    nc.vector.tensor_scalar(hid_hi[:, half, at, :], hid[:, half, at, :], SH, None, ALU.mult)\
                        .then_inc(hi_ready, 1)
                    dve.wait_ge(hi_ready, n * 2 + (c2 + 1))
                    nc.vector.scalar_tensor_tensor(hid_lo[:, half, at, :], hid[:, half, at, :], SH,
                                                   hid_hi[:, half, at, :], ALU.mult, ALU.subtract)\
                        .then_inc(h_ready, 1)

            def take_result(tile, e):
                n, half = tile.n, tile.half
                dve.wait_ge(y_ready, n + 1)
                if not early(tile):
                    dve.wait_ge(tile_out[half], tile.half_laps * 16)
                bias = b2_flat[:, bass.ds(e * D, D)].unsqueeze(1).to_broadcast([P, 2, D])
                nc.vector.scalar_tensor_tensor(tile_y[:, half], y_ps[half][:, 0:2 * D].rearrange(
                    "p (s d) -> p s d", s=2), INVY, bias, ALU.mult, ALU.add).then_inc(y_taken, 1)

            def step(tile, e, before, e_before):
                split_hidden(tile)
                if e_before is not None:
                    take_result(before, e_before)

            def tiles(r):
                run_tiles(dve, r, step)
                take_result(*last_tile(dve, r))

            def collect(r, at=slice(0, STEPS)):
                g = r % GROUPS
                wait_gathered(dve, g, r // GROUPS + 1, range(at.start * 2 // STEPS, at.stop * 2 // STEPS))
                for k in range(2):
                    for j in range(at.start, at.stop):
                        ins = nc.vector.scalar_tensor_tensor(xn[:, g, j, :], stage[:, g, k, j, :],
                                                             share[:, g, k, j:j + 1], xn[:, g, j, :],
                                                             ALU.mult, ALU.add)
                    settle(ins)
                if r < GROUPS:
                    dve.sem_inc(combined, 1)

            def combine(r, at=slice(0, STEPS)):
                g = r % GROUPS
                statistics(xn[:, g], LN_EPS_FFN, at)
                for j in range(at.start, at.stop):
                    ins = apply_norm(xn[:, g], xn[:, g], j)
                settle(ins)
                z = xn[:, g, at]
                settle(nc.vector.tensor_tensor(
                    z, z, half_w_bc[:, :].unsqueeze(1).to_broadcast([P, at.stop - at.start, D]), ALU.mult))
                dve.wait_ge(half_b_added, r + 1)
                settle(nc.vector.tensor_tensor(resid[:, g, at], resid[:, g, at], z, ALU.add))

            def mixer(g):
                block_norm(g)
                for k in range(QUADS):
                    key = ("conv", g, k)
                    wait_unit(dve, key)
                    shape = [P, 4, CGROUPS, CPG]
                    by_cg = mix[:, :].rearrange("p (g j c) -> p j g c", g=CGROUPS, c=CPG)
                    freed(nc.vector.tensor_tensor(
                        by_cg[:, 4 * k:4 * k + 4], bank(key).rearrange("p (j g c) -> p j g c", j=4, c=CPG),
                        convb_bc[:, :].rearrange("p (g c) -> p g c", c=CPG).unsqueeze(1).to_broadcast(shape),
                        ALU.add), key)
                    wait_emptied(dve, key)
                    dve.sem_inc(conv_ready, 1)
                for k in range(QUADS):
                    key = ("v", g, k)
                    wait_unit(dve, key)
                    freed(nc.vector.tensor_tensor(
                        gate[:, 4 * k:4 * k + 4, :], bank(key).rearrange("p (j c) -> p j c", j=4),
                        v1b_bc[:, :].unsqueeze(1).to_broadcast([P, 4, D]), ALU.add), key)
                    wait_emptied(dve, key)
                    dve.sem_inc(gate_in, 1)
                for k in range(QUADS):
                    key = ("u", g, k)
                    wait_unit(dve, key)
                    at = states[:, 1 + 4 * k * P:1 + 4 * (k + 1) * P]
                    settle(nc.vector.tensor_tensor_scan(
                        at, chunk_decay[:, 4 * k:4 * k + 4, :].rearrange("p g n -> p (g n)"), bank(key), 0.0,
                        ALU.mult, ALU.add))
                    free_now(dve, key)
                    nc.vector.memset(at[:, CHUNKS_PER_SEQ - 1:4 * P:CHUNKS_PER_SEQ], 0.0).then_inc(states_ready, 1)
                dve.wait_ge(gate_ready, QUADS * (g + 1))
                for k in range(QUADS):
                    key = ("y", g, k)
                    wait_unit(dve, key)
                    view = "p (g t c) -> p g t c"
                    freed(nc.vector.tensor_tensor(
                        mix[:, :].rearrange("p (t g c) -> p g t c", g=CGROUPS, c=CPG)[:, 4 * k:4 * k + 4],
                        bank(key).rearrange(view, g=4, c=CPG),
                        gate[:, :, :].rearrange("p t (g c) -> p g t c", c=CPG)[:, 4 * k:4 * k + 4], ALU.mult), key)
                    wait_emptied(dve, key)
                    dve.sem_inc(mix_ready, 1)
                dve.wait_ge(w2b_added, g + 1)
                for k in range(QUADS):
                    key = ("o", g, k)
                    wait_unit(dve, key)
                    x_at = resid[:, g, 4 * k:4 * k + 4, :]
                    ins = nc.vector.tensor_tensor(x_at, x_at, bank(key).rearrange("p (j c) -> p j c", j=4),
                                                  ALU.add)
                    freed(ins, key)
                    wait_emptied(dve, key)

            route_rows(0)
            dve.wait_ge(small_in, 16 * SMALL_LOADS)
            for k in range(3):
                ins = nc.vector.tensor_scalar(tap_w[:, k, :], small_w[:, 0, :], conv_c[:, k:k + 1], None, ALU.mult)
            ins.then_inc(small_ready, 1)
            nc.vector.tensor_scalar(half_w_bc[:, :], half_w_bc[:, :], 0.5, None, ALU.mult)
            nc.vector.tensor_scalar(half_b_bc[:, :], half_b_bc[:, :], 0.5, None, ALU.mult).then_inc(half_b_ready, 1)
            for edge, tap in ((0, 0), (1, 2)):
                nc.vector.scalar_tensor_tensor(edge_w[:, edge, :], w1b_bc[0:1, :], -1.0, conv_bc[0:1, :, tap],
                                               ALU.mult, ALU.mult)
            settle(nc.vector.tensor_reduce(convb_bc[:, :], conv_bc[:, :, :], X_AXIS, ALU.add))
            settle(nc.vector.tensor_tensor(convb_bc[:, :], convb_bc[:, :], w1b_bc[:, :], ALU.mult))
            dve.wait_ge(pool_const, 2)
            find_largest()
            route(0)
            route_rows(1)
            find_scales()
            weights_lo()
            route(1)
            ssm_constants()
            for g in range(GROUPS):
                tiles(g)
            collect(0)
            combine(0)
            mixer(0)
            route_rows(GROUPS)
            collect(1)
            route(GROUPS)
            combine(1)
            mixer(1)
            route_rows(GROUPS + 1)
            route(GROUPS + 1)
            for g in range(GROUPS):
                tiles(GROUPS + g)
            for g in range(GROUPS):
                for at in final_parts(GROUPS + g):
                    collect(GROUPS + g, at)
                    combine(GROUPS + g, at)
                    dve.sem_inc(x_final, 1)


_INS = ["x", "w1_w", "w1_b", "v1_w", "v1_b", "w2_w", "w2_b", "conv_w", "A", "B_ssm", "C_ssm", "D_ssm",
        "Wr", "br", "W1", "b1", "W2", "b2", "ln_w", "ln_b"]


def kernel(**inputs):
    import numpy as np
    import concourse.bacc as bacc
    from concourse.bass_utils import run_bass_kernel_spmd

    nc = bacc.Bacc("TRN2", target_bir_lowering=False, num_devices=1)
    arrays, args = {}, []
    for n, name in enumerate(_INS):
        a = np.ascontiguousarray(inputs[("L0_attn_" if n < 12 else "L0_ffn_") + name])
        arrays["in_" + name] = a
        args.append(nc.dram_tensor("in_" + name, a.shape, F32, kind="ExternalInput").ap())
    args.append(nc.dram_tensor("out_x", (BATCH, SEQ, D), F32, kind="ExternalOutput").ap())
    build(nc, *args)
    return run_bass_kernel_spmd(nc, [arrays], core_ids=[0]).results[0]["out_x"]
```

```python
from collections import namedtuple
from contextlib import ExitStack

import concourse.bass as bass
from concourse import mybir

F32 = mybir.dt.float32
F16 = mybir.dt.float16
I32 = mybir.dt.int32
ALU = mybir.AluOpType
ACT = mybir.ActivationFunctionType
X_AXIS = mybir.AxisListType.X

P = 128
D = 128
BATCH, SEQ = 8, 512
GROUPS = 2
CHUNK = 16
STEPS = CHUNK
TOKENS = BATCH * SEQ // GROUPS
SEQS = BATCH // GROUPS
CHUNKS_PER_SEQ = SEQ // CHUNK
EXPERTS = 8
HIDDEN = 512
FC = HIDDEN // P
TILE = 2 * P
RING = 4
PEELED = RING - 1
ROUNDS = -(-(2 * TOKENS // TILE + EXPERTS - 1 - PEELED) // RING)
TILES = PEELED + ROUNDS * RING
LAG = 2
DIGIT = 3
OWNER_PAD = RING + LAG - PEELED
assert EXPERTS == 2 ** DIGIT and DIGIT * (RING + LAG) <= 24
SLOTS = TILES * TILE
STATES = 16
CPG = P // CHUNK
CGROUPS = D // CPG
QUADS = STEPS // 4
LN_EPS_BLOCK = 1e-5
LN_EPS_FFN = 1e-12
RUNS = 2 * GROUPS
EXPONENT_BITS = 0x7F800000

Tile = namedtuple("Tile", "n half half_laps slot slot_laps")


def tile_at(start, rounds):
    return Tile(n=rounds * RING + start, half=start % 2, half_laps=rounds * (RING // 2) + start // 2,
                slot=start % RING, slot_laps=rounds + start // RING)


def early(tile):
    return isinstance(tile.n, int) and tile.n < 2


HALVES = [slice(0, STEPS // 2), slice(STEPS // 2, STEPS)]


def build(nc, x, w1_w, w1_b, v1_w, v1_b, w2_w, w2_b, conv_w, A, B_ssm, C_ssm, D_ssm,
          Wr, br, W1, b1, W2, b2, ln_w, ln_b, out):
    ctx = ExitStack()
    with ctx:
        def sb(name, shape, dt=F32):
            return ctx.enter_context(nc.sbuf_tensor(name, shape, dt))

        def sem(name):
            return ctx.enter_context(nc.semaphore(name))

        slot_x = [nc.dram_tensor(f"slot_x{g}", (SLOTS, 2 * D), F16).ap() for g in range(GROUPS)]
        slot_y = [nc.dram_tensor(f"slot_y{g}", (SLOTS, D), F32).ap() for g in range(GROUPS)]
        taps_dram = nc.dram_tensor("taps_dram", (D, 2 * CHUNK - 1), F32).ap()
        decay_dram = nc.dram_tensor("decay_dram", (D, CHUNK + 1, STATES), F32).ap()
        readout_dram = nc.dram_tensor("readout_dram", (D, STATES, CHUNK + 1), F32).ap()

        z_ps = [ctx.enter_context(nc.psum_tensor(f"z_ps{i}", [P, FC, TILE], F32)) for i in range(2)]
        y_ps = [ctx.enter_context(nc.psum_tensor(f"y_ps{i}", [P, 512], F32)) for i in range(2)]
        banks = [ctx.enter_context(nc.psum_tensor(f"aux_ps{i}", [P, 512], F32))[:, :] for i in range(2)]
        banks += [z_ps[k // 2][:, 2 * (k % 2):2 * (k % 2) + 2, :].rearrange("p c n -> p (c n)") for k in range(4)]
        BANKS = len(banks)

        resid = sb("resid", [P, GROUPS, STEPS, D])
        xn = sb("xn", [P, GROUPS, STEPS, D])
        halves = sb("halves", [P, GROUPS, STEPS, 2 * D], F16)
        stage = sb("stage", [P, GROUPS, 2, STEPS, D])
        W1T = sb("W1T", [P, 2, EXPERTS, HIDDEN], F16)
        W2T = sb("W2T", [P, 2, EXPERTS, FC, D], F16)
        b1T = sb("b1T", [P, EXPERTS * FC])
        b1_rows = sb("b1_rows", [EXPERTS * FC, P])
        b2_bc = sb("b2_bc", [P, EXPERTS, D])
        br_bc = sb("br_bc", [P, EXPERTS])
        half_w_bc = sb("half_w_bc", [P, D])
        half_b_bc = sb("half_b_bc", [P, D])
        ident = sb("ident", [P, P])
        before = sb("before", [P, P])
        ones = sb("ones", [P, P])
        low_first = sb("low_first", [P, EXPERTS, STEPS])
        not_step0 = sb("not_step0", [P, EXPERTS, STEPS])
        tile_start = sb("tile_start", [1, TILES])
        WrT = sb("WrT", [P, EXPERTS])
        wr_rows = sb("wr_rows", [EXPERTS, D])
        projT = sb("projT", [P, 5, D])
        conv_c = sb("conv_c", [P, 3])
        w1b_bc = sb("w1b_bc", [P, D])
        convb_bc = sb("convb_bc", [P, D])
        edge_w = sb("edge_w", [1, 2, D])
        edge_at = sb("edge_at", [1, 2, P])
        v1b_bc = sb("v1b_bc", [P, D])
        w2b_bc = sb("w2b_bc", [P, D])
        ssm_in = sb("ssm_in", [P, 3, STATES])
        d_in = sb("d_in", [P, 1])
        decay = sb("decay", [P, CHUNK + 1, STATES])
        cb = sb("cb", [P, STATES])
        taps = sb("taps", [P, 2 * CHUNK - 1])
        readout = sb("readout", [P, STATES, CHUNK + 1])
        mT = sb("mT", [P, CGROUPS, CHUNK])
        mU = sb("mU", [P, CGROUPS, STATES])
        mV = sb("mV", [P, CGROUPS, CHUNK + 1])
        same_c = sb("same_c", [P, CPG])
        T = sb("T", [P, CGROUPS, CHUNK * CPG])
        U = sb("U", [P, CGROUPS, STATES * CPG])
        V = sb("V", [P, CGROUPS, CHUNK * CPG])
        keep_chunk = sb("keep_chunk", [P, P])
        chunk_decay = sb("chunk_decay", [P, CGROUPS, P])
        turned = sb("turned", [P, STEPS + 2, P])
        states = sb("states", [P, 1 + CGROUPS * P])
        tile_x = [sb(f"tile_x{k}", [P, 2, TILE], F16)[:, :, :] for k in range(2)]
        tile_x += [a[:, :, :].rearrange("p a b -> p (a b)")[:, 0:TILE].bitcast(F16).rearrange(
            "p (k n) -> p k n", k=2) for a in (decay, readout)]
        hid = sb("hid", [P, 2, FC, TILE])
        split_buf = sb("split_buf", [P, 2, 2, FC, TILE], F16)
        spare = turned[:, 1:STEPS + 1, :].rearrange("p j n -> p (j n)").bitcast(F16).rearrange(
            "p (s k c n) -> p s k c n", s=2, k=2, c=FC)
        hid_hi = [buf[:, s, 0] for buf in (split_buf, spare) for s in range(2)]
        hid_lo = [buf[:, s, 1] for buf in (split_buf, spare) for s in range(2)]
        tile_y = sb("tile_y", [P, 2, 2, D])
        mix = stage[:, 0, 0].rearrange("p j d -> p (j d)")
        ssm_x = stage[:, 0, 1]
        gate = halves[:, 1].rearrange("p j d -> p (j d)").bitcast(F32).rearrange("p (j d) -> p j d", j=STEPS)
        routed = hid[:, :, :, :].rearrange("p a b c -> p (a b c)").rearrange("p (j n) -> p j n", n=P)
        setup = iter(range(1, 1 + 4 * 3 * D, 3 * D))

        def setup_rows(shape):
            at = next(setup)
            flat = states[:, at:at + shape[0] * shape[1]]
            return flat.rearrange("p (a b) -> p a b", a=shape[0])

        small_w = setup_rows([3, D])
        tap_w = setup_rows([3, D])
        conv_bc = setup_rows([D, 3])
        tap_terms = setup_rows([CHUNK, STATES])
        st = sb("st", [P, STEPS, 6])
        mean = sb("mean", [P, STEPS])
        var = sb("var", [P, STEPS])
        rstd = [sb(f"rstd{k}", [P, STEPS]) for k in range(2)]
        shift = [sb(f"shift{k}", [P, STEPS]) for k in range(2)]
        t1 = sb("t1", [P, STEPS])
        lg = sb("lg", [P, EXPERTS, STEPS])
        r1 = sb("r1", [P, EXPERTS, STEPS])
        pick = [sb(f"pick{k}", [P, EXPERTS, STEPS]) for k in range(2)]
        rank = sb("rank", [P, EXPERTS, STEPS])
        best = [sb(f"best{k}", [P, STEPS]) for k in range(2)]
        gap = sb("gap", [P, STEPS])
        gap_exp = sb("gap_exp", [P, STEPS])
        share = sb("share", [P, GROUPS, 2, STEPS])
        counts = sb("counts", [P, 2, EXPERTS])
        whole_i = sb("whole_i", [P, EXPERTS], I32)
        whole = sb("whole", [P, EXPERTS])
        ends = sb("ends", [P, EXPERTS])
        start_f = sb("start_f", [P, EXPERTS])
        slot_f = sb("slot_f", [P, 2, STEPS])
        slots = sb("slots", [P, GROUPS, 2, STEPS], I32)
        past = split_buf[0:1, 0].rearrange("p k c n -> p (k c n)").bitcast(F32)[:, 0:TILES * EXPERTS].rearrange(
            "p (i e) -> p i e", e=EXPERTS)
        owner_f = sb("owner_f", [1, OWNER_PAD + TILES])
        owners_f = sb("owners_f", [1, ROUNDS + 1])
        owners = sb("owners", [1, GROUPS, ROUNDS + 1], I32)
        zero_rows = tile_y[:, 0]
        big = sb("big", [P, 4])
        big_all = sb("big_all", [P, 4])
        scale_t = sb("scale_t", [P, 4])
        scales = sb("scales", [P, 8])
        S1, INV1, S2, INV2, SH, INVH, INVY = (scales[:, k:k + 1] for k in range(7))

        x_in = [sem(f"x_in{g}") for g in range(GROUPS)]
        small_in = sem("small_in")
        rest_in = sem("rest_in")
        ffn_in = sem("ffn_in")
        pool_const = sem("pool_const")
        pool_step = sem("pool_step")
        zeros_ready = sem("zeros_ready")
        zeroed = [sem(f"zeroed{g}") for g in range(GROUPS)]
        v_step = sem("v_step")
        small_ready = sem("small_ready")
        normed = [sem("normed_v"), sem("normed_s")]
        halves_ready = sem("halves_ready")
        slots_ready = sem("slots_ready")
        owner_ready = sem("owner_ready")
        gap_ready = sem("gap_ready")
        gap_exp_ready = sem("gap_exp_ready")
        ones_counted = sem("ones_counted")
        max_ready = sem("max_ready")
        max_all = sem("max_all")
        scales_ready = sem("scales_ready")
        weight_hi = sem("weight_hi")
        weights_ready = sem("weights_ready")
        half_b_added = sem("half_b_added")
        half_b_ready = sem("half_b_ready")
        w2b_added = sem("w2b_added")
        decay_in = sem("decay_in")
        ssm_const = sem("ssm_const")
        ssm_dram = sem("ssm_dram")
        ssm_back = sem("ssm_back")
        ssm_mats = sem("ssm_mats")
        aux_full = sem("aux_full")
        aux_free = [sem(f"aux_free{b}") for b in range(BANKS)]
        scattered = [sem(f"scattered{g}") for g in range(GROUPS)]
        gathered = [[sem(f"gathered{g}_{k}") for k in range(QUADS)] for g in range(GROUPS)]
        stage_used = sem("stage_used")
        collected = sem("collected")
        half_combined = sem("half_combined")
        shares_ready = sem("shares_ready")
        stats_ready = sem("stats_ready")
        tile_in = [sem(f"tile_in{k}") for k in range(RING)]
        tile_out = [sem(f"tile_out{h}") for h in range(2)]
        z_ready = sem("z_ready")
        gelu_done = sem("gelu_done")
        hi_ready = sem("hi_ready")
        h_ready = sem("h_ready")
        y_ready = sem("y_ready")
        y_taken = sem("y_taken")
        turned_ready = sem("turned_ready")
        conv_ready = sem("conv_ready")
        gate_in = sem("gate_in")
        gate_ready = sem("gate_ready")
        ssm_x_ready = sem("ssm_x_ready")
        states_ready = sem("states_ready")
        mix_ready = sem("mix_ready")
        x_out = sem("x_out")
        x_final = sem("x_final")

        def turned_units(r):
            return [("xnT", r, k) for k in range(QUADS)]

        aux = [("small", 0), ("small", 1)] + turned_units(0) + [("logits", 0), ("ranks", 0)]
        aux += turned_units(1) + [("logits", 1), ("ranks", 1)]
        aux += [("W1T", k) for k in range(EXPERTS)] + [("W2T", k) for k in range(EXPERTS)]
        def mixer_units(g, *kinds):
            return [(kind, g, k) for kind in kinds for k in range(QUADS)]

        aux += mixer_units(0, "aT", "conv", "v", "cT", "u", "y", "yT", "o")
        aux += mixer_units(1, "aT", "conv") + turned_units(2) + [("logits", 2)]
        aux += mixer_units(1, "v", "cT") + [("ranks", 2)] + mixer_units(1, "u", "y", "yT", "o")
        aux += turned_units(3) + [("logits", 3), ("ranks", 3)]
        aux_index = {key: n for n, key in enumerate(aux)}

        def bank(key):
            return banks[aux_index[key] % BANKS]

        def wait_bank(pe, key):
            n = aux_index[key]
            if n >= BANKS:
                pe.wait_ge(aux_free[n % BANKS], n // BANKS)

        def wait_unit(eng, key):
            eng.wait_ge(aux_full, aux_index[key] + 1)

        def wait_emptied(eng, key):
            n = aux_index[key]
            eng.wait_ge(aux_free[n % BANKS], n // BANKS + 1)

        def freed(ins, key):
            ins.then_inc(aux_free[aux_index[key] % BANKS], 1)

        def free_now(eng, key):
            eng.sem_inc(aux_free[aux_index[key] % BANKS], 1)

        def token_rows(ap, g):
            return ap[g * TOKENS:(g + 1) * TOKENS, :].rearrange("(p j) d -> p j d", p=P)

        def final_parts(r):
            return HALVES if r == RUNS - 1 else [slice(0, STEPS)]

        norms = [("x", 0), ("x", 1), ("c", 0, 0), ("a", 0), ("c", 1, 0), ("a", 1), ("x", 2), ("x", 3)]
        norms += [("c", r, part) for r in range(GROUPS, RUNS) for part in range(len(final_parts(r)))]
        shared_norms = [key for key in norms if key not in (("x", 1), ("c", 1, 0))]

        def norm_steps(key):
            return final_parts(key[1])[key[2]] if key[0] == "c" else slice(0, STEPS)

        def norm_quads(key):
            at = norm_steps(key)
            quads = range(at.start // 4, at.stop // 4)
            cut = len(quads) // 2 if key in shared_norms else 0
            return quads[:cut], quads[cut:]

        def wait_normed(eng, key, quad=None):
            for by, signal in enumerate(normed):
                own = norm_quads(key)[by]
                earlier = sum(len(norm_quads(k)[by]) for k in norms[:norms.index(key)])
                if own and (quad is None or quad in own):
                    eng.wait_ge(signal, earlier + (len(own) if quad is None else quad - own.start + 1))

        def wait_gathered(eng, g, times, quads=range(QUADS)):
            for quad in quads:
                eng.wait_ge(gathered[g][quad], 16 * 2 * 4 * times)

        x_rows = x.rearrange("b t d -> (b t) d")
        out_rows = out.rearrange("b t d -> (b t) d")

        def row(ap):
            return ap.rearrange("(a n) -> a n", a=1)

        def uses(half, n):
            return (n + 1 - half) // 2

        def experts(word):
            return [(word >> (DIGIT * k)) & (EXPERTS - 1) for k in range(RING + LAG)]

        def run_tiles(eng, r, step):
            first = r * TILES
            words = owners[0:1, r % GROUPS, :]
            e = experts(eng.value_load(words[:, 0:1]))[-PEELED:]
            for k in range(PEELED):
                step(tile_at(first + k, 0), e[k], tile_at(first + k - LAG, 0), e[k - LAG] if k >= LAG else None)
            with eng.Fori(1, ROUNDS + 1) as rounds:
                e = experts(eng.value_load(words[:, bass.ds(rounds, 1)]))
                for k in range(RING):
                    start = first + PEELED - RING + k
                    step(tile_at(start, rounds), e[k + LAG], tile_at(start - LAG, rounds), e[k])

        def last_tiles(eng, r):
            word = eng.value_load(owners[0:1, r % GROUPS, ROUNDS:ROUNDS + 1])
            return [(tile_at((r + 1) * TILES - k, 0), experts(word)[-k]) for k in range(LAG, 0, -1)]

        SMALL_LOADS, REST_LOADS = 7, 11
        block = ctx.enter_context(nc.Block())

        def weight_unit(n):
            if n < EXPERTS:
                key, w = ("W1T", n), W1T[:, :, :, :].rearrange("p k e f -> p k (e f)")
            else:
                key, w = ("W2T", n - EXPERTS), W2T[:, :, :, :, :].rearrange("p k e c h -> p k (e c h)")
            return key, w, slice(key[1] * HIDDEN, (key[1] + 1) * HIDDEN)

        @block.sync
        def _(sp):
            sp.dma_start(resid[:, 0], token_rows(x_rows, 0)).then_inc(x_in[0], 16)
            for dst, src in ((wr_rows[:, :], Wr), (br_bc[:, :], row(br).to_broadcast([P, EXPERTS])),
                             (small_w[:, 0], w1_w), (small_w[:, 1], v1_w), (small_w[:, 2], w2_w),
                             (b1_rows[:, :], b1.rearrange("e (c f) -> (e c) f", f=P)),
                             (conv_c[:, :], conv_w.rearrange("c a k -> c (a k)"))):
                sp.dma_start(dst, src).then_inc(small_in, 16)
            for g in range(1, GROUPS):
                sp.dma_start(resid[:, g], token_rows(x_rows, g)).then_inc(x_in[g], 16)
            for dst, src in ((conv_bc[:, :, :], conv_w.rearrange("c a k -> a c k").to_broadcast([P, D, 3])),
                             (w1b_bc[:, :], row(w1_b).to_broadcast([P, D])),
                             (v1b_bc[:, :], row(v1_b).to_broadcast([P, D])),
                             (w2b_bc[:, :], row(w2_b).to_broadcast([P, D])),
                             (half_w_bc[:, :], row(ln_w).to_broadcast([P, D])),
                             (half_b_bc[:, :], row(ln_b).to_broadcast([P, D])),
                             (ssm_in[:, 0], A), (ssm_in[:, 1], B_ssm), (ssm_in[:, 2], C_ssm),
                             (d_in[:, :], D_ssm.rearrange("(c a) -> c a", a=1)),
                             (b2_bc[:, :, :], b2.rearrange("(a e) h -> a e h", a=1).to_broadcast([P, EXPERTS, D]))):
                sp.dma_start(dst, src).then_inc(rest_in, 16)

            sp.wait_ge(zeros_ready, 1)
            for g in range(GROUPS):
                sp.dma_start(slot_x[g].rearrange("(p a) d -> p a d", p=P),
                             zero_rows[:, 0:1, :].bitcast(F16).to_broadcast([P, SLOTS // P, 2 * D]))\
                    .then_inc(zeroed[g], 16)
            sp.wait_ge(ssm_const, 1)
            sp.dma_start(taps_dram, taps[:, :]).then_inc(ssm_dram, 16)
            sp.dma_start(decay_dram, decay[:, :, :]).then_inc(ssm_dram, 16)
            sp.dma_start(readout_dram, readout[:, :, :]).then_inc(ssm_dram, 16)
            sp.wait_ge(ssm_dram, 48)
            for j in range(CHUNK):
                at = slice(j * CPG, (j + 1) * CPG)
                back = CHUNK - 1 - j
                sp.dma_start(mT[at], taps_dram.rearrange("(g c) t -> c g t", c=CPG)[:, :, back:back + CHUNK])\
                    .then_inc(ssm_back, 16)
                sp.dma_start(mU[at], decay_dram.rearrange("(g c) k s -> c g k s", c=CPG)[:, :, back, :])\
                    .then_inc(ssm_back, 16)
                sp.dma_start(mV[at], readout_dram.rearrange("(g c) s t -> c g s t", c=CPG)[:, :, j, :])\
                    .then_inc(ssm_back, 16)

            def load_tile(r, i, tile):
                if not (isinstance(tile.n, int) and tile.n < RING):
                    sp.wait_ge(z_ready, tile.n + (1 - RING))
                sp.dma_start_transpose(out=tile_x[tile.slot], in_=slot_x[r % GROUPS][bass.ds(i * TILE, TILE), :])\
                    .then_inc(tile_in[tile.slot], 16)

            def store_tile(r, i, tile):
                sp.wait_ge(y_taken, tile.n + 1)
                sp.dma_start(slot_y[r % GROUPS][bass.ds(i * TILE, TILE), :].rearrange("(a p) d -> p a d", p=P),
                             tile_y[:, tile.half]).then_inc(tile_out[tile.half], 16)

            def start_run(r):
                g = r % GROUPS
                sp.wait_ge(scattered[g], 16 * 2 * STEPS * (r // GROUPS + 1))
                if r >= GROUPS:
                    wait_gathered(sp, g, 1)

            for r in range(RUNS):
                g, first = r % GROUPS, r * TILES
                if g == 0:
                    start_run(r)
                    for i in range(RING):
                        load_tile(r, i, tile_at(first + i, 0))
                for i in range(PEELED):
                    load_tile(r, i + RING, tile_at(first + i + RING, 0))
                    if i > 0:
                        store_tile(r, i - 1, tile_at(first + i - 1, 0))
                with sp.Fori(1, ROUNDS) as rounds:
                    for k in range(RING):
                        i = PEELED - RING + k
                        load_tile(r, rounds * RING + (i + RING), tile_at(first + i + RING, rounds))
                        store_tile(r, rounds * RING + (i - 1), tile_at(first + i - 1, rounds))
                if g < GROUPS - 1:
                    start_run(r + 1)
                for i in range(TILES - RING, TILES):
                    if g < GROUPS - 1:
                        load_tile(r + 1, i - (TILES - RING), tile_at(first + i + RING, 0))
                    store_tile(r, i - 1, tile_at(first + i - 1, 0))
                store_tile(r, TILES - 1, tile_at(first + TILES - 1, 0))
            stores = [(g, part) for g in range(GROUPS) for part in final_parts(GROUPS + g)]
            for n, (g, at) in enumerate(stores):
                sp.wait_ge(x_final, n + 1)
                sp.dma_start(token_rows(out_rows, g)[:, at], resid[:, g, at]).then_inc(x_out, 16)
            sp.wait_ge(x_out, 16 * len(stores))
            for half in range(2):
                sp.wait_ge(tile_out[half], 16 * uses(half, TILES * RUNS))

        @block.gpsimd
        def _(pool):
            steps = 0

            def settle(ins):
                nonlocal steps
                steps += 1
                ins.then_inc(pool_step, 1)
                pool.wait_ge(pool_step, steps)

            nc.gpsimd.memset(zero_rows[:, 0, :], 0.0).then_inc(zeros_ready, 1)
            nc.gpsimd.memset(ones[:, :], 1.0)
            nc.gpsimd.memset(before[:, :], 1.0)
            settle(nc.gpsimd.memset(ident[:, :], 0.0))
            nc.gpsimd.affine_select(out=ident[:, :], in_=ident[:, :], compare_op=ALU.not_equal, fill=1.0,
                                    base=0, pattern=[[-1, P]], channel_multiplier=1).then_inc(pool_const, 1)
            nc.gpsimd.affine_select(out=before[:, :], in_=before[:, :], compare_op=ALU.is_gt, fill=0.0,
                                    base=0, pattern=[[1, P]], channel_multiplier=-1)
            for e in range(EXPERTS):
                nc.gpsimd.memset(low_first[:, e, :], float(EXPERTS - e))
            nc.gpsimd.iota(tile_start[:, :], pattern=[[TILE, TILES]], base=0, channel_multiplier=0,
                           allow_small_or_imprecise_dtypes=True)
            nc.gpsimd.memset(owner_f[:, :], 0.0)
            settle(nc.gpsimd.memset(not_step0[:, :, :], 1.0))
            settle(nc.gpsimd.memset(keep_chunk[:, :], 1.0))
            settle(nc.gpsimd.memset(edge_at[:, :, :], 0.0))
            nc.gpsimd.memset(not_step0[:, :, 0:1], 0.0)
            nc.gpsimd.memset(keep_chunk[:, 0:P:CHUNKS_PER_SEQ], 0.0)
            nc.gpsimd.memset(edge_at[:, 0, 0:P:CHUNKS_PER_SEQ], 1.0)
            nc.gpsimd.memset(edge_at[:, 1, CHUNKS_PER_SEQ - 1:P:CHUNKS_PER_SEQ], 1.0)
            nc.gpsimd.memset(turned[:, 0, :], 0.0)
            nc.gpsimd.memset(turned[:, STEPS + 1, :], 0.0)
            nc.gpsimd.memset(taps[:, 0:CHUNK - 1], 0.0)
            nc.gpsimd.memset(decay[:, 0, :], 1.0)
            settle(nc.gpsimd.memset(states[:, 0:1], 0.0))
            pool.sem_inc(pool_const, 1)

            def scatter(r, picks=(0, 1)):
                g, f = r % GROUPS, r // GROUPS
                if f == 0:
                    pool.wait_ge(zeroed[g], 16)
                else:
                    for slot in range(RING):
                        pool.wait_ge(tile_in[slot], 16 * len(range(slot, TILES * (g + 1), RING)))
                pool.wait_ge(halves_ready, r + 1)
                pool.wait_ge(slots_ready, r + 1)
                for k in picks:
                    for j in range(STEPS):
                        pool.indirect_dma_start(
                            out=slot_x[g], in_=halves[:, g, j, :], in_offset=None,
                            out_offset=bass.IndirectOffsetOnAxis(ap=slots[:, g, k, j:j + 1], axis=0))\
                            .then_inc(scattered[g], 16)

            def gather(r):
                g, f = r % GROUPS, r // GROUPS
                for half in range(2):
                    pool.wait_ge(tile_out[half], 16 * uses(half, TILES * (r + 1)))
                if f:
                    pool.wait_ge(stage_used, 1)
                else:
                    pool.wait_ge(weights_ready, 1)
                for quad in range(QUADS):
                    for k in range(2):
                        for j in range(4 * quad, 4 * quad + 4):
                            pool.indirect_dma_start(
                                out=stage[:, g, k, j, :], out_offset=None, in_=slot_y[g],
                                in_offset=bass.IndirectOffsetOnAxis(ap=slots[:, g, k, j:j + 1], axis=0))\
                                .then_inc(gathered[g][quad], 16)

            def collect(r):
                g = r % GROUPS
                wait_gathered(pool, g, r // GROUPS + 1)
                pool.wait_ge(shares_ready, r + 1)
                rows = [P, STEPS, D]
                for k in range(2):
                    ins = nc.gpsimd.tensor_tensor(stage[:, g, k], stage[:, g, k],
                                                  share[:, g, k, :].unsqueeze(2).to_broadcast(rows), ALU.mult)
                settle(ins)
                settle(nc.gpsimd.tensor_tensor(xn[:, g], xn[:, g], stage[:, g, 0], ALU.add))
                nc.gpsimd.tensor_tensor(xn[:, g], xn[:, g], stage[:, g, 1], ALU.add).then_inc(collected, 1)

            def ssm_constants():
                mult = lambda *ops: nc.gpsimd.tensor_tensor(*ops, ALU.mult)
                add = lambda *ops: nc.gpsimd.tensor_tensor(*ops, ALU.add)
                fold = T[:, 0, :]
                width = P // 2
                settle(add(fold[:, 0:width], ident[:, 0:width], ident[:, width:P]))
                while width > 2 * CPG:
                    width //= 2
                    settle(add(fold[:, 0:width], fold[:, 0:width], fold[:, width:2 * width]))
                add(same_c[:, :], fold[:, 0:CPG], fold[:, CPG:2 * CPG])
                pool.wait_ge(rest_in, 16 * REST_LOADS)
                pool.wait_ge(decay_in, 1)
                mult(cb[:, :], ssm_in[:, 1], ssm_in[:, 2])
                for k in (1, 2, 4, 8):
                    settle(mult(decay[:, k + 1:2 * k + 1, :], decay[:, 1:k + 1, :],
                                decay[:, k:k + 1, :].to_broadcast([P, k, STATES])))
                nc.gpsimd.tensor_copy(readout[:, :, CHUNK], decay[:, CHUNK, :])
                mult(readout[:, :, 0:CHUNK], decay[:, 1:CHUNK + 1, :].rearrange("p k s -> p s k"),
                     cb[:, :].unsqueeze(2).to_broadcast([P, STATES, CHUNK]))
                settle(mult(tap_terms[:, :, :], decay[:, 0:CHUNK, :],
                            cb[:, :].unsqueeze(1).to_broadcast([P, CHUNK, STATES])))
                width = STATES
                while width > 2:
                    width //= 2
                    settle(add(tap_terms[:, :, 0:width], tap_terms[:, :, 0:width], tap_terms[:, :, width:2 * width]))
                settle(add(taps[:, CHUNK - 1:], tap_terms[:, :, 0], tap_terms[:, :, 1]))
                add(taps[:, CHUNK - 1:CHUNK], taps[:, CHUNK - 1:CHUNK], d_in[:, :]).then_inc(ssm_const, 1)

            def ssm_matrices():
                pool.wait_ge(ssm_back, 16 * 3 * CHUNK)
                shape = [P, CGROUPS, CHUNK, CPG]
                for dst, src in ((T, mT[:, :, :]), (U, mU[:, :, :]), (V, mV[:, :, 0:CHUNK])):
                    nc.gpsimd.tensor_tensor(dst[:, :, :].rearrange("p g (t c) -> p g t c", c=CPG),
                                            src.unsqueeze(3).to_broadcast(shape),
                                            same_c[:, :].unsqueeze(1).unsqueeze(1).to_broadcast(shape), ALU.mult)
                nc.gpsimd.tensor_tensor(
                    chunk_decay[:, :, :], mV[:, :, CHUNK:CHUNK + 1].to_broadcast([P, CGROUPS, P]),
                    keep_chunk[:, :].unsqueeze(1).to_broadcast([P, CGROUPS, P]), ALU.mult).then_inc(ssm_mats, 1)

            def add_to_rows(g, bias, signal):
                nc.gpsimd.tensor_tensor(resid[:, g], resid[:, g],
                                        bias[:, :].unsqueeze(1).to_broadcast([P, STEPS, D]), ALU.add)\
                    .then_inc(signal, 1)

            ssm_constants()
            def combine_half():
                key, at = ("c", 1, 0), HALVES[1]
                wait_normed(pool, key)
                settle(nc.gpsimd.tensor_tensor(
                    xn[:, 1, at], xn[:, 1, at],
                    half_w_bc[:, :].unsqueeze(1).to_broadcast([P, at.stop - at.start, D]), ALU.mult))
                nc.gpsimd.tensor_tensor(resid[:, 1, at], resid[:, 1, at], xn[:, 1, at], ALU.add)\
                    .then_inc(half_combined, 1)

            scatter(0, (0,))
            pool.wait_ge(max_ready, 1)
            nc.gpsimd.partition_all_reduce(big_all[:, 0:3], big[:, 0:3], P,
                                           bass.bass_isa.ReduceOp.max).then_inc(max_all, 1)
            scatter(0, (1,))
            scatter(1)
            pool.wait_ge(half_b_ready, 1)
            ssm_matrices()
            for g in range(GROUPS):
                add_to_rows(g, half_b_bc, half_b_added)
            gather(0)
            collect(0)
            gather(1)
            for g in range(GROUPS):
                if g == 1:
                    combine_half()
                wait_normed(pool, ("a", g))
                add_to_rows(g, w2b_bc, w2b_added)
            for g in range(GROUPS):
                scatter(GROUPS + g)
            for g in range(GROUPS):
                add_to_rows(g, half_b_bc, half_b_added)
            gather(GROUPS)
            collect(GROUPS)
            gather(GROUPS + 1)
            for g in range(GROUPS):
                wait_gathered(pool, g, 2)

        @block.scalar
        def _(act):
            w1_stage = stage[:, 0].rearrange("p k j d -> p (k j) d")
            w2_stage = stage[:, 1].rearrange("p k j d -> p (k j d)").rearrange("p (e f) -> p e f", e=EXPERTS)
            for g in range(GROUPS):
                act.wait_ge(x_in[g], 16)
            act.dma_start(w1_stage, W1.rearrange("e (c f) d -> f (e c) d", f=P)).then_inc(ffn_in, 16)
            act.dma_start(w2_stage, W2.rearrange("e h f -> h e f")).then_inc(ffn_in, 16)

            def copy_small():
                wait_unit(act, ("small", 0))
                freed(nc.scalar.activation(projT[:, 0:4, :], bank(("small", 0)), ACT.Copy), ("small", 0))
                wait_unit(act, ("small", 1))
                nc.scalar.activation(projT[:, 4, :], bank(("small", 1))[:, 0:P], ACT.Copy)
                nc.scalar.activation(b1T[:, :], bank(("small", 1))[:, P:P + EXPERTS * FC], ACT.Copy)
                ins = nc.scalar.activation(WrT[:, :], bank(("small", 1))[:, 2 * P:2 * P + EXPERTS], ACT.Copy)
                freed(ins, ("small", 1))

            def copy_turned(kind, g, k, last_reader):
                if k == 0 and last_reader is not None:
                    wait_unit(act, last_reader)
                key = (kind, g, k)
                wait_unit(act, key)
                src = bank(key)
                ins = nc.scalar.activation(turned[:, 1 + 4 * k:5 + 4 * k, :], src, ACT.Copy)
                if kind == "aT" and k in (0, QUADS - 1):
                    m = CHUNKS_PER_SEQ
                    seqs = src.rearrange("d (i s c) -> d i s c", i=4, c=m)
                    if k == 0:
                        ins = nc.scalar.activation(
                            turned[:, STEPS + 1, :].rearrange("d (s c) -> d s c", c=m)[:, :, 0:m - 1],
                            seqs[:, 0, :, 1:m], ACT.Copy)
                    else:
                        ins = nc.scalar.activation(
                            turned[:, 0, :].rearrange("d (s c) -> d s c", c=m)[:, :, 1:m],
                            seqs[:, 3, :, 0:m - 1], ACT.Copy)
                freed(ins, key)

            def apply_norm(key):
                n, kind, g = norms.index(key), key[0], key[1] % GROUPS
                src = xn if kind == "c" else resid
                act.wait_ge(stats_ready, n + 1)
                for quad in norm_quads(key)[1]:
                    for j in range(4 * quad, 4 * quad + 4):
                        ins = nc.scalar.activation(xn[:, g, j, :], src[:, g, j, :], ACT.Identity,
                                                   bias=shift[n % 2][:, j:j + 1], scale=rstd[n % 2][:, j:j + 1])
                    ins.then_inc(normed[1], 1)

            def turn_rows(r):
                if r > 0:
                    wait_unit(act, ("logits", r - 1))
                for k in range(QUADS):
                    key = ("xnT", r, k)
                    wait_unit(act, key)
                    freed(nc.scalar.activation(routed[:, 4 * k:4 * k + 4, :], bank(key), ACT.Copy), key)

            def exp_gap(r):
                act.wait_ge(gap_ready, r + 1)
                nc.scalar.activation(gap_exp[:, :], gap[:, :], ACT.Exp).then_inc(gap_exp_ready, 1)

            def weights_hi():
                act.wait_ge(scales_ready, 1)
                for n in range(2 * EXPERTS):
                    key, w, at = weight_unit(n)
                    wait_unit(act, key)
                    nc.scalar.activation(w[:, 0, at], bank(key), ACT.Copy, scale=S1 if n < EXPERTS else S2)\
                        .then_inc(weight_hi, 1)

            def gelu(tile, e, _, e_before):
                n, half = tile.n, tile.half
                act.wait_ge(z_ready, n + 1)
                for c2 in range(2):
                    if not early(tile):
                        act.wait_ge(h_ready, n * 2 + (c2 - 3))
                    for c in (2 * c2, 2 * c2 + 1):
                        ins = nc.scalar.activation(hid[:, half, c, :], z_ps[half][:, c, :], ACT.Gelu,
                                                   bias=b1T[:, bass.ds(e * FC + c, 1)], scale=INV1)
                    ins.then_inc(gelu_done, 1)

            def tiles(r):
                act.wait_ge(owner_ready, r + 1)
                run_tiles(act, r, gelu)

            def turn_mixer_rows(g):
                for k in range(QUADS):
                    copy_turned("aT", g, k, None if g == 0 else ("o", g - 1, QUADS - 1))
                wait_emptied(act, ("aT", g, QUADS - 1))
                act.sem_inc(turned_ready, 1)

            def silu_gates(g):
                for k in range(QUADS):
                    act.wait_ge(gate_in, QUADS * g + k + 1)
                    nc.scalar.activation(gate[:, 4 * k:4 * k + 4, :], gate[:, 4 * k:4 * k + 4, :], ACT.Silu)\
                        .then_inc(gate_ready, 1)

            def silu_conv(g):
                for k in range(QUADS):
                    key = ("cT", g, k)
                    wait_unit(act, key)
                    ins = nc.scalar.activation(ssm_x[:, 4 * k:4 * k + 4, :], bank(key), ACT.Silu)
                    ins.then_inc(ssm_x_ready, 1)
                    act.wait_ge(ssm_x_ready, QUADS * g + k + 1)
                    free_now(act, key)

            def turn_gated(g):
                for k in range(QUADS):
                    copy_turned("yT", g, k, ("v", g, QUADS - 1))

            apply_norm(("x", 0))
            copy_small()
            turn_rows(0)
            apply_norm(("x", 1))
            act.wait_ge(rest_in, 16 * REST_LOADS)
            nc.scalar.activation(decay[:, 1, :], ssm_in[:, 0], ACT.Sigmoid).then_inc(decay_in, 1)
            exp_gap(0)
            turn_rows(1)
            exp_gap(1)
            weights_hi()
            wait_unit(act, ("logits", 1))
            for g in range(GROUPS):
                tiles(g)
            apply_norm(("c", 0, 0))
            apply_norm(("a", 0))
            act.wait_ge(y_ready, GROUPS * TILES)
            turn_mixer_rows(0)
            silu_gates(0)
            silu_conv(0)
            apply_norm(("c", 1, 0))
            turn_gated(0)
            apply_norm(("a", 1))
            turn_mixer_rows(1)
            apply_norm(("x", 2))
            act.wait_ge(h_ready, 2 * GROUPS * TILES)
            turn_rows(2)
            silu_gates(1)
            silu_conv(1)
            exp_gap(2)
            turn_gated(1)
            apply_norm(("x", 3))
            turn_rows(3)
            exp_gap(3)
            wait_unit(act, ("logits", 3))
            for g in range(GROUPS):
                tiles(GROUPS + g)
            for key in norms[-1 - len(HALVES):]:
                apply_norm(key)
        @block.tensor
        def _(pe):
            def turn(key, sources, rows=P):
                wait_bank(pe, key)
                for i, src in enumerate(sources):
                    ins = nc.tensor.transpose(bank(key)[:, i * P:i * P + src.shape[0]], src,
                                              ident[0:src.shape[0], 0:src.shape[0]])
                ins.then_inc(aux_full, 1)

            def turn_rows(kind, index, norm):
                for k in range(QUADS):
                    wait_normed(pe, norm, k)
                    turn((kind, index, k), [xn[:, index % GROUPS, 4 * k + i, :] for i in range(4)])

            def logits(r):
                key = ("logits", r)
                wait_bank(pe, key)
                for k in range(QUADS):
                    wait_emptied(pe, ("xnT", r, k))
                    for j in range(4 * k, 4 * k + 4):
                        ins = nc.tensor.matmul(bank(key)[:, j * EXPERTS:(j + 1) * EXPERTS], routed[:, j, :],
                                               WrT[:, :], start=True, stop=True)
                ins.then_inc(aux_full, 1)

            def ranks(r):
                key = ("ranks", r)
                wait_bank(pe, key)
                pe.wait_ge(ones_counted, r + 1)
                nc.tensor.matmul(bank(key)[:, 0:EXPERTS], before[:, :], rank[:, :, STEPS - 1],
                                 start=True, stop=True)
                nc.tensor.matmul(bank(key)[:, EXPERTS:2 * EXPERTS], ones[:, :], rank[:, :, STEPS - 1],
                                 start=True, stop=True).then_inc(aux_full, 1)

            def wait_all_emptied(last):
                for n in range(aux_index[last] + 1 - BANKS, aux_index[last] + 1):
                    wait_emptied(pe, aux[n])

            w1_flat = W1T[:, :, :, :].rearrange("p k e f -> p (k e f)")
            w2_flat = W2T[:, :, :, :, :].rearrange("p k e c h -> p (k e c h)")

            def hidden(tile, e):
                n, half = tile.n, tile.half
                pe.wait_ge(tile_in[tile.slot], tile.slot_laps * 16 + 16)
                if not early(tile):
                    pe.wait_ge(gelu_done, n * 2 - 2)
                x_hi, x_lo = tile_x[tile.slot][:, 0, :], tile_x[tile.slot][:, 1, :]
                for c in range(FC):
                    z = z_ps[half][:, c, :]
                    w_hi = w1_flat[:, bass.ds(e * HIDDEN + c * P, P)]
                    w_lo = w1_flat[:, bass.ds(e * HIDDEN + (EXPERTS * HIDDEN + c * P), P)]
                    nc.tensor.matmul(z, w_hi, x_hi, start=True, stop=False)
                    nc.tensor.matmul(z, w_hi, x_lo, start=False, stop=False)
                    ins = nc.tensor.matmul(z, w_lo, x_hi, start=False, stop=True)
                ins.then_inc(z_ready, 1)

            def result(tile, e):
                n, half = tile.n, tile.half
                if not early(tile):
                    pe.wait_ge(y_taken, n - 1)
                for c in range(FC):
                    if c % 2 == 0:
                        pe.wait_ge(h_ready, n * 2 + (c // 2 + 1))
                    w_hi = w2_flat[:, bass.ds(e * (FC * D) + c * D, D)]
                    w_lo = w2_flat[:, bass.ds(e * (FC * D) + (EXPERTS * FC * D + c * D), D)]
                    for s in range(2):
                        y = y_ps[half][:, s * D:(s + 1) * D]
                        at = slice(s * P, (s + 1) * P)
                        nc.tensor.matmul(y, hid_hi[tile.slot][:, c, at], w_hi, start=(c == 0 and s == 0), stop=False,
                                         skip_group_check=True)
                        nc.tensor.matmul(y, hid_hi[tile.slot][:, c, at], w_lo, start=False, stop=False,
                                         skip_group_check=True)
                        ins = nc.tensor.matmul(y, hid_lo[tile.slot][:, c, at], w_hi, start=False, stop=(c == FC - 1),
                                               skip_group_check=True)
                ins.then_inc(y_ready, 1)

            def step(tile, e, before, e_before):
                hidden(tile, e)
                if e_before is not None:
                    result(before, e_before)

            def tiles(r):
                pe.wait_ge(owner_ready, r + 1)
                run_tiles(pe, r, step)
                for tile, e in last_tiles(pe, r):
                    result(tile, e)

            def conv(g):
                pe.wait_ge(turned_ready, g + 1)
                for k in range(QUADS):
                    key = ("conv", g, k)
                    wait_bank(pe, key)
                    for i in range(4):
                        j = 4 * k + i
                        y = bank(key)[:, i * D:(i + 1) * D]
                        edge = 0 if j == 0 else 1 if j == STEPS - 1 else None
                        if edge is not None:
                            nc.tensor.matmul(y, edge_at[:, edge, :], edge_w[:, edge, :], start=True, stop=False)
                        for tap in range(3):
                            ins = nc.tensor.matmul(y, turned[:, j + tap, :], projT[:, tap, :],
                                                   start=(tap == 0 and edge is None), stop=(tap == 2))
                    ins.then_inc(aux_full, 1)

            def gate_products(g):
                for k in range(QUADS):
                    key = ("v", g, k)
                    wait_bank(pe, key)
                    for i in range(4):
                        ins = nc.tensor.matmul(bank(key)[:, i * D:(i + 1) * D], turned[:, 1 + 4 * k + i, :],
                                               projT[:, 3, :], start=True, stop=True)
                    ins.then_inc(aux_full, 1)

            def turn_conv(g):
                pe.wait_ge(conv_ready, QUADS * (g + 1))
                by_cg = mix[:, :].rearrange("p (g m) -> p g m", g=CGROUPS)
                for k in range(QUADS):
                    turn(("cT", g, k), [by_cg[:, 4 * k + i, :] for i in range(4)])

            def states_products(g):
                if g == 0:
                    pe.wait_ge(ssm_mats, 1)
                for k in range(QUADS):
                    key = ("u", g, k)
                    wait_bank(pe, key)
                    pe.wait_ge(ssm_x_ready, QUADS * g + k + 1)
                    for i in range(4):
                        cg = 4 * k + i
                        ins = nc.tensor.matmul(bank(key)[:, i * P:(i + 1) * P], U[:, cg, :], ssm_x[:, cg, :],
                                               start=True, stop=True)
                    ins.then_inc(aux_full, 1)

            def output_products(g):
                for k in range(QUADS):
                    key = ("y", g, k)
                    wait_bank(pe, key)
                    pe.wait_ge(states_ready, QUADS * g + k + 1)
                    for i in range(4):
                        cg = 4 * k + i
                        y = bank(key)[:, i * P:(i + 1) * P]
                        nc.tensor.matmul(y, ssm_x[:, cg, :], T[:, cg, :], start=True, stop=False)
                        ins = nc.tensor.matmul(y, states[:, cg * P:(cg + 1) * P], V[:, cg, :],
                                               start=False, stop=True)
                    ins.then_inc(aux_full, 1)

            def project(g):
                pe.wait_ge(mix_ready, QUADS * (g + 1))
                by_step = mix[:, :].rearrange("p (j c) -> p j c", j=STEPS)
                for k in range(QUADS):
                    turn(("yT", g, k), [by_step[:, 4 * k + i, :] for i in range(4)])
                for k in range(QUADS):
                    key = ("o", g, k)
                    wait_bank(pe, key)
                    wait_emptied(pe, ("yT", g, k))
                    for i in range(4):
                        ins = nc.tensor.matmul(bank(key)[:, i * D:(i + 1) * D], turned[:, 1 + 4 * k + i, :],
                                               projT[:, 4, :], start=True, stop=True)
                    ins.then_inc(aux_full, 1)

            pe.wait_ge(pool_const, 1)
            pe.wait_ge(small_in, 16 * SMALL_LOADS)
            pe.wait_ge(small_ready, 1)
            turn(("small", 0), [tap_w[:, 0], tap_w[:, 1], tap_w[:, 2], small_w[:, 1]])
            turn(("small", 1), [small_w[:, 2], b1_rows[:, :], wr_rows[:, :]])
            wait_emptied(pe, ("small", 1))
            pe.wait_ge(pool_const, 2)
            turn_rows("xnT", 0, ("x", 0))
            logits(0)
            ranks(0)
            turn_rows("xnT", 1, ("x", 1))
            logits(1)
            ranks(1)
            pe.wait_ge(ffn_in, 32)
            w1_stage = stage[:, 0].rearrange("p k j d -> p (k j) d")
            w2_stage = stage[:, 1].rearrange("p k j d -> p (k j d)").rearrange("p (e f) -> p e f", e=EXPERTS)
            for e in range(EXPERTS):
                turn(("W1T", e), [w1_stage[:, e * FC + c, :] for c in range(FC)])
            for e in range(EXPERTS):
                turn(("W2T", e), [w2_stage[:, e, c * P:(c + 1) * P] for c in range(FC)])
            pe.wait_ge(weights_ready, 1)
            wait_all_emptied(("W2T", EXPERTS - 1))
            for g in range(GROUPS):
                tiles(g)
            pe.wait_ge(gelu_done, 2 * GROUPS * TILES)
            turn_rows("aT", 0, ("a", 0))
            conv(0)
            gate_products(0)
            turn_conv(0)
            states_products(0)
            output_products(0)
            project(0)
            turn_rows("aT", 1, ("a", 1))
            conv(1)
            turn_rows("xnT", 2, ("x", 2))
            logits(2)
            gate_products(1)
            turn_conv(1)
            ranks(2)
            states_products(1)
            output_products(1)
            project(1)
            turn_rows("xnT", 3, ("x", 3))
            logits(3)
            ranks(3)
            wait_all_emptied(("ranks", RUNS - 1))
            for g in range(GROUPS):
                tiles(GROUPS + g)

        @block.vector
        def _(dve):
            steps = 0

            def settle(ins):
                nonlocal steps
                steps += 1
                ins.then_inc(v_step, 1)
                dve.wait_ge(v_step, steps)
                return ins

            def publish(ins, signal, value):
                ins.then_inc(signal, 1)
                dve.wait_ge(signal, value)

            def measure(key):
                at, g = norm_steps(key), key[1] % GROUPS
                src = (xn if key[0] == "c" else resid)[:, g]
                for j in range(at.start, at.stop):
                    ins = nc.vector.bn_stats(st[:, j, :], src[:, j, :])
                settle(ins)

            def statistics(key, eps, measured=False):
                n, at, g = norms.index(key), norm_steps(key), key[1] % GROUPS
                src = (xn if key[0] == "c" else resid)[:, g]
                scale, offset = rstd[n % 2][:, at], shift[n % 2][:, at]
                if not measured:
                    measure(key)
                nc.vector.tensor_tensor(mean[:, at], st[:, at, 1], st[:, at, 4], ALU.add)
                nc.vector.tensor_tensor(t1[:, at], st[:, at, 1], st[:, at, 4], ALU.subtract)
                settle(nc.vector.scalar_tensor_tensor(var[:, at], st[:, at, 2], float(D * eps), st[:, at, 5],
                                                      ALU.add, ALU.add))
                nc.vector.tensor_scalar(mean[:, at], mean[:, at], 0.5, None, ALU.mult)
                settle(nc.vector.scalar_tensor_tensor(t1[:, at], t1[:, at], 0.25, t1[:, at], ALU.mult, ALU.mult))
                settle(nc.vector.scalar_tensor_tensor(var[:, at], var[:, at], 1.0 / D, t1[:, at], ALU.mult, ALU.add))
                if n >= 2:
                    wait_normed(dve, norms[n - 2])
                settle(nc.vector.tensor_scalar(t1[:, at].bitcast(I32), var[:, at].bitcast(I32), 1, None,
                                               ALU.arith_shift_right))
                nc.vector.tensor_scalar(var[:, at], var[:, at], -0.5, None, ALU.mult)
                settle(nc.vector.tensor_scalar(scale.bitcast(I32), t1[:, at].bitcast(I32), -1.0,
                                               float(0x5F3759DF), ALU.mult, ALU.add))
                for _ in range(3):
                    settle(nc.vector.tensor_tensor(t1[:, at], scale, scale, ALU.mult))
                    settle(nc.vector.tensor_tensor(t1[:, at], t1[:, at], var[:, at], ALU.mult))
                    settle(nc.vector.scalar_tensor_tensor(scale, t1[:, at], 1.5, scale, ALU.add, ALU.mult))
                publish(nc.vector.scalar_tensor_tensor(offset, mean[:, at], -1.0, scale, ALU.mult, ALU.mult),
                        stats_ready, n + 1)
                for quad in norm_quads(key)[0]:
                    for j in range(4 * quad, 4 * quad + 4):
                        ins = nc.vector.tensor_scalar(xn[:, g, j, :], src[:, j, :], rstd[n % 2][:, j:j + 1],
                                                      shift[n % 2][:, j:j + 1], ALU.mult, ALU.add)
                    ins.then_inc(normed[0], 1)

            def split_rows(r):
                g = r % GROUPS
                wait_normed(dve, ("x", r))
                if r >= GROUPS:
                    dve.wait_ge(scattered[g], 16 * 2 * STEPS)
                settle(nc.vector.tensor_copy(halves[:, g, :, 0:D], xn[:, g]))
                nc.vector.tensor_tensor(halves[:, g, :, D:2 * D], xn[:, g], halves[:, g, :, 0:D],
                                        ALU.subtract).then_inc(halves_ready, 1)

            def choose(r):
                key = ("logits", r)
                wait_unit(dve, key)
                by_expert = bank(key)[:, 0:EXPERTS * STEPS].rearrange("p (j e) -> p e j", e=EXPERTS)
                ins = nc.vector.tensor_tensor(lg[:, :, :], by_expert,
                                              br_bc[:, :].unsqueeze(2).to_broadcast([P, EXPERTS, STEPS]), ALU.add)
                settle(ins)
                free_now(dve, key)
                for k in range(2):
                    e_last = lg[:, :, :].rearrange("p e j -> p j e")
                    settle(nc.vector.tensor_reduce(best[k][:, :], e_last, X_AXIS, ALU.max))
                    every = [P, EXPERTS, STEPS]
                    settle(nc.vector.tensor_tensor(r1[:, :, :], lg[:, :, :],
                                                   best[k][:, :].unsqueeze(1).to_broadcast(every), ALU.is_equal))
                    settle(nc.vector.tensor_tensor(r1[:, :, :], r1[:, :, :], low_first[:, :, :], ALU.mult))
                    settle(nc.vector.tensor_reduce(t1[:, :], r1[:, :, :].rearrange("p e j -> p j e"),
                                                   X_AXIS, ALU.max))
                    settle(nc.vector.tensor_tensor(pick[k][:, :, :], low_first[:, :, :],
                                                   t1[:, :].unsqueeze(1).to_broadcast(every), ALU.is_equal))
                    if k == 0:
                        settle(nc.vector.scalar_tensor_tensor(lg[:, :, :], pick[0][:, :, :], -3e38, lg[:, :, :],
                                                              ALU.mult, ALU.add))
                nc.vector.tensor_tensor(gap[:, :], best[1][:, :], best[0][:, :], ALU.subtract).then_inc(gap_ready, 1)
                settle(nc.vector.tensor_tensor(r1[:, :, :], pick[0][:, :, :], pick[1][:, :, :], ALU.add))
                flat = "p e j -> p (e j)"
                nc.vector.tensor_tensor_scan(rank[:, :, :].rearrange(flat), not_step0[:, :, :].rearrange(flat),
                                             r1[:, :, :].rearrange(flat), 0.0, ALU.mult, ALU.add)\
                    .then_inc(ones_counted, 1)

            def place(r):
                g = r % GROUPS
                key = ("ranks", r)
                wait_unit(dve, key)
                settle(nc.vector.tensor_copy(counts[:, :, :], bank(key)[:, 0:2 * EXPERTS]))
                free_now(dve, key)
                settle(nc.vector.tensor_scalar(whole_i[:, :], counts[:, 1, :], float(TILE - 1), None, ALU.add))
                shift_bits = TILE.bit_length() - 1
                settle(nc.vector.tensor_scalar(whole_i[:, :], whole_i[:, :], shift_bits, None,
                                               ALU.arith_shift_right))
                settle(nc.vector.tensor_scalar(whole[:, :], whole_i[:, :], float(TILE), None, ALU.mult))
                settle(nc.vector.tensor_tensor_scan(ends[:, :], ones[:, 0:EXPERTS], whole[:, :], 0.0,
                                                    ALU.mult, ALU.add))
                settle(nc.vector.tensor_tensor(start_f[:, :], ends[:, :], whole[:, :], ALU.subtract))
                settle(nc.vector.tensor_tensor(start_f[:, :], start_f[:, :], counts[:, 0, :], ALU.add))
                settle(nc.vector.tensor_tensor(rank[:, :, :], rank[:, :, :], r1[:, :, :], ALU.subtract))
                settle(nc.vector.tensor_tensor(rank[:, :, :], rank[:, :, :],
                                               start_f[:, :].unsqueeze(2).to_broadcast([P, EXPERTS, STEPS]), ALU.add))
                if r >= GROUPS:
                    wait_gathered(dve, g, 1)
                for k in range(2):
                    settle(nc.vector.tensor_tensor(r1[:, :, :], rank[:, :, :], pick[k][:, :, :], ALU.mult))
                    settle(nc.vector.tensor_reduce(slot_f[:, k, :], r1[:, :, :].rearrange("p e j -> p j e"),
                                                   X_AXIS, ALU.add))
                nc.vector.tensor_copy(slots[:, g], slot_f[:, :, :]).then_inc(slots_ready, 1)
                if r >= GROUPS:
                    dve.wait_ge(y_taken, TILES * (g + 1))
                shape = [1, TILES, EXPERTS]
                settle(nc.vector.tensor_tensor(past, ends[0:1, :].unsqueeze(1).to_broadcast(shape),
                                               tile_start[:, :].unsqueeze(2).to_broadcast(shape), ALU.is_le))
                of_tile = owner_f[:, OWNER_PAD:]
                settle(nc.vector.tensor_reduce(of_tile, past, X_AXIS, ALU.add))
                settle(nc.vector.tensor_scalar(of_tile, of_tile, float(EXPERTS - 1), None, ALU.min))
                every = RING * ROUNDS + 1
                top = RING + LAG - 1
                settle(nc.vector.scalar_tensor_tensor(owners_f[:, :], owner_f[:, top:top + every:RING],
                                                      float(EXPERTS), owner_f[:, top - 1:top - 1 + every:RING],
                                                      ALU.mult, ALU.add))
                for k in range(top - 2, -1, -1):
                    settle(nc.vector.scalar_tensor_tensor(owners_f[:, :], owners_f[:, :], float(EXPERTS),
                                                          owner_f[:, k:k + every:RING], ALU.mult, ALU.add))
                nc.vector.tensor_copy(owners[:, g], owners_f[:, :]).then_inc(owner_ready, 1)
                dve.wait_ge(gap_exp_ready, r + 1)
                settle(nc.vector.tensor_scalar(t1[:, :], gap_exp[:, :], 1.0, None, ALU.add))
                settle(nc.vector.reciprocal(share[:, g, 0, :], t1[:, :]))
                nc.vector.tensor_tensor(share[:, g, 1, :], gap_exp[:, :], share[:, g, 0, :], ALU.mult)\
                    .then_inc(shares_ready, 1)

            def find_largest():
                dve.wait_ge(ffn_in, 32)
                nc.vector.tensor_reduce(big[:, 0:1], stage[:, 0].rearrange("p k j d -> p (k j d)"), X_AXIS,
                                        ALU.max, apply_absolute_value=True)
                nc.vector.tensor_reduce(big[:, 1:2], stage[:, 1].rearrange("p k j d -> p (k j d)"), X_AXIS,
                                        ALU.max, apply_absolute_value=True)
                wait_emptied(dve, ("small", 1))
                nc.vector.tensor_reduce(big[:, 2:3], b1T[:, :], X_AXIS, ALU.max, apply_absolute_value=True)\
                    .then_inc(max_ready, 1)

            def find_scales():
                dve.wait_ge(max_all, 1)
                settle(nc.vector.scalar_tensor_tensor(big_all[:, 2:3], big_all[:, 0:1], float(D), big_all[:, 2:3],
                                                      ALU.mult, ALU.add))
                settle(nc.vector.tensor_scalar(big_all[:, 0:3], big_all[:, 0:3], 1e-25, None, ALU.max))
                settle(nc.vector.tensor_scalar(scale_t[:, 0:3].bitcast(I32), big_all[:, 0:3].bitcast(I32),
                                               EXPONENT_BITS, None, ALU.bitwise_and))
                settle(nc.vector.reciprocal(big[:, 0:3], scale_t[:, 0:3]))
                for k, (s, inv, top) in enumerate(((S1, INV1, 13), (S2, INV2, 13), (SH, INVH, 14))):
                    nc.vector.tensor_scalar(s, big[:, k:k + 1], 2.0 ** top, None, ALU.mult)
                    settle(nc.vector.tensor_scalar(inv, scale_t[:, k:k + 1], 2.0 ** -top, None, ALU.mult))
                publish(nc.vector.tensor_tensor(INVY, INV2, INVH, ALU.mult), scales_ready, 1)

            def weights_lo():
                for n in range(2 * EXPERTS):
                    key, w, at = weight_unit(n)
                    dve.wait_ge(weight_hi, n + 1)
                    freed(nc.vector.scalar_tensor_tensor(w[:, 1, at], bank(key), S1 if n < EXPERTS else S2,
                                                         w[:, 0, at], ALU.mult, ALU.subtract), key)
                wait_emptied(dve, key)
                dve.sem_inc(weights_ready, 1)

            b2_flat = b2_bc[:, :, :].rearrange("p e h -> p (e h)")

            def split_hidden(tile, c2):
                n, half, at = tile.n, tile.half, slice(2 * c2, 2 * c2 + 2)
                if c2 == 0 and not (isinstance(n, int) and n < RING):
                    dve.wait_ge(y_ready, n + (1 - RING))
                dve.wait_ge(gelu_done, n * 2 + (c2 + 1))
                nc.vector.tensor_scalar(hid_hi[tile.slot][:, at, :], hid[:, half, at, :], SH, None, ALU.mult)\
                    .then_inc(hi_ready, 1)
                dve.wait_ge(hi_ready, n * 2 + (c2 + 1))
                nc.vector.scalar_tensor_tensor(hid_lo[tile.slot][:, at, :], hid[:, half, at, :], SH,
                                               hid_hi[tile.slot][:, at, :], ALU.mult, ALU.subtract)\
                    .then_inc(h_ready, 1)

            def take_result(tile, e):
                n, half = tile.n, tile.half
                dve.wait_ge(y_ready, n + 1)
                if not early(tile):
                    dve.wait_ge(tile_out[half], tile.half_laps * 16)
                bias = b2_flat[:, bass.ds(e * D, D)].unsqueeze(1).to_broadcast([P, 2, D])
                nc.vector.scalar_tensor_tensor(tile_y[:, half], y_ps[half][:, 0:2 * D].rearrange(
                    "p (s d) -> p s d", s=2), INVY, bias, ALU.mult, ALU.add).then_inc(y_taken, 1)

            def step(tile, e, before, e_before):
                split_hidden(tile, 0)
                if e_before is not None:
                    take_result(before, e_before)
                split_hidden(tile, 1)

            def tiles(r):
                run_tiles(dve, r, step)
                if r == GROUPS - 1:
                    dve.wait_ge(collected, 1)
                    measure(("c", 0, 0))
                for tile, e in last_tiles(dve, r):
                    take_result(tile, e)

            def collect(r, quads):
                g = r % GROUPS
                for quad in quads:
                    wait_gathered(dve, g, r // GROUPS + 1, [quad])
                    for k in range(2):
                        for j in range(4 * quad, 4 * quad + 4):
                            ins = nc.vector.scalar_tensor_tensor(xn[:, g, j, :], stage[:, g, k, j, :],
                                                                 share[:, g, k, j:j + 1], xn[:, g, j, :],
                                                                 ALU.mult, ALU.add)
                        settle(ins)

            def combine(key, at=None):
                r, at = key[1], at or norm_steps(key)
                g = r % GROUPS
                half = (at.stop - at.start) // 2
                for piece in (slice(at.start, at.start + half), slice(at.start + half, at.stop)):
                    for quad in range(piece.start // 4, piece.stop // 4):
                        wait_normed(dve, key, quad)
                    ins = nc.vector.tensor_tensor(
                        xn[:, g, piece], xn[:, g, piece],
                        half_w_bc[:, :].unsqueeze(1).to_broadcast([P, half, D]), ALU.mult)
                settle(ins)
                dve.wait_ge(half_b_added, r + 1)
                settle(nc.vector.tensor_tensor(resid[:, g, at], resid[:, g, at], xn[:, g, at], ALU.add))

            def take_conv(g):
                for k in range(QUADS):
                    key = ("conv", g, k)
                    wait_unit(dve, key)
                    shape = [P, 4, CGROUPS, CPG]
                    by_cg = mix[:, :].rearrange("p (g j c) -> p j g c", g=CGROUPS, c=CPG)
                    freed(nc.vector.tensor_tensor(
                        by_cg[:, 4 * k:4 * k + 4], bank(key).rearrange("p (j g c) -> p j g c", j=4, c=CPG),
                        convb_bc[:, :].rearrange("p (g c) -> p g c", c=CPG).unsqueeze(1).to_broadcast(shape),
                        ALU.add), key)
                    wait_emptied(dve, key)
                    dve.sem_inc(conv_ready, 1)

            def take_gates(g):
                for k in range(QUADS):
                    key = ("v", g, k)
                    wait_unit(dve, key)
                    freed(nc.vector.tensor_tensor(
                        gate[:, 4 * k:4 * k + 4, :], bank(key).rearrange("p (j c) -> p j c", j=4),
                        v1b_bc[:, :].unsqueeze(1).to_broadcast([P, 4, D]), ALU.add), key)
                    wait_emptied(dve, key)
                    dve.sem_inc(gate_in, 1)

            def scan_states(g):
                for k in range(QUADS):
                    key = ("u", g, k)
                    wait_unit(dve, key)
                    at = states[:, 1 + 4 * k * P:1 + 4 * (k + 1) * P]
                    settle(nc.vector.tensor_tensor_scan(
                        at, chunk_decay[:, 4 * k:4 * k + 4, :].rearrange("p g n -> p (g n)"), bank(key), 0.0,
                        ALU.mult, ALU.add))
                    free_now(dve, key)
                    nc.vector.memset(at[:, CHUNKS_PER_SEQ - 1:4 * P:CHUNKS_PER_SEQ], 0.0).then_inc(states_ready, 1)

            def gate_outputs(g):
                dve.wait_ge(gate_ready, QUADS * (g + 1))
                for k in range(QUADS):
                    key = ("y", g, k)
                    wait_unit(dve, key)
                    view = "p (g t c) -> p g t c"
                    freed(nc.vector.tensor_tensor(
                        mix[:, :].rearrange("p (t g c) -> p g t c", g=CGROUPS, c=CPG)[:, 4 * k:4 * k + 4],
                        bank(key).rearrange(view, g=4, c=CPG),
                        gate[:, :, :].rearrange("p t (g c) -> p g t c", c=CPG)[:, 4 * k:4 * k + 4], ALU.mult), key)
                    wait_emptied(dve, key)
                    dve.sem_inc(mix_ready, 1)

            def add_mixed(g):
                dve.wait_ge(w2b_added, g + 1)
                for k in range(QUADS):
                    key = ("o", g, k)
                    wait_unit(dve, key)
                    x_at = resid[:, g, 4 * k:4 * k + 4, :]
                    ins = nc.vector.tensor_tensor(x_at, x_at, bank(key).rearrange("p (j c) -> p j c", j=4),
                                                  ALU.add)
                    freed(ins, key)
                    wait_emptied(dve, key)

            dve.wait_ge(x_in[0], 16)
            statistics(("x", 0), LN_EPS_BLOCK)
            dve.wait_ge(small_in, 16 * SMALL_LOADS)
            for k in range(3):
                ins = nc.vector.tensor_scalar(tap_w[:, k, :], small_w[:, 0, :], conv_c[:, k:k + 1], None, ALU.mult)
            ins.then_inc(small_ready, 1)
            split_rows(0)
            dve.wait_ge(x_in[1], 16)
            statistics(("x", 1), LN_EPS_BLOCK)
            dve.wait_ge(pool_const, 2)
            choose(0)
            place(0)
            find_largest()
            dve.wait_ge(rest_in, 16 * REST_LOADS)
            nc.vector.tensor_scalar(half_w_bc[:, :], half_w_bc[:, :], 0.5, None, ALU.mult)
            nc.vector.tensor_scalar(half_b_bc[:, :], half_b_bc[:, :], 0.5, None, ALU.mult).then_inc(half_b_ready, 1)
            for edge, tap in ((0, 0), (1, 2)):
                nc.vector.scalar_tensor_tensor(edge_w[:, edge, :], w1b_bc[0:1, :], -1.0, conv_bc[0:1, :, tap],
                                               ALU.mult, ALU.mult)
            settle(nc.vector.tensor_reduce(convb_bc[:, :], conv_bc[:, :, :], X_AXIS, ALU.add))
            settle(nc.vector.tensor_tensor(convb_bc[:, :], convb_bc[:, :], w1b_bc[:, :], ALU.mult))
            split_rows(1)
            choose(1)
            place(1)
            find_scales()
            weights_lo()
            for g in range(GROUPS):
                tiles(g)
            statistics(("c", 0, 0), LN_EPS_FFN, measured=True)
            combine(("c", 0, 0))
            statistics(("a", 0), LN_EPS_BLOCK)
            collect(1, range(0, 2))
            take_conv(0)
            collect(1, range(2, 4))
            take_gates(0)
            statistics(("c", 1, 0), LN_EPS_FFN)
            scan_states(0)
            gate_outputs(0)
            combine(("c", 1, 0), HALVES[0])
            dve.wait_ge(half_combined, 1)
            statistics(("a", 1), LN_EPS_BLOCK)
            add_mixed(0)
            statistics(("x", 2), LN_EPS_BLOCK)
            take_conv(1)
            split_rows(2)
            choose(2)
            take_gates(1)
            place(2)
            scan_states(1)
            gate_outputs(1)
            add_mixed(1)
            dve.sem_inc(stage_used, 1)
            statistics(("x", 3), LN_EPS_BLOCK)
            split_rows(3)
            choose(3)
            place(3)
            for g in range(GROUPS):
                tiles(GROUPS + g)
            dve.wait_ge(collected, 2)
            statistics(("c", 2, 0), LN_EPS_FFN)
            combine(("c", 2, 0))
            dve.sem_inc(x_final, 1)
            for part in range(len(HALVES)):
                collect(3, range(2 * part, 2 * part + 2))
                statistics(("c", 3, part), LN_EPS_FFN)
                combine(("c", 3, part))
                dve.sem_inc(x_final, 1)


_INS = ["x", "w1_w", "w1_b", "v1_w", "v1_b", "w2_w", "w2_b", "conv_w", "A", "B_ssm", "C_ssm", "D_ssm",
        "Wr", "br", "W1", "b1", "W2", "b2", "ln_w", "ln_b"]


def kernel(**inputs):
    import numpy as np
    import concourse.bacc as bacc
    from concourse.bass_utils import run_bass_kernel_spmd

    nc = bacc.Bacc("TRN2", target_bir_lowering=False, num_devices=1)
    arrays, args = {}, []
    for n, name in enumerate(_INS):
        a = np.ascontiguousarray(inputs[("L0_attn_" if n < 12 else "L0_ffn_") + name])
        arrays["in_" + name] = a
        args.append(nc.dram_tensor("in_" + name, a.shape, F32, kind="ExternalInput").ap())
    args.append(nc.dram_tensor("out_x", (BATCH, SEQ, D), F32, kind="ExternalOutput").ap())
    build(nc, *args)
    return run_bass_kernel_spmd(nc, [arrays], core_ids=[0]).results[0]["out_x"]
```
